# Optimizing a Trainium2 kernel written in Bass

```python
import numpy as np
import jax
import jax.numpy as jnp

def _softmax(x, axis=-1):
    return jax.nn.softmax(x, axis=axis)

def _gelu(x):
    return jax.nn.gelu(x, approximate=True)

def _silu(x):
    return jax.nn.silu(x)

def _sigmoid(x):
    return jax.nn.sigmoid(x)

def _layernorm(x, axis=-1, eps=1e-05):
    m = jnp.mean(x, axis=axis, keepdims=True)
    v = jnp.var(x, axis=axis, keepdims=True)
    return (x - m) / jnp.sqrt(v + eps)

def _scatter_add(tgt, idx, src, axis=0):
    return tgt.at[idx].add(src)

def _segment_sum(src, seg, n):
    return jax.ops.segment_sum(src, seg, n)
kernel_name = 'mk_prb_d2_jaxref_r4_de5c35'

def setup_inputs(seed: int=0):
    np.random.seed(seed)
    _w = jnp.asarray

    def _L0_attn_setup():
        import jax, jax.numpy as jnp
        import numpy as np
        import math
        N_HEAD = 16
        HEAD_DIM = 64
        N_EMBD = 256
        EPS_RMS = 1e-05
        U_L2_EPS = 1e-06

        def _get_alibi_slopes(n_heads):

            def pow2(n):
                start = 2 ** (-2 ** (-(math.log2(n) - 3)))
                return [start * start ** i for i in range(n)]
            if math.log2(n_heads).is_integer():
                return pow2(n_heads)
            c = 2 ** math.floor(math.log2(n_heads))
            s = pow2(c)
            extra = _get_alibi_slopes(2 * c)
            return s + extra[0::2][:n_heads - c]

        def _rmsnorm(x, w):
            var = jnp.mean(jnp.square(x), axis=-1, keepdims=True)
            return x * jax.lax.rsqrt(var + EPS_RMS) * w
        key = jax.random.key(seed)
        ks = jax.random.split(key, 9)
        B, T = (2, 512)
        H, D, C = (N_HEAD, HEAD_DIM, N_EMBD)
        x = jax.random.normal(ks[0], (B, T, C), dtype=jnp.float32)
        sc = 1.0 / math.sqrt(C)
        Wq = jax.random.normal(ks[1], (C, H * D), dtype=jnp.float32) * sc
        Wk = jax.random.normal(ks[2], (C, H * D), dtype=jnp.float32) * sc
        Wv = jax.random.normal(ks[3], (C, H * D), dtype=jnp.float32) * sc
        Wproj = jax.random.normal(ks[4], (H * D, C), dtype=jnp.float32) * (0.5 / math.sqrt(C) / math.sqrt(12))
        q_rms_w = jnp.ones((D,), dtype=jnp.float32)
        k_rms_w = jnp.ones((D,), dtype=jnp.float32)
        omega = jnp.full((H,), math.log(math.expm1(1.0)), dtype=jnp.float32)
        u = jax.random.normal(ks[5], (H, D), dtype=jnp.float32) * (1.0 / math.sqrt(D))
        return {'x': x, 'Wq': Wq, 'Wk': Wk, 'Wv': Wv, 'Wproj': Wproj, 'q_rms_w': q_rms_w, 'k_rms_w': k_rms_w, 'omega': omega, 'u': u}
    _L0_attn_in = _L0_attn_setup()

    def _L0_ffn_setup():
        import jax, jax.numpy as jnp
        import numpy as np
        B, S, D, E, H, K = (64, 512, 256, 32, 1024, 8)
        key = jax.random.key(seed)
        k0, k1, k2, k3 = jax.random.split(key, 4)
        x = jax.random.normal(k0, (B, S, D), jnp.float32)
        gate_w = jax.random.normal(k1, (E, D), jnp.float32) * (1.0 / np.sqrt(D))
        gate_b = jnp.zeros((E,), jnp.float32)
        w1 = jax.random.normal(k2, (E, D + 1, H), jnp.float32) * (1.0 / np.sqrt(D + 1))
        w2 = jax.random.normal(k3, (E, H + 1, D), jnp.float32) * (1.0 / np.sqrt(H + 1))
        return {'x': x, 'gate_w': gate_w, 'gate_b': gate_b, 'w1': w1, 'w2': w2}
    _L0_ffn_in = _L0_ffn_setup()

    def _L1_attn_setup():
        import jax, jax.numpy as jnp
        import numpy as np
        from jax.scipy.special import erf
        INV_SQRT2 = 0.7071067811865476
        INV_SQRT2PI = 0.3989422804014327
        ETA, BETA, ALPHA = (0.1, 0.9, 0.99)

        def gelu(x):
            return 0.5 * x * (1.0 + erf(x * INV_SQRT2))

        def gelu_grad(x):
            cdf = 0.5 * (1.0 + erf(x * INV_SQRT2))
            pdf = jnp.exp(-0.5 * x * x) * INV_SQRT2PI
            return cdf + x * pdf

        def _reference_tuple_inner(x, W_K, W_V, W1, W2, m1, m2):
            B, T, H = x.shape
            denom = B * H
            K = jnp.einsum('bth,kh->btk', x, W_K)
            V = jnp.einsum('bth,vh->btv', x, W_V)
            reads = jnp.einsum('btd,hd->bth', gelu(jnp.einsum('btk,dk->btd', K, W1)), W2)
            assoc_losses = jnp.mean((reads - V) ** 2, axis=(0, 2))

            def step(carry, kv):
                W1c, W2c, m1c, m2c = carry
                k_t, v_t = kv
                h = k_t @ W1c.T
                a = gelu(h)
                pred = a @ W2c.T
                dpred = 2.0 / denom * (pred - v_t)
                g2 = dpred.T @ a
                dh = dpred @ W2c * gelu_grad(h)
                g1 = dh.T @ k_t
                n1 = jnp.linalg.norm(g1)
                n2 = jnp.linalg.norm(g2)
                surprise = 0.5 * (n1 + n2)
                g1 = jnp.where(n1 > 1.0, g1 / n1, g1)
                g2 = jnp.where(n2 > 1.0, g2 / n2, g2)
                m1n = BETA * m1c - ETA * g1
                m2n = BETA * m2c - ETA * g2
                W1n = ALPHA * W1c + m1n
                W2n = ALPHA * W2c + m2n
                return ((W1n, W2n, m1n, m2n), surprise)
            Kt = jnp.swapaxes(K, 0, 1)
            Vt = jnp.swapaxes(V, 0, 1)
            (W1f, W2f, m1f, m2f), surprises = jax.lax.scan(step, (W1, W2, m1, m2), (Kt, Vt))
            return (reads, surprises, assoc_losses, W1f, W2f)
        key = jax.random.key(seed)
        k0, k1, k2, k3, k4 = jax.random.split(key, 5)
        B, T, H, D = (32, 256, 256, 64)
        x = jax.random.normal(k0, (B, T, H), dtype=jnp.float32)
        W_K = jax.random.normal(k1, (H, H), dtype=jnp.float32) / np.float32(np.sqrt(H))
        W_V = jax.random.normal(k2, (H, H), dtype=jnp.float32) / np.float32(np.sqrt(H))
        W1 = jax.random.normal(k3, (D, H), dtype=jnp.float32) * 0.02
        W2 = jax.random.normal(k4, (H, D), dtype=jnp.float32) * 0.02
        m1 = jnp.zeros((D, H), dtype=jnp.float32)
        m2 = jnp.zeros((H, D), dtype=jnp.float32)
        return {'x': x, 'W_K': W_K, 'W_V': W_V, 'W1': W1, 'W2': W2, 'm1': m1, 'm2': m2}
    _L1_attn_in = _L1_attn_setup()

    def _L1_ffn_setup():
        import jax, jax.numpy as jnp
        import numpy as np
        IN_F, OUT_F, BLOCK, NBLK = (256, 1024, 64, 16)
        TOPK = NBLK // 4
        key = jax.random.key(seed)
        ks = jax.random.split(key, 7)
        s = 1.0 / np.sqrt(IN_F)
        s2 = 1.0 / np.sqrt(OUT_F)
        return {'x': jax.random.normal(ks[0], (4, 1024, IN_F), jnp.float32), 'router_w': jax.random.uniform(ks[1], (NBLK, IN_F), jnp.float32, -s, s), 'router_b': jax.random.uniform(ks[2], (NBLK,), jnp.float32, -s, s), 'w1': jax.random.uniform(ks[3], (OUT_F, IN_F), jnp.float32, -s, s), 'b1': jax.random.uniform(ks[4], (OUT_F,), jnp.float32, -s, s), 'w2': jax.random.uniform(ks[5], (IN_F, OUT_F), jnp.float32, -s2, s2), 'b2': jax.random.uniform(ks[6], (IN_F,), jnp.float32, -s2, s2)}
    _L1_ffn_in = _L1_ffn_setup()
    _d = {'L0_attn_x': _L0_attn_in['x'], 'L0_attn_Wq': _L0_attn_in['Wq'], 'L0_attn_Wk': _L0_attn_in['Wk'], 'L0_attn_Wv': _L0_attn_in['Wv'], 'L0_attn_Wproj': _L0_attn_in['Wproj'], 'L0_attn_q_rms_w': _L0_attn_in['q_rms_w'], 'L0_attn_k_rms_w': _L0_attn_in['k_rms_w'], 'L0_attn_omega': _L0_attn_in['omega'], 'L0_attn_u': _L0_attn_in['u'], 'L0_ffn_gate_w': _L0_ffn_in['gate_w'], 'L0_ffn_gate_b': _L0_ffn_in['gate_b'], 'L0_ffn_w1': _L0_ffn_in['w1'], 'L0_ffn_w2': _L0_ffn_in['w2'], 'L1_attn_W_K': _L1_attn_in['W_K'], 'L1_attn_W_V': _L1_attn_in['W_V'], 'L1_attn_W1': _L1_attn_in['W1'], 'L1_attn_W2': _L1_attn_in['W2'], 'L1_attn_m1': _L1_attn_in['m1'], 'L1_attn_m2': _L1_attn_in['m2'], 'L1_ffn_router_w': _L1_ffn_in['router_w'], 'L1_ffn_router_b': _L1_ffn_in['router_b'], 'L1_ffn_w1': _L1_ffn_in['w1'], 'L1_ffn_b1': _L1_ffn_in['b1'], 'L1_ffn_w2': _L1_ffn_in['w2'], 'L1_ffn_b2': _L1_ffn_in['b2']}
    _x0 = _d['L0_attn_x']
    _d['L0_attn_x'] = jax.random.normal(jax.random.fold_in(jax.random.key(seed), 1), (8, 512, 256), dtype=_x0.dtype)
    del _x0
    return _d

def reference(L0_attn_x, L0_attn_Wq, L0_attn_Wk, L0_attn_Wv, L0_attn_Wproj, L0_attn_q_rms_w, L0_attn_k_rms_w, L0_attn_omega, L0_attn_u, L0_ffn_gate_w, L0_ffn_gate_b, L0_ffn_w1, L0_ffn_w2, L1_attn_W_K, L1_attn_W_V, L1_attn_W1, L1_attn_W2, L1_attn_m1, L1_attn_m2, L1_ffn_router_w, L1_ffn_router_b, L1_ffn_w1, L1_ffn_b1, L1_ffn_w2, L1_ffn_b2):

    def _L0_attn_ref(x, Wq, Wk, Wv, Wproj, q_rms_w, k_rms_w, omega, u):
        import jax, jax.numpy as jnp
        import numpy as np
        import math
        N_HEAD = 16
        HEAD_DIM = 64
        N_EMBD = 256
        EPS_RMS = 1e-05
        U_L2_EPS = 1e-06

        def _get_alibi_slopes(n_heads):

            def pow2(n):
                start = 2 ** (-2 ** (-(math.log2(n) - 3)))
                return [start * start ** i for i in range(n)]
            if math.log2(n_heads).is_integer():
                return pow2(n_heads)
            c = 2 ** math.floor(math.log2(n_heads))
            s = pow2(c)
            extra = _get_alibi_slopes(2 * c)
            return s + extra[0::2][:n_heads - c]

        def _rmsnorm(x, w):
            var = jnp.mean(jnp.square(x), axis=-1, keepdims=True)
            return x * jax.lax.rsqrt(var + EPS_RMS) * w
        B, T, C = x.shape
        H, D = (N_HEAD, HEAD_DIM)
        q = (x @ Wq).reshape(B, T, H, D)
        k = (x @ Wk).reshape(B, T, H, D)
        v = (x @ Wv).reshape(B, T, H, D)
        q = _rmsnorm(q, q_rms_w)
        k = _rmsnorm(k, k_rms_w)
        slopes = jnp.asarray(_get_alibi_slopes(H), dtype=jnp.float32)
        omega_eff = jax.nn.softplus(omega) * slopes
        u_n = u / jnp.maximum(jnp.linalg.norm(u, axis=-1, keepdims=True), U_L2_EPS)
        gate_logits = jnp.einsum('bthd,hd->bht', k, u_n) / math.sqrt(D)
        gate = jax.nn.softplus(gate_logits)
        idx = jnp.arange(T)
        dist = jnp.maximum(idx[:, None] - idx[None, :], 0).astype(jnp.float32)
        bias = -dist[None, None] * omega_eff[None, :, None, None] * gate[:, :, None, :]
        causal = idx[:, None] >= idx[None, :]
        bias = jnp.where(causal[None, None], bias, -jnp.inf)
        scale = 1.0 / math.sqrt(D)
        scores = jnp.einsum('bihd,bjhd->bhij', q, k) * scale + bias
        attn = jax.nn.softmax(scores, axis=-1)
        y = jnp.einsum('bhij,bjhd->bihd', attn, v).reshape(B, T, H * D)
        return y @ Wproj

    def _L0_ffn_ref(x, gate_w, gate_b, w1, w2):
        import jax, jax.numpy as jnp
        import numpy as np
        B, S, D, E, H, K = (64, 512, 256, 32, 1024, 8)
        b, s, d = x.shape
        logits = jnp.einsum('bsd,ed->bse', x, gate_w) + gate_b
        probs = jax.nn.softmax(logits, axis=-2)
        vals_t, idx_t = jax.lax.top_k(probs.transpose(0, 2, 1), K)
        vals = vals_t.transpose(0, 2, 1)
        idx = idx_t.transpose(0, 2, 1)
        flat_idx = idx.reshape(b, K * E)
        tok = jnp.take_along_axis(x, flat_idx[:, :, None], axis=1)
        tok = tok.reshape(b, K, E, d)
        merged = jnp.einsum('bked,bke->bed', tok, vals)
        ones = jnp.ones(merged.shape[:-1] + (1,), merged.dtype)
        h = jnp.einsum('bei,eih->beh', jnp.concatenate([merged, ones], -1), w1)
        h = jax.nn.gelu(h, approximate=False)
        o = jnp.einsum('bej,ejo->beo', jnp.concatenate([h, ones], -1), w2)
        out_tok = jnp.einsum('beo,bke->bkeo', o, vals).reshape(b, K * E, d)
        out = jnp.zeros_like(x).at[jnp.arange(b)[:, None], flat_idx].add(out_tok)
        return out

    def _L1_attn_ref(x, W_K, W_V, W1, W2, m1, m2):
        import jax, jax.numpy as jnp
        import numpy as np
        from jax.scipy.special import erf
        INV_SQRT2 = 0.7071067811865476
        INV_SQRT2PI = 0.3989422804014327
        ETA, BETA, ALPHA = (0.1, 0.9, 0.99)

        def gelu(x):
            return 0.5 * x * (1.0 + erf(x * INV_SQRT2))

        def gelu_grad(x):
            cdf = 0.5 * (1.0 + erf(x * INV_SQRT2))
            pdf = jnp.exp(-0.5 * x * x) * INV_SQRT2PI
            return cdf + x * pdf

        def _reference_tuple_inner(x, W_K, W_V, W1, W2, m1, m2):
            B, T, H = x.shape
            denom = B * H
            K = jnp.einsum('bth,kh->btk', x, W_K)
            V = jnp.einsum('bth,vh->btv', x, W_V)
            reads = jnp.einsum('btd,hd->bth', gelu(jnp.einsum('btk,dk->btd', K, W1)), W2)
            assoc_losses = jnp.mean((reads - V) ** 2, axis=(0, 2))

            def step(carry, kv):
                W1c, W2c, m1c, m2c = carry
                k_t, v_t = kv
                h = k_t @ W1c.T
                a = gelu(h)
                pred = a @ W2c.T
                dpred = 2.0 / denom * (pred - v_t)
                g2 = dpred.T @ a
                dh = dpred @ W2c * gelu_grad(h)
                g1 = dh.T @ k_t
                n1 = jnp.linalg.norm(g1)
                n2 = jnp.linalg.norm(g2)
                surprise = 0.5 * (n1 + n2)
                g1 = jnp.where(n1 > 1.0, g1 / n1, g1)
                g2 = jnp.where(n2 > 1.0, g2 / n2, g2)
                m1n = BETA * m1c - ETA * g1
                m2n = BETA * m2c - ETA * g2
                W1n = ALPHA * W1c + m1n
                W2n = ALPHA * W2c + m2n
                return ((W1n, W2n, m1n, m2n), surprise)
            Kt = jnp.swapaxes(K, 0, 1)
            Vt = jnp.swapaxes(V, 0, 1)
            (W1f, W2f, m1f, m2f), surprises = jax.lax.scan(step, (W1, W2, m1, m2), (Kt, Vt))
            return (reads, surprises, assoc_losses, W1f, W2f)
        return _reference_tuple_inner(x, W_K, W_V, W1, W2, m1, m2)[0]

    def _L1_ffn_ref(x, router_w, router_b, w1, b1, w2, b2):
        import jax, jax.numpy as jnp
        import numpy as np
        IN_F, OUT_F, BLOCK, NBLK = (256, 1024, 64, 16)
        TOPK = NBLK // 4
        x_shape = x.shape
        xf = x.reshape(-1, IN_F)
        n = xf.shape[0]
        prob = jax.nn.softmax(xf @ router_w.T + router_b, axis=-1)
        _, idx = jax.lax.top_k(prob, TOPK)
        mask = jnp.zeros((n, NBLK), bool).at[jnp.arange(n)[:, None], idx].set(True)
        w1b = w1.reshape(NBLK, BLOCK, IN_F)
        b1b = b1.reshape(NBLK, BLOCK)
        h = jnp.einsum('nd,ibd->nib', xf, w1b) + b1b
        h = jnp.where(mask[:, :, None], h, jnp.zeros((), h.dtype))
        h = jax.nn.relu(h)
        w2b = w2.reshape(IN_F, NBLK, BLOCK)
        y = jnp.einsum('nib,dib->nd', jnp.where(mask[:, :, None], h, 0.0), w2b) + b2
        return y.reshape(x_shape)
    x = L0_attn_x
    xn = _layernorm(x, axis=-1)
    x = x + _L0_attn_ref(xn, L0_attn_Wq, L0_attn_Wk, L0_attn_Wv, L0_attn_Wproj, L0_attn_q_rms_w, L0_attn_k_rms_w, L0_attn_omega, L0_attn_u) + _L0_ffn_ref(xn, L0_ffn_gate_w, L0_ffn_gate_b, L0_ffn_w1, L0_ffn_w2)
    xn = _layernorm(x, axis=-1)
    x = x + _L1_attn_ref(xn, L1_attn_W_K, L1_attn_W_V, L1_attn_W1, L1_attn_W2, L1_attn_m1, L1_attn_m2) + _L1_ffn_ref(xn, L1_ffn_router_w, L1_ffn_router_b, L1_ffn_w1, L1_ffn_b1, L1_ffn_w2, L1_ffn_b2)
    return x

_drawn_inputs = setup_inputs


def setup_inputs(seed=0):
    import zlib

    import numpy as np

    out = dict(_drawn_inputs(seed))
    spreads = {'L0_attn_q_rms_w': (1.0, 0.6),
     'L0_attn_k_rms_w': (1.0, 0.6),
     'L0_attn_omega': (0.5413248538970947, 0.6),
     'L0_ffn_gate_b': (0.0, 0.8),
     'L1_attn_m1': (0.0, 0.1),
     'L1_attn_m2': (0.0, 0.1)}
    factors = {'L0_attn_u': 5.674, 'L1_ffn_b1': 8.0, 'L1_ffn_b2': 3.088}
    for name, (base, spread) in spreads.items():
        noise = np.random.default_rng([zlib.crc32(name.encode()), seed]).standard_normal(out[name].shape)
        drawn = base * np.exp(spread * noise) if base else spread * noise
        out[name] = jnp.asarray(drawn.astype(out[name].dtype))
    for name, factor in factors.items():
        out[name] = (out[name] * factor).astype(out[name].dtype)
    return out
```

```python
from contextlib import ExitStack

import concourse.bass as bass
import concourse.mybir as mybir

F32 = mybir.dt.float32
F32R = mybir.dt.float32r
U32 = mybir.dt.uint32
ALU = mybir.AluOpType
ACT = mybir.ActivationFunctionType
AX = mybir.AxisListType

P = 128
EPS = 1e-5
NEG = -1.0e30
LOWEST = -3.0e38


class Event:

    def __init__(self, ctx, nc, name, per, unit=1, carrier=None):
        self.name, self.per, self.unit, self.n = name, per, unit, 0
        self.carrier = carrier
        self.sem = ctx.enter_context(nc.semaphore(name))

    def credit(self, eng):
        eng.sem_inc(self.sem, self.per * self.unit)

    def mark(self, instruction):
        self.n += 1
        instruction.then_inc(self.sem, self.unit)
        return instruction

    def turn_ends(self):
        assert self.n == self.per, (self.name, self.n, self.per)
        self.n = 0

    def wait(self, eng, turn, n=None, alone=False):
        n = self.per if n is None else n
        eng.wait_ge(self.sem, (turn + 1) * (self.per * self.unit) + n * self.unit)
        if alone:
            eng.sem_inc(self.carrier, 1)


class Chain(Event):

    def settle(self, eng, turn, alone=False):
        self.wait(eng, turn, self.n, alone)


def alibi_slopes(heads):
    start = 2.0 ** (-8.0 / heads)
    return [start * start ** i for i in range(heads)]


def build(nc, t, out):
    x_in = t["L0_attn_x"]
    B, T, C = x_in.shape
    NT = T // P
    KC = C // P
    H, D = t["L0_attn_u"].shape
    HP = H // 2
    E = t["L0_ffn_gate_w"].shape[0]
    F = t["L0_ffn_w1"].shape[2]
    NB = t["L1_ffn_router_w"].shape[0]
    HID = t["L1_ffn_w1"].shape[0]
    HC = HID // P
    M1 = t["L1_attn_W1"].shape[0]
    TOPK = NB // 4
    GRP = P // E
    assert (B, T, C, H, D, E, F) == (8, 512, 256, 16, 64, 32, 1024) and GRP == 4

    scratch = lambda name, shape, dt=F32: nc.dram_tensor(name, shape, dt, kind="Internal").ap()
    xnT_hi_d = scratch("xnT_hi_d", (B, P, KC, T))
    xnT_lo_d = scratch("xnT_lo_d", (B, P, KC, T))
    pick_d = scratch("pick_d", (B, E, T))
    x1_d = scratch("x1_d", (B, T, C))
    eo_d = scratch("eo_d", (GRP, B, E, C))

    with ExitStack() as whole:
        def sb_in(ctx):
            return lambda name, shape, dt=F32: ctx.enter_context(nc.sbuf_tensor(name, shape, dt))

        def banks(ctx, n, name):
            return [ctx.enter_context(nc.psum_tensor(f"{name}{i}", [P, 512], F32)) for i in range(n)]

        sb = sb_in(whole)
        ident = sb("ident", [P, P])
        merged = sb("merged", [P, KC, E, B])
        half = sb("half", [P, 16])
        carrier = whole.enter_context(nc.semaphore("carrier"))

        with ExitStack() as ctx, nc.Block() as block:
            s_zero = ctx.enter_context(nc.semaphore("s_zero"))

            @block.gpsimd
            def _(eng):
                eng.memset(ident[:, :], 0.0).then_inc(s_zero, 1)
                eng.memset(half[:, :], -0.5)
                eng.wait_ge(s_zero, 1)
                eng.affine_select(out=ident[:, :], in_=ident[:, :], compare_op=ALU.not_equal, fill=1.0,
                                  base=0, pattern=[[-1, P]], channel_multiplier=1)

        g = dict(B=B, T=T, C=C, NT=NT, KC=KC, H=H, D=D, HP=HP, E=E, F=F, NB=NB, HC=HC, M1=M1, TOPK=TOPK, GRP=GRP,
                 sb_in=sb_in, banks=banks, ident=ident, merged=merged, half=half, carrier=carrier,
                 xnT_hi_d=xnT_hi_d, xnT_lo_d=xnT_lo_d, pick_d=pick_d, x1_d=x1_d, eo_d=eo_d)
        route_tokens(nc, t, g)
        attend(nc, t, g)
        run_experts(nc, t, g)
        second_layer(nc, t, out, g)


def route_tokens(nc, t, g):
    B, T, C, NT, KC, E = (g[k] for k in ("B", "T", "C", "NT", "KC", "E"))
    ident, merged, half = g["ident"], g["merged"], g["half"]
    xnT_hi_d, xnT_lo_d, pick_d = g["xnT_hi_d"], g["xnT_lo_d"], g["pick_d"]
    with ExitStack() as ctx:
        sb = g["sb_in"](ctx)
        gate_in = sb("gate_in", [E, C])
        gateT = sb("gateT", [P, KC, E])
        gate_b = sb("gate_b", [E, 1])
        x = sb("x", [P, NT, C])
        xn = sb("xn", [P, NT, C])
        stats = sb("stats", [P, NT, 6])
        mv = sb("mv", [P, NT, 2])
        var = sb("var", [P, NT])
        rstd = sb("rstd", [P, NT])
        xT = sb("xT", [P, KC, T])
        xT_hi = sb("xT_hi", [P, KC, T], F32R)
        xT_lo = sb("xT_lo", [P, KC, T], F32R)
        logits = sb("logits", [E, T])
        top8 = sb("top8", [E, 8])
        left = sb("left", [E, T])
        nmax = sb("nmax", [E, 1])
        expd = sb("expd", [E, T])
        den = sb("den", [E, 1])
        rden = sb("rden", [E, 1])
        pick = sb("pick", [E, T])
        pickT = sb("pickT", [P, NT, E])
        bT0, bT1, bL, bG, bP, bM = g["banks"](ctx, 6, "rt")
        bT = [bT0, bT1]

        ev = lambda name, per, unit=1: Event(ctx, nc, name, per, unit, g["carrier"])
        gate_load, gate_t, gate_copied = ev("gate_load", 2, 16), ev("gate_t", 1), ev("gate_copied", 1)
        load, store, store_p = ev("load", 1, 16), ev("store", 2, 16), ev("store_p", 1, 16)
        dve, act, pool = (Chain(ctx, nc, n, k, 1, g["carrier"]) for n, k in (("dve_rt", 21), ("act_rt", 4), ("pool_rt", 1)))
        xn_done, split_done, pick_done = ev("xn_done", 1), ev("split_done", 2), ev("pick_done", 1)
        var_done, merged_done, pickT_done = ev("var_done", 1), ev("merged_done", 1), ev("pickT_done", 1)
        pe_xT, pe_gate, pe_pickT, pe_merged = ev("pe_xT", 2), ev("pe_gate", 1), ev("pe_pickT", 1), ev("pe_merged", 1)
        xT_done, logits_done, exp_done = ev("xT_done", 2), ev("logits_done", 1), ev("exp_done", 1)

        with nc.Block() as block:
            @block.sync
            def _(eng):
                for e in (gate_load, load, store, store_p):
                    e.credit(eng)
                gate_load.mark(eng.dma_start(gate_in[:, :], t["L0_ffn_gate_w"]))
                gate_load.mark(eng.dma_start(gate_b[:, :], t["L0_ffn_gate_b"].unsqueeze(1)))
                load.mark(eng.dma_start(x[:, :, :], t["L0_attn_x"][0].rearrange("(n p) c -> p n c", p=P)))
                load.turn_ends()

                def put(b):
                    split_done.wait(eng, b)
                    store.mark(eng.dma_start(xnT_hi_d[b], xT_hi[:, :, :].bitcast(F32)))
                    store.mark(eng.dma_start(xnT_lo_d[b], xT_lo[:, :, :].bitcast(F32)))
                    pick_done.wait(eng, b)
                    store_p.mark(eng.dma_start(pick_d[b], pick[:, :]))
                    store.turn_ends()
                    store_p.turn_ends()
                with eng.Fori(0, B - 1) as b:
                    xn_done.wait(eng, b)
                    load.mark(eng.dma_start(x[:, :, :],
                                            t["L0_attn_x"][b + 1].rearrange("(n p) c -> p n c", p=P)))
                    load.turn_ends()
                    put(b)
                put(B - 1)
                store.wait(eng, B - 1)
                store_p.wait(eng, B - 1)

            @block.tensor
            def _(eng):
                for e in (gate_t, pe_xT, pe_gate, pe_pickT, pe_merged):
                    e.credit(eng)
                gate_load.wait(eng, 0)
                for k in range(KC):
                    m = eng.transpose(bG[:, k * E:(k + 1) * E], gate_in[:, k * P:(k + 1) * P], ident[0:E, 0:E])
                gate_t.mark(m)
                with eng.Fori(0, B) as b:
                    xn_done.wait(eng, b)
                    for k in range(KC):
                        xT_done.wait(eng, b - 1, k + 1)
                        for n in range(NT):
                            m = eng.transpose(bT[k][:, n * P:(n + 1) * P], xn[:, n, k * P:(k + 1) * P], ident[:, :])
                        pe_xT.mark(m)
                    pe_xT.turn_ends()
                    gate_copied.wait(eng, 0)
                    logits_done.wait(eng, b - 1)
                    for k in range(KC):
                        xT_done.wait(eng, b, k + 1)
                        m = eng.matmul(bL[0:E, :], gateT[:, k, :], xT[:, k, :], start=(k == 0), stop=(k == KC - 1))
                    pe_gate.mark(m)
                    pe_gate.turn_ends()
                    pick_done.wait(eng, b)
                    pickT_done.wait(eng, b - 1, alone=True)
                    for n in range(NT):
                        m = eng.transpose(bP[:, n * E:(n + 1) * E], pick[:, n * P:(n + 1) * P], ident[0:E, 0:E])
                    pe_pickT.mark(m)
                    pe_pickT.turn_ends()
                    pickT_done.wait(eng, b)
                    merged_done.wait(eng, b - 1)
                    for k in range(KC):
                        for n in range(NT):
                            m = eng.matmul(bM[:, k * E:(k + 1) * E], xn[:, n, k * P:(k + 1) * P], pickT[:, n, :],
                                           start=(n == 0), stop=(n == NT - 1))
                    pe_merged.mark(m)
                    pe_merged.turn_ends()

            @block.scalar
            def _(eng):
                for e in (act, xT_done, logits_done, exp_done):
                    e.credit(eng)
                with eng.Fori(0, B) as b:
                    split_done.wait(eng, b - 1)
                    for k in range(KC):
                        pe_xT.wait(eng, b, k + 1)
                        xT_done.mark(eng.activation(xT[:, k, :], bT[k][:, :], ACT.Copy))
                    xT_done.turn_ends()
                    gate_load.wait(eng, 0)
                    pe_gate.wait(eng, b)
                    pick_done.wait(eng, b - 1)
                    logits_done.mark(eng.activation(logits[:, :], bL[0:E, :], ACT.Identity, bias=gate_b[:, 0:1]))
                    logits_done.turn_ends()
                    var_done.wait(eng, b)
                    exp_done.mark(eng.activation(expd[:, :], logits[:, :], ACT.Exp, bias=nmax[:, 0:1],
                                                 accum_out=den[:, 0:1]))
                    exp_done.turn_ends()

            @block.gpsimd
            def _(eng):
                pool.credit(eng)
                with eng.Fori(0, B) as b:
                    dve.wait(eng, b, 9)
                    pool.mark(eng.tensor_tensor(rstd[:, :], var[:, :], half[:, 0:NT], ALU.pow))
                    pool.turn_ends()

            @block.vector
            def _(eng):
                for e in (dve, xn_done, split_done, pick_done, var_done, merged_done, pickT_done, gate_copied):
                    e.credit(eng)
                gate_t.wait(eng, 0)
                gate_copied.mark(eng.tensor_copy(gateT[:, :, :], bG[:, 0:KC * E].rearrange("p (k e) -> p k e", k=KC)))
                with eng.Fori(0, B) as b:
                    load.wait(eng, b)
                    for n in range(NT):
                        dve.mark(eng.bn_stats(stats[:, n, :], x[:, n, :]))
                    dve.settle(eng, b, alone=True)
                    for n in range(NT):
                        dve.mark(eng.bn_aggr(mv[:, n, :], stats[:, n, :]))
                    dve.settle(eng, b)
                    dve.mark(eng.tensor_scalar(var[:, :], mv[:, :, 1], EPS, None, ALU.add))
                    pool.wait(eng, b)
                    pe_merged.wait(eng, b - 1)
                    for n in range(NT):
                        m = eng.tensor_scalar(xn[:, n, :], x[:, n, :], mv[:, n, 0:1], rstd[:, n:n + 1],
                                              ALU.subtract, ALU.mult)
                        if n == NT - 1:
                            xn_done.mark(m)
                        else:
                            dve.mark(m)
                    xn_done.turn_ends()
                    store.wait(eng, b - 1)
                    for k in range(KC):
                        xT_done.wait(eng, b, k + 1)
                        dve.mark(eng.tensor_copy(xT_hi[:, k, :], xT[:, k, :]))
                    dve.settle(eng, b)
                    for k in range(KC):
                        split_done.mark(eng.tensor_tensor(xT_lo[:, k, :], xT[:, k, :], xT_hi[:, k, :].bitcast(F32),
                                                          ALU.subtract))
                    split_done.turn_ends()
                    logits_done.wait(eng, b, alone=True)
                    dve.mark(eng.max(top8[:, :], logits[:, :]))
                    dve.settle(eng, b)
                    var_done.mark(eng.tensor_scalar(nmax[:, :], top8[:, 0:1], -1.0, None, ALU.mult))
                    var_done.turn_ends()
                    dve.mark(eng.match_replace(left[:, :], top8[:, :], logits[:, :], LOWEST))
                    exp_done.wait(eng, b)
                    dve.mark(eng.reciprocal(rden[:, :], den[:, :]))
                    dve.settle(eng, b)
                    dve.mark(eng.scalar_tensor_tensor(left[:, :], left[:, :], LOWEST / 2, expd[:, :],
                                                      ALU.is_le, ALU.mult))
                    dve.settle(eng, b)
                    store_p.wait(eng, b - 1)
                    pick_done.mark(eng.tensor_scalar(pick[:, :], left[:, :], rden[:, 0:1], None, ALU.mult))
                    pick_done.turn_ends()
                    pe_pickT.wait(eng, b)
                    pickT_done.mark(eng.tensor_copy(pickT[:, :, :],
                                                    bP[:, 0:NT * E].rearrange("p (n e) -> p n e", n=NT)))
                    pickT_done.turn_ends()
                    pe_merged.wait(eng, b)
                    merged_done.mark(eng.tensor_copy(merged[:, :, :, b],
                                                     bM[:, 0:KC * E].rearrange("p (k e) -> p k e", k=KC)))
                    merged_done.turn_ends()
                    while dve.n < dve.per:
                        dve.mark(eng.engine_nop())
                    dve.turn_ends()


def attend(nc, t, g):
    B, T, C, NT, KC, H, D, HP = (g[k] for k in ("B", "T", "C", "NT", "KC", "H", "D", "HP"))
    ident, half = g["ident"], g["half"]
    xnT_hi_d, xnT_lo_d, x1_d = g["xnT_hi_d"], g["xnT_lo_d"], g["x1_d"]
    W = 3 * P + 2
    DA = D + 2
    off = [P * c * (c + 1) // 2 for c in range(NT + 1)]
    offT = [0, 512, 896, 1152, 1280]
    slopes = alibi_slopes(H)
    with ExitStack() as ctx:
        sb = g["sb_in"](ctx)
        w_hi = sb("w_hi", [P, KC, HP, W], F32R)
        w_lo = sb("w_lo", [P, KC, HP, W], F32R)
        w_proj = sb("w_proj", [P, HP, C])
        mask = sb("mask", [P, T])
        pos = sb("pos", [P, NT])
        omega = sb("omega", [P, H])
        q_scale = sb("q_scale", [DA, 1])

        with ExitStack() as c2:
            sb2 = g["sb_in"](c2)
            raw_w = sb2("raw_w", [P, KC, 3, H * D])
            u = sb2("u", [P, H, D])
            kw = sb2("kw", [P, D])
            tmp = sb2("tmp", [P, H, D])
            ss = sb2("ss", [P, H])
            slope = sb2("slope", [P, H])
            om = sb2("om", [P, H])
            e0 = sb2("e0", [P, H])
            l0 = sb2("l0", [P, H])
            gk = sb2("gk", [P, KC, H])
            qk_w = sb2("qk_w", [DA, 2])
            s_ld = c2.enter_context(nc.semaphore("s_ld"))
            dv, po, ac = (Chain(c2, nc, n, 0) for n in ("dv_s", "po_s", "ac_s"))
            with nc.Block() as block:
                @block.sync
                def _(eng):
                    for m, w in enumerate(("L0_attn_Wq", "L0_attn_Wk", "L0_attn_Wv")):
                        eng.dma_start(raw_w[:, :, m, :], t[w].rearrange("(k p) n -> p k n", p=P)).then_inc(s_ld, 16)
                    eng.dma_start(w_proj[:, :, :], t["L0_attn_Wproj"].rearrange("(h p) c -> p h c", p=P)).then_inc(s_ld, 16)
                    eng.dma_start(u[:, :, :], t["L0_attn_u"].partition_broadcast(P)).then_inc(s_ld, 16)
                    eng.dma_start(kw[:, :], t["L0_attn_k_rms_w"].partition_broadcast(P)).then_inc(s_ld, 16)
                    eng.dma_start(om[:, :], t["L0_attn_omega"].partition_broadcast(P)).then_inc(s_ld, 16)
                    eng.dma_start(qk_w[0:D, 0:1], t["L0_attn_q_rms_w"].unsqueeze(1)).then_inc(s_ld, 16)
                    eng.dma_start(qk_w[0:D, 1:2], t["L0_attn_k_rms_w"].unsqueeze(1)).then_inc(s_ld, 16)

                @block.gpsimd
                def _(eng):
                    po.mark(eng.memset(mask[:, :], 0.0))
                    po.mark(eng.iota(pos[:, :], pattern=[[P, NT]], base=-(T // 2), channel_multiplier=1,
                                     allow_small_or_imprecise_dtypes=True))
                    po.mark(eng.memset(q_scale[:, :], 1.0))
                    for h in range(H):
                        po.mark(eng.memset(slope[:, h:h + 1], slopes[h]))
                    po.wait(eng, -1, 1)
                    po.mark(eng.affine_select(out=mask[:, T - P:T], in_=mask[:, T - P:T], compare_op=ALU.is_ge,
                                              fill=NEG, base=0, pattern=[[-1, P]], channel_multiplier=1))
                    dv.wait(eng, -1, 4)
                    po.mark(eng.tensor_tensor(ss[:, :], ss[:, :], half[:, 0:H], ALU.pow))

                @block.scalar
                def _(eng):
                    dv.wait(eng, -1, 5)
                    ac.mark(eng.activation(e0[:, :], e0[:, :], ACT.Exp))
                    ac.settle(eng, -1)
                    ac.mark(eng.activation(l0[:, :], e0[:, :], ACT.Ln, bias=1.0))

                @block.vector
                def _(eng):
                    eng.wait_ge(s_ld, 9 * 16)
                    dv.mark(eng.tensor_tensor(tmp[:, :, :], u[:, :, :], u[:, :, :], ALU.mult))
                    dv.settle(eng, -1)
                    dv.mark(eng.tensor_reduce(ss[:, :], tmp[:, :, :], AX.X, ALU.add))
                    dv.mark(eng.tensor_tensor(u[:, :, :], u[:, :, :],
                                              kw[:, :].unsqueeze(1).to_broadcast([P, H, D]), ALU.mult))
                    dv.settle(eng, -1)
                    dv.mark(eng.tensor_scalar(ss[:, :], ss[:, :], 1e-12, None, ALU.max))
                    dv.mark(eng.scalar_tensor_tensor(e0[:, :], om[:, :], -1.0, om[:, :], ALU.mult, ALU.min))
                    ac.wait(eng, -1, 2)
                    dv.mark(eng.scalar_tensor_tensor(om[:, :], om[:, :], 0.0, l0[:, :], ALU.max, ALU.add))
                    po.wait(eng, -1, 3 + H)
                    dv.settle(eng, -1)
                    dv.mark(eng.tensor_tensor(omega[:, :], om[:, :], slope[:, :], ALU.mult))
                    dv.mark(eng.scalar_tensor_tensor(q_scale[0:D, :], qk_w[0:D, 0:1], float(D) ** -0.5, qk_w[0:D, 1:2],
                                                     ALU.mult, ALU.mult))
                    po.wait(eng, -1, 5 + H)
                    dv.mark(eng.tensor_tensor(u[:, :, :], u[:, :, :],
                                              ss[:, :].unsqueeze(2).to_broadcast([P, H, D]), ALU.mult))
                    dv.settle(eng, -1)
                    dv.mark(eng.tensor_scalar(u[:, :, :], u[:, :, :], float(D) ** -0.5, None, ALU.mult))
                    for k in range(KC):
                        dv.settle(eng, -1)
                        dv.mark(eng.tensor_tensor(tmp[:, :, :], raw_w[:, k, 1, :].rearrange("p (h d) -> p h d", h=H),
                                                  u[:, :, :], ALU.mult))
                        dv.settle(eng, -1)
                        dv.mark(eng.tensor_reduce(gk[:, k, :], tmp[:, :, :], AX.X, ALU.add))
                    dv.settle(eng, -1)
                    for k in range(KC):
                        parts = [(m * P, P, raw_w[:, k, m, :]) for m in range(3)] + [(3 * P, 2, gk[:, k, :])]
                        for at, n, src in parts:
                            src = src.rearrange("p (h n) -> p h n", n=n)
                            dv.mark(eng.tensor_copy(w_hi[:, k, :, at:at + n], src))
                            dv.settle(eng, -1)
                            dv.mark(eng.tensor_tensor(w_lo[:, k, :, at:at + n], src,
                                                      w_hi[:, k, :, at:at + n].bitcast(F32), ALU.subtract))

        xT_hi = sb("cT_hi", [P, KC, T], F32R)
        xT_lo = sb("cT_lo", [P, KC, T], F32R)
        raw = sb("raw", [P, NT, W])
        sq = sb("sq", [P, NT, 2 * P])
        ss = sb("ssq", [P, NT * 4])
        rs = sb("rs", [P, NT, 4])
        gl = sb("gl", [P, NT, 2])
        ge = sb("ge", [P, NT, 2])
        gp = sb("gp", [P, NT, 2])
        qk = sb("qk", [P, NT, 4, DA])
        qkT = sb("qkT", [DA, 4, T])
        v = sb("v", [P, NT, P])
        prob = [sb(f"prob{h}", [P, off[NT]]) for h in range(2)]
        probT = [sb(f"probT{h}", [P, off[NT]]) for h in range(2)]
        mx = sb("mx", [P, 2 * NT])
        nm = sb("nm", [P, 2 * NT])
        den = sb("dens", [P, 2 * NT])
        rec = sb("rec", [P, 2 * NT])
        yT = sb("yT", [P, HP, T])
        xr = sb("xr", [P, NT, C])
        bank = g["banks"](ctx, 8, "at")
        bQ, bR, bS, bY = bank[0:2], bank[2:5], bank[5:7], bank[7]

        ev = lambda name, per, unit=1: Event(ctx, nc, name, per, unit, g["carrier"])
        xT_load, xr_load, xr_store = ev("xT_load", 2, 16), ev("xr_load", 1, 16), ev("xr_store", 1, 16)
        pe_q, pe_t, pe_s, pe_pt, pe_y = ev("pe_q", 4), ev("pe_t", 4), ev("pe_s", 8), ev("pe_pt", 6), ev("pe_y", 1)
        pe_o = ev("pe_o", 4)
        raw_even, squared, gate_exp, qT_done = ev("raw_even", 2), ev("squared", 1), ev("gate_exp", 2), ev("qT_done", 2)
        exp_done, ptA = ev("p_exp", 8), ev("ptA", 3)
        raw_odd, ssd, norm_done, gate_in, gate_g = ev("raw_odd", 2), ev("ssd", 2), ev("norm_done", 1), ev("gate_in", 2), ev("gate_g", 1)
        kT_done, maxed, negated, rec_done, ptD = ev("kT_done", 2), ev("maxed", 8), ev("negated", 2), ev("rec_done", 2), ev("ptD", 3)
        y_done, o_done = ev("y_done", 1), ev("o_done", 4)
        rs_done, aug_done, v_done, p_done = ev("rs_done", 1), ev("aug_done", 2), ev("v_done", 1), ev("p_done", 8)
        consts = ev("consts", 3)

        def ends(*events):
            for e in events:
                e.turn_ends()

        def free_R(eng, u, s):
            if u == 0:
                kT_done.wait(eng, s, 2)
            elif u == 1:
                qT_done.wait(eng, s, 2)
            elif u == 2:
                kT_done.wait(eng, s, 1)
            elif u < 9:
                (ptD if (u - 3) % 2 == 0 else ptA).wait(eng, s, (u - 3) // 2 + 1)
            else:
                qT_done.wait(eng, s + 1, 1)

        with nc.Block() as block:
            def slots(eng, turn):
                with eng.Fori(0, B) as b:
                    with eng.Fori(0, HP - 1) as hp:
                        turn(b * HP + hp, b, hp, False)
                    turn(b * HP + (HP - 1), b, HP - 1, True)

            @block.sync
            def _(eng):
                for e in (xT_load, xr_load, xr_store):
                    e.credit(eng)

                def load_xT(b):
                    xT_load.mark(eng.dma_start(xT_hi[:, :, :].bitcast(F32), xnT_hi_d[b]))
                    xT_load.mark(eng.dma_start(xT_lo[:, :, :].bitcast(F32), xnT_lo_d[b]))
                    ends(xT_load)
                load_xT(0)

                def batch(b, nxt):
                    xr_store.wait(eng, b - 1)
                    xr_load.mark(eng.dma_start(xr[:, :, :], t["L0_attn_x"][b].rearrange("(n p) c -> p n c", p=P)))
                    pe_q.wait(eng, b * HP + (HP - 1))
                    load_xT(nxt)
                    o_done.wait(eng, b)
                    xr_store.mark(eng.dma_start(x1_d[b].rearrange("(n p) c -> p n c", p=P), xr[:, :, :]))
                    ends(xr_load, xr_store)
                with eng.Fori(0, B - 1) as b:
                    batch(b, b + 1)
                batch(B - 1, B - 1)
                xr_store.wait(eng, B - 1)
                xT_load.wait(eng, B)

            @block.tensor
            def _(eng):
                for e in (pe_q, pe_t, pe_s, pe_pt, pe_y, pe_o):
                    e.credit(eng)

                def project(j, b, hp, tiles):
                    for n in tiles:
                        if n < 2:
                            (raw_even if n == 0 else raw_odd).wait(eng, j - 1, 2)
                        else:
                            (raw_even if n == 2 else raw_odd).wait(eng, j, 1)
                        first = True
                        for k in range(KC):
                            for a, w in ((xT_lo, w_hi), (xT_hi, w_lo), (xT_hi, w_hi)):
                                m = eng.matmul(bQ[n % 2][:, 0:W], a[:, k, n * P:(n + 1) * P], w[:, k, hp, :],
                                               start=first, stop=(k == KC - 1 and a is xT_hi and w is w_hi))
                                first = False
                        pe_q.mark(m)

                def turn_qk(j):
                    norm_done.wait(eng, j)
                    aug_done.wait(eng, j)
                    for i in range(4):
                        free_R(eng, 6 + i, j - 1)
                        for n in range(NT):
                            m = eng.transpose(bR[i % 3][0:DA, n * P:(n + 1) * P], qk[:, n, i, :], ident[:, :])
                        pe_t.mark(m)
                    ends(pe_t)

                def scores(s, h):
                    for c in range(NT):
                        i = NT * h + c
                        if i < 2:
                            maxed.wait(eng, s - 1, i + 7)
                        else:
                            maxed.wait(eng, s, i - 1)
                        m = eng.matmul(bS[i % 2][:, 0:(c + 1) * P], qkT[:, h, c * P:(c + 1) * P],
                                       qkT[:, 2 + h, 0:(c + 1) * P], start=True, stop=True)
                        pe_s.mark(m)

                def turn_p(s, h):
                    p_done.wait(eng, s, 4 * h + 4)
                    for i, chunks in enumerate(((0,), (1,), (2, 3))):
                        free_R(eng, 3 * h + i, s)
                        at = 0
                        for kc in chunks:
                            for c in range(kc, NT):
                                m = eng.transpose(bR[i][:, at:at + P],
                                                  prob[h][:, off[c] + kc * P:off[c] + (kc + 1) * P], ident[:, :])
                                at += P
                        pe_pt.mark(m)

                def values(s):
                    ptA.wait(eng, s)
                    ptD.wait(eng, s)
                    v_done.wait(eng, s)
                    y_done.wait(eng, s - 1)
                    for kc in range(NT):
                        for h in range(2):
                            m = eng.matmul(bY[h * D:(h + 1) * D, kc * P:T], v[:, kc, h * D:(h + 1) * D],
                                           probT[h][:, offT[kc]:offT[kc + 1]], start=(kc == 0), stop=(kc == NT - 1))
                    pe_y.mark(m)
                    ends(pe_y)

                consts.wait(eng, 0)
                xT_load.wait(eng, 0)
                project(0, 0, 0, range(NT))
                ends(pe_q)
                turn_qk(0)

                def turn(s, b, hp, last):
                    nxt = (s + 1, b, 0 if last else hp + 1)
                    if last:
                        xT_load.wait(eng, b + 1)
                    qT_done.wait(eng, s)
                    kT_done.wait(eng, s)
                    o_done.wait(eng, b - 1)
                    scores(s, 0)
                    project(*nxt, (0, 1))
                    scores(s, 1)
                    project(*nxt, (2, 3))
                    turn_p(s, 0)
                    turn_p(s, 1)
                    ends(pe_s, pe_q, pe_pt)
                    turn_qk(s + 1)
                    values(s)
                    if last:
                        y_done.wait(eng, s)
                        for n in range(NT):
                            if n < 2:
                                (raw_even if n == 0 else raw_odd).wait(eng, s + 1, 2)
                            else:
                                o_done.wait(eng, b, n - 1)
                            for h in range(HP):
                                m = eng.matmul(bQ[n % 2][:, 0:C], yT[:, h, n * P:(n + 1) * P], w_proj[:, h, :],
                                               start=(h == 0), stop=(h == HP - 1))
                            pe_o.mark(m)
                        ends(pe_o)
                slots(eng, turn)

            @block.scalar
            def _(eng):
                for e in (raw_even, squared, gate_exp, qT_done, exp_done, ptA):
                    e.credit(eng)

                def copy_raw(j, n):
                    pe_q.wait(eng, j, n + 1)
                    if n == 0:
                        v_done.wait(eng, j - 1)
                        norm_done.wait(eng, j - 1)
                        gate_in.wait(eng, j - 1)
                    raw_even.mark(eng.activation(raw[:, n, :], bQ[n % 2][:, 0:W], ACT.Copy))

                def square(j):
                    raw_even.wait(eng, j)
                    raw_odd.wait(eng, j)
                    ssd.wait(eng, j - 1, 1)
                    squared.mark(eng.activation(sq[:, :, :], raw[:, :, 0:2 * P], ACT.Square))
                    ends(squared)

                def gate(j):
                    gate_in.wait(eng, j)
                    gate_g.wait(eng, j - 1)
                    gate_exp.mark(eng.activation(ge[:, :, :], ge[:, :, :], ACT.Exp))
                    gate_exp.wait(eng, j, 1)
                    gate_exp.mark(eng.activation(gp[:, :, :], ge[:, :, :], ACT.Ln, bias=1.0))
                    ends(gate_exp)

                def copy_q(j):
                    pe_s.wait(eng, j - 1)
                    for i in range(2):
                        pe_t.wait(eng, j, i + 1)
                        qT_done.mark(eng.activation(qkT[:, i, :], bR[i % 3][0:DA, :], ACT.Copy, scale=q_scale[:, 0:1]))
                    ends(qT_done)

                def exps(s, h):
                    negated.wait(eng, s, h + 1)
                    if h == 0:
                        rec_done.wait(eng, s - 1)
                    for c in range(NT):
                        i = NT * h + c
                        sl = prob[h][:, off[c]:off[c + 1]]
                        exp_done.mark(eng.activation(sl, sl, ACT.Exp, bias=nm[:, i:i + 1], accum_out=den[:, i:i + 1]))

                def copy_p(s, us):
                    for u in us:
                        pe_pt.wait(eng, s, u + 1)
                        h, i = u // 3, u % 3
                        ptA.mark(eng.activation(probT[h][:, seg[i][0]:seg[i][1]], bR[i][:, 0:seg[i][1] - seg[i][0]], ACT.Copy))

                seg = ((0, 512), (512, 896), (896, 1280))
                copy_raw(0, 0)
                copy_raw(0, 2)
                ends(raw_even)
                square(0)
                gate(0)
                copy_q(0)

                def turn(s, b, hp, last):
                    exps(s, 0)
                    copy_raw(s + 1, 0)
                    exps(s, 1)
                    copy_raw(s + 1, 2)
                    ends(raw_even, exp_done)
                    square(s + 1)
                    pe_y.wait(eng, s - 1)
                    copy_p(s, (1,))
                    gate(s + 1)
                    copy_p(s, (3, 5))
                    ends(ptA)
                    copy_q(s + 1)
                slots(eng, turn)

            @block.vector
            def _(eng):
                for e in (raw_odd, ssd, norm_done, gate_in, gate_g, kT_done, maxed, negated, rec_done, ptD, y_done,
                          o_done):
                    e.credit(eng)
                seg = ((0, 512), (512, 896), (896, 1280))

                def copy_raw(j, n):
                    pe_q.wait(eng, j, n + 1)
                    if n == 1:
                        v_done.wait(eng, j - 1)
                        squared.wait(eng, j - 1)
                    raw_odd.mark(eng.tensor_copy(raw[:, n, :], bQ[n % 2][:, 0:W]))

                def mean_square(j):
                    squared.wait(eng, j)
                    ssd.mark(eng.tensor_reduce(ss[:, :], sq[:, :, :].rearrange("p n (i d) -> p (n i) d", d=D), AX.X, ALU.add))
                    ssd.wait(eng, j, 1)
                    ssd.mark(eng.tensor_scalar(ss[:, :], ss[:, :], 1.0 / D, EPS, ALU.mult, ALU.add))
                    ends(ssd)

                def norm(j):
                    rs_done.wait(eng, j)
                    raw_even.wait(eng, j)
                    pe_t.wait(eng, j - 1)
                    gate_exp.wait(eng, j - 1)
                    gate_in.mark(eng.tensor_tensor(gl[:, :, :], raw[:, :, 3 * P:W], rs[:, :, 2:4], ALU.mult))
                    norm_done.mark(eng.tensor_tensor(
                        qk[:, :, :, 0:D], raw[:, :, 0:2 * P].rearrange("p n (i d) -> p n i d", d=D),
                        rs[:, :, :].unsqueeze(3).to_broadcast([P, NT, 4, D]), ALU.mult))
                    gate_in.wait(eng, j, 1)
                    gate_in.mark(eng.scalar_tensor_tensor(ge[:, :, :], gl[:, :, :], -1.0, gl[:, :, :], ALU.mult, ALU.min))
                    ends(norm_done, gate_in)

                def gate(j):
                    gate_exp.wait(eng, j)
                    aug_done.wait(eng, j - 1)
                    gate_g.mark(eng.scalar_tensor_tensor(gl[:, :, :], gl[:, :, :], 0.0, gp[:, :, :], ALU.max, ALU.add))
                    ends(gate_g)

                def copy_k(j):
                    pe_s.wait(eng, j - 1)
                    for i in range(2, 4):
                        pe_t.wait(eng, j, i + 1)
                        kT_done.mark(eng.tensor_copy(qkT[:, i, :], bR[i % 3][0:DA, :]))
                    ends(kT_done)

                def maxes(s, h):
                    for c in range(NT):
                        i = NT * h + c
                        if i == 0:
                            pe_pt.wait(eng, s - 1)
                            exp_done.wait(eng, s - 1)
                        pe_s.wait(eng, s, i + 1, alone=True)
                        maxed.mark(eng.tensor_tensor_reduce(
                            out=prob[h][:, off[c]:off[c + 1]], in0=bS[i % 2][:, 0:(c + 1) * P],
                            in1=mask[:, (NT - 1 - c) * P:T], scale=1.0, scalar=LOWEST, op0=ALU.add, op1=ALU.max,
                            accum_out=mx[:, i:i + 1]))
                    maxed.wait(eng, s, 4 * h + 4)
                    negated.mark(eng.tensor_scalar(nm[:, 4 * h:4 * h + 4], mx[:, 4 * h:4 * h + 4], -1.0, None, ALU.mult))

                def recip(s, h):
                    exp_done.wait(eng, s, 4 * h + 4)
                    if h == 0:
                        p_done.wait(eng, s - 1)
                    rec_done.mark(eng.reciprocal(rec[:, 4 * h:4 * h + 4], den[:, 4 * h:4 * h + 4]))

                def copy_p(s, us):
                    for u in us:
                        pe_pt.wait(eng, s, u + 1)
                        h, i = u // 3, u % 3
                        ptD.mark(eng.tensor_copy(probT[h][:, seg[i][0]:seg[i][1]], bR[i][:, 0:seg[i][1] - seg[i][0]]))

                copy_raw(0, 1)
                copy_raw(0, 3)
                ends(raw_odd)
                mean_square(0)
                norm(0)
                gate(0)
                copy_k(0)

                def turn(s, b, hp, last):
                    maxes(s, 0)
                    copy_raw(s + 1, 1)
                    maxes(s, 1)
                    recip(s, 0)
                    copy_raw(s + 1, 3)
                    recip(s, 1)
                    mean_square(s + 1)
                    pe_y.wait(eng, s - 1)
                    copy_p(s, (0,))
                    norm(s + 1)
                    copy_p(s, (2,))
                    gate(s + 1)
                    copy_p(s, (4,))
                    ends(raw_odd, maxed, negated, rec_done, ptD)
                    copy_k(s + 1)
                    pe_y.wait(eng, s)
                    pe_o.wait(eng, b - 1)
                    y_done.mark(eng.tensor_copy(yT[:, hp, :], bY[:, :]))
                    ends(y_done)
                    if last:
                        xr_load.wait(eng, b)
                        for n in range(NT):
                            pe_o.wait(eng, b, n + 1)
                            o_done.mark(eng.tensor_tensor(xr[:, n, :], bQ[n % 2][:, 0:C], xr[:, n, :], ALU.add))
                        ends(o_done)
                slots(eng, turn)

            @block.gpsimd
            def _(eng):
                for e in (rs_done, aug_done, v_done, p_done, consts):
                    e.credit(eng)
                for h in range(2):
                    consts.mark(eng.tensor_scalar(qk[:, :, h, D], pos[:, :], -1.0, None, ALU.mult))
                consts.mark(eng.memset(qk[:, :, 0:2, D + 1], 1.0))

                def rsqrt(j):
                    ssd.wait(eng, j)
                    norm_done.wait(eng, j - 1)
                    rs_done.mark(eng.tensor_tensor(rs[:, :, :].rearrange("p n i -> p (n i)"), ss[:, :], half[:, :],
                                                   ALU.pow))
                    ends(rs_done)

                def augment(j, hp):
                    gate_g.wait(eng, j)
                    pe_t.wait(eng, j - 1)
                    aug_done.mark(eng.tensor_tensor(
                        qk[:, :, 2:4, D], gl[:, :, :],
                        omega[:, bass.ds(hp * 2, 2)].unsqueeze(1).to_broadcast([P, NT, 2]), ALU.mult))
                    aug_done.wait(eng, j, 1)
                    aug_done.mark(eng.tensor_tensor(
                        qk[:, :, 2:4, D + 1], qk[:, :, 2:4, D],
                        pos[:, :].unsqueeze(2).to_broadcast([P, NT, 2]), ALU.mult))
                    ends(aug_done)

                rsqrt(0)
                augment(0, 0)

                def turn(s, b, hp, last):
                    raw_even.wait(eng, s)
                    raw_odd.wait(eng, s)
                    pe_y.wait(eng, s - 1, alone=True)
                    v_done.mark(eng.tensor_copy(v[:, :, :], raw[:, :, 2 * P:3 * P]))
                    ends(v_done)
                    for h in range(2):
                        rec_done.wait(eng, s, h + 1, alone=True)
                        for c in range(NT):
                            i = NT * h + c
                            sl = prob[h][:, off[c]:off[c + 1]]
                            p_done.mark(eng.tensor_scalar(sl, sl, rec[:, i:i + 1], None, ALU.mult))
                    ends(p_done)
                    rsqrt(s + 1)
                    augment(s + 1, 0 if last else hp + 1)
                slots(eng, turn)


def run_experts(nc, t, g):
    B, C, KC, E, F, GRP = (g[k] for k in ("B", "C", "KC", "E", "F", "GRP"))
    ident, merged, eo_d = g["ident"], g["merged"], g["eo_d"]
    FW = F // GRP
    NF = FW // P
    U = 4
    with ExitStack() as ctx:
        sb = g["sb_in"](ctx)
        w1 = [sb(f"w1_{u}", [P, KC, F]) for u in range(U)]
        w1b = [sb(f"w1b_{u}", [1, F]) for u in range(U)]
        w2 = [sb(f"w2_{u}", [P, GRP * NF, C]) for u in range(U)]
        tok = sb("tok", [P, U, KC, E])
        one = sb("one", [1, E])
        hid = [sb(f"hid{u}", [P, FW]) for u in range(2)]
        hidT = [sb(f"hidT{u}", [P, NF, P]) for u in range(2)]
        eo = sb("eo", [P, E, C])
        bH, bT, bO = (g["banks"](ctx, 2, n) for n in ("xh", "xt", "xo"))
        ev = lambda name, per, unit=1: Event(ctx, nc, name, per, unit, g["carrier"])
        wl = [ev(f"wl{u}", 3, 16) for u in range(U)]
        st = ev("eo_store", GRP, 16)
        tok0, tok_done = ev("tok0", 2), ev("tok_done", 1)
        pe_h, pe_t, pe_o = ev("xpe_h", U), ev("xpe_t", U), ev("xpe_o", U)
        hid_done, hidT_done, eo_done = ev("hid_done", U), ev("hidT_done", U), ev("eo_done", U)
        NTURN = E // U
        with nc.Block() as block:
            @block.sync
            def _(eng):
                for e in (*wl, st):
                    e.credit(eng)
                with eng.Fori(0, NTURN) as i:
                    for u in range(U):
                        e = i * U + u
                        pe_o.wait(eng, i - 1, u + 1)
                        wl[u].mark(eng.dma_start(w1[u][:, :, :], t["L0_ffn_w1"][e, 0:C, :].rearrange("(k p) f -> p k f", p=P)))
                        wl[u].mark(eng.dma_start(w1b[u][:, :], t["L0_ffn_w1"][e, C:C + 1, :]))
                        wl[u].mark(eng.dma_start(w2[u][:, :, :], t["L0_ffn_w2"][e, 0:F, :].rearrange("(j p) c -> p j c", p=P)))
                        wl[u].turn_ends()
                eo_done.wait(eng, NTURN - 1)
                for j in range(GRP):
                    st.mark(eng.dma_start(eo_d[j], eo[j * E:j * E + B, :, :]))
                st.wait(eng, 0)

            @block.gpsimd
            def _(eng):
                for e in (tok0, tok_done):
                    e.credit(eng)
                tok0.mark(eng.memset(tok[:, :, :, :], 0.0))
                tok0.mark(eng.memset(one[:, :], 1.0))
                tok0.wait(eng, 0)
                with eng.Fori(0, NTURN) as i:
                    pe_h.wait(eng, i - 1)
                    tok_done.mark(eng.tensor_copy(
                        tok[:, :, :, 0:B], merged[:, :, bass.ds(i * U, U), :].rearrange("p k u b -> p u k b")))
                    tok_done.turn_ends()

            @block.tensor
            def _(eng):
                for e in (pe_h, pe_t, pe_o):
                    e.credit(eng)
                tok0.wait(eng, 0)
                with eng.Fori(0, NTURN) as i:
                    tok_done.wait(eng, i)
                    for u in range(U):
                        wl[u].wait(eng, i)
                        if u < 2:
                            hid_done.wait(eng, i - 1, u + 3)
                        else:
                            hid_done.wait(eng, i, u - 1)
                        for k in range(KC + 1):
                            for j in range(GRP):
                                o = bH[u % 2][j * E:(j + 1) * E, 0:FW]
                                if k < KC:
                                    m = eng.matmul(o, tok[:, u, k, :], w1[u][:, k, j * FW:(j + 1) * FW],
                                                   start=(k == 0), stop=False)
                                else:
                                    m = eng.matmul(o, one[:, :], w1b[u][:, j * FW:(j + 1) * FW], start=False, stop=True,
                                                   tile_position=(0, j * E))
                        pe_h.mark(m)
                        hid_done.wait(eng, i, u + 1)
                        for f in range(NF):
                            m = eng.transpose(bT[u % 2][:, f * P:(f + 1) * P], hid[u % 2][:, f * P:(f + 1) * P], ident[:, :])
                        pe_t.mark(m)
                        hidT_done.wait(eng, i, u + 1)
                        if u < 2:
                            eo_done.wait(eng, i - 1, u + 3)
                        else:
                            eo_done.wait(eng, i, u - 1)
                        for f in range(NF):
                            for j in range(GRP):
                                m = eng.matmul(bO[u % 2][j * E:(j + 1) * E, 0:C], hidT[u % 2][:, f, j * E:(j + 1) * E],
                                               w2[u][:, j * NF + f, :], start=(f == 0), stop=(f == NF - 1))
                        pe_o.mark(m)
                    for e in (pe_h, pe_t, pe_o):
                        e.turn_ends()

            @block.scalar
            def _(eng):
                hid_done.credit(eng)
                with eng.Fori(0, NTURN) as i:
                    for u in range(U):
                        pe_h.wait(eng, i, u + 1)
                        if u < 2:
                            pe_t.wait(eng, i - 1, u + 3)
                        else:
                            pe_t.wait(eng, i, u - 1)
                        hid_done.mark(eng.activation(hid[u % 2][:, :], bH[u % 2][:, 0:FW], ACT.Gelu))
                    hid_done.turn_ends()

            @block.vector
            def _(eng):
                for e in (hidT_done, eo_done):
                    e.credit(eng)
                with eng.Fori(0, NTURN) as i:
                    for u in range(U):
                        pe_t.wait(eng, i, u + 1)
                        hidT_done.mark(eng.tensor_copy(hidT[u % 2][:, :, :],
                                                       bT[u % 2][:, 0:FW].rearrange("p (f q) -> p f q", f=NF)))
                        pe_o.wait(eng, i, u + 1)
                        eo_done.mark(eng.tensor_copy(eo[:, i * U + u, :], bO[u % 2][:, 0:C]))
                    hidT_done.turn_ends()
                    eo_done.turn_ends()


def second_layer(nc, t, out, g):
    B, T, C, NT, KC, E, NB, HC, M1, TOPK, GRP, F = (g[k] for k in (
        "B", "T", "C", "NT", "KC", "E", "NB", "HC", "M1", "TOPK", "GRP", "F"))
    ident, half, pick_d, x1_d, eo_d = g["ident"], g["half"], g["pick_d"], g["x1_d"], g["eo_d"]
    with ExitStack() as ctx:
        sb = g["sb_in"](ctx)
        b2e = sb("b2e", [E, C])
        rT = sb("rT", [P, KC, NB])
        rb = sb("rb", [P, NB])
        b1 = sb("b1", [P, HC])
        up_hi = sb("up_hi", [P, KC, HC, P], F32R)
        up_lo = sb("up_lo", [P, KC, HC, P], F32R)
        downT = sb("downT", [P, HC, C])
        readT_hi = sb("readT_hi", [P, KC, P], F32R)
        readT_lo = sb("readT_lo", [P, KC, P], F32R)
        backT = sb("backT", [M1 + 1, C])
        spread = sb("spread", [NB, HC, P], F32R)
        number = sb("number", [P, NB])

        with ExitStack() as c2:
            sb2 = g["sb_in"](c2)
            w1n = sb2("w1n", [P, HC, C])
            w2n = sb2("w2n", [P, KC, HC * P])
            wk = sb2("wk", [P, KC, C])
            m1n = sb2("m1n", [M1, C])
            m1T = sb2("m1T", [P, KC, M1])
            m2n = sb2("m2n", [P, KC, M1])
            rn = sb2("rn", [NB, C])
            sp = sb2("sp", [NB, HC, P])
            sld = c2.enter_context(nc.semaphore("sld"))
            pe, dv, hi, po = (Chain(c2, nc, n, 0) for n in ("pe_s3", "dv_s3", "hi_s3", "po_s3"))
            bk = g["banks"](c2, 2, "s3")
            jobs = []
            for h in range(HC):
                for k in range(KC):
                    jobs.append(("up", (k, h), w1n[:, h, k * P:(k + 1) * P], P, P))
            for h in range(HC):
                for k in range(KC):
                    jobs.append(("down", (k, h), w2n[:, k, h * P:(h + 1) * P], P, P))
            for k in range(KC):
                jobs.append(("m1", k, m1n[:, k * P:(k + 1) * P], M1, P))
                jobs.append(("m2", k, m2n[:, k, :], P, M1))
                jobs.append(("r", k, rn[:, k * P:(k + 1) * P], NB, P))
            for k in range(KC):
                jobs.append(("read", k, None, 0, 0))
            with nc.Block() as block:
                @block.sync
                def _(eng):
                    for dst, src in (
                        (w1n[:, :, :], t["L1_ffn_w1"].rearrange("(h p) c -> p h c", p=P)),
                        (w2n[:, :, :], t["L1_ffn_w2"].rearrange("(k p) f -> p k f", p=P)),
                        (wk[:, :, :], t["L1_attn_W_K"].rearrange("(k p) c -> p k c", p=P)),
                        (m1n[:, :], t["L1_attn_W1"]),
                        (m2n[:, :, :], t["L1_attn_W2"].rearrange("(k p) m -> p k m", p=P)),
                        (rn[:, :], t["L1_ffn_router_w"]),
                        (rb[:, :], t["L1_ffn_router_b"].partition_broadcast(P)),
                        (b2e[:, :], t["L0_ffn_w2"][:, F, :]),
                        (backT[M1:M1 + 1, :], t["L1_ffn_b2"].unsqueeze(0)),
                    ):
                        eng.dma_start(dst, src).then_inc(sld, 16)
                    with nc.allow_non_contiguous_dma(reason="1024 biases, once"):
                        eng.dma_start(b1[:, :], t["L1_ffn_b1"].rearrange("(h p) -> p h", p=P)).then_inc(sld, 16)
                    eng.wait_ge(sld, 160)

                @block.gpsimd
                def _(eng):
                    po.mark(eng.iota(number[:, :], pattern=[[1, NB]], base=0, channel_multiplier=0,
                                     allow_small_or_imprecise_dtypes=True))
                    po.mark(eng.memset(sp[:, :, :], 1.0))
                    po.settle(eng, -1)
                    w = HC * P // NB
                    po.mark(eng.affine_select(out=sp[:, :, :], in_=sp[:, :, :], compare_op=ALU.is_ge, fill=0.0, base=0,
                                              pattern=[[P, HC], [1, P]], channel_multiplier=-w))
                    po.settle(eng, -1)
                    po.mark(eng.affine_select(out=sp[:, :, :], in_=sp[:, :, :], compare_op=ALU.is_ge, fill=0.0,
                                              base=w - 1, pattern=[[-P, HC], [-1, P]], channel_multiplier=w))

                @block.tensor
                def _(eng):
                    eng.wait_ge(sld, 160)
                    for n, (what, _, src, rows, cols) in enumerate(jobs):
                        if n >= 2:
                            dv.wait(eng, -1, n - 1)
                        if what == "read":
                            k = jobs[n][1]
                            dv.wait(eng, -1, len(jobs) - KC)
                            for kk in range(KC):
                                m = eng.matmul(bk[n % 2][:, 0:M1], wk[:, kk, k * P:(k + 1) * P], m1T[:, kk, :],
                                               start=(kk == 0), stop=(kk == KC - 1))
                        else:
                            m = eng.transpose(bk[n % 2][0:cols, 0:rows], src, ident[0:rows, 0:rows])
                        pe.mark(m)

                @block.vector
                def _(eng):
                    for n, (what, at, _, rows, cols) in enumerate(jobs):
                        pe.wait(eng, -1, n + 1)
                        b = bk[n % 2]
                        if what == "up":
                            k, h = at
                            hi.mark(eng.tensor_copy(up_hi[:, k, h, :], b[:, 0:P]))
                            hi.settle(eng, -1)
                            m = eng.tensor_tensor(up_lo[:, k, h, :], b[:, 0:P], up_hi[:, k, h, :].bitcast(F32), ALU.subtract)
                        elif what == "down":
                            k, h = at
                            m = eng.tensor_copy(downT[:, h, k * P:(k + 1) * P], b[:, 0:P])
                        elif what == "m1":
                            m = eng.tensor_copy(m1T[:, at, :], b[:, 0:M1])
                        elif what == "m2":
                            m = eng.tensor_copy(backT[0:M1, at * P:(at + 1) * P], b[0:M1, 0:P])
                        elif what == "r":
                            m = eng.tensor_copy(rT[:, at, :], b[:, 0:NB])
                        else:
                            hi.mark(eng.tensor_copy(readT_hi[:, at, 0:M1], b[:, 0:M1]))
                            hi.settle(eng, -1)
                            m = eng.tensor_tensor(readT_lo[:, at, 0:M1], b[:, 0:M1],
                                                  readT_hi[:, at, 0:M1].bitcast(F32), ALU.subtract)
                        dv.mark(m)
                    for part in (readT_hi, readT_lo):
                        eng.tensor_scalar(part[:, :, M1:P], up_lo[:, :, 0, M1:P].bitcast(F32), 0.0, None, ALU.mult)
                    po.wait(eng, -1, 4)
                    eng.tensor_copy(spread[:, :, :], sp[:, :, :])

        xr = sb("xr3", [P, NT, C])
        x1 = sb("x1", [P, 2, NT, C])
        xT_hi = sb("xT3_hi", [P, 2, KC, T], F32R)
        xT_lo = sb("xT3_lo", [P, 2, KC, T], F32R)
        shutT = sb("shutT", [NB, 2, T], F32R)
        pick4 = sb("pick4", [P, T])
        eo = sb("eo3", [P, C])
        stats = sb("stats3", [P, NT, 6])
        mv = sb("mv3", [P, NT, 2])
        var = sb("var3", [P, NT])
        rstd = sb("rstd3", [P, NT])
        xn = sb("xn3", [P, NT, C])
        xT = sb("xT3", [P, KC, T])
        logit = sb("logit3", [P, NT, NB])
        top = sb("top3", [P, NT, 8])
        idx = sb("idx3", [P, NT, 8], U32)
        idxf = sb("idxf3", [P, NT, 8])
        eq = sb("eq3", [P, NT, NB, TOPK])
        shut = sb("shut3", [P, NT, NB])
        mem = sb("mem3", [M1 + 1, T])
        hT = sb("hT3", [P, HC, T])
        xo = sb("xo3", [P, NT, C])
        b8 = g["banks"](ctx, 7, "l1")
        bF, bR, bU, bD = b8[0:2], b8[2], b8[3:5], b8[5:7]

        ev = lambda name, per, unit=1: Event(ctx, nc, name, per, unit, g["carrier"])
        load, store = ev("load3", 2 * GRP + 1, 16), ev("store3", 1, 16)
        pe_add, pe_xT, pe_r, pe_shut = ev("pe_add", 2), ev("pe_xT3", 2), ev("pe_r", 1), ev("pe_shut", 1)
        pe_mem, pe_up, pe_down = ev("pe_mem", 1), ev("pe_up", HC), ev("pe_down", 2)
        xT_done, mem_done, relu_done = ev("xT_done3", 2), ev("mem_done", 1), ev("relu_done", HC)
        eo_biased, x1_done, stat, agg, var_done = ev("eo_biased", 1), ev("x1_done", 2), ev("stat", NT), ev("agg", NT), ev("var_done3", 1)
        xn_done, hi_done, lo_done = ev("xn_done3", NT), ev("hi_done", 1), ev("lo_done", 1)
        logit_done, route, shut_done, shutT_done, out_done = (
            ev("logit_done", 1), ev("route", 2 * NT + 3), ev("shut_done", 1), ev("shutT_done", 1), ev("out_done", 2))
        rstd_done, mem_one = ev("rstd_done", 1), ev("mem_one", 1)

        def ends(*events):
            for e in events:
                e.turn_ends()

        with nc.Block() as block:
            @block.sync
            def _(eng):
                for e in (load, store):
                    e.credit(eng)

                def get(b):
                    load.mark(eng.dma_start(xr[:, :, :], x1_d[b].rearrange("(n p) c -> p n c", p=P)))
                    for j in range(GRP):
                        load.mark(eng.dma_start(pick4[j * E:(j + 1) * E, :], pick_d[b]))
                        load.mark(eng.dma_start(eo[j * E:(j + 1) * E, :], eo_d[j, b]))
                    ends(load)

                def put(b):
                    out_done.wait(eng, b)
                    store.mark(eng.dma_start(out[b].rearrange("(n p) c -> p n c", p=P), xo[:, :, :]))
                    ends(store)

                def free(b):
                    pe_add.wait(eng, b)
                    x1_done.wait(eng, b)
                get(0)
                free(0)
                get(1)
                with eng.Fori(0, B - 2) as b:
                    free(b + 1)
                    get(b + 2)
                    put(b)
                put(B - 2)
                put(B - 1)
                store.wait(eng, B - 1)

            def turns(eng, front_of_first, turn, last):
                front_of_first()
                with eng.Fori(0, B - 1) as b:
                    turn(b)
                last(B - 1)

            @block.tensor
            def _(eng):
                for e in (pe_add, pe_xT, pe_r, pe_shut, pe_mem, pe_up, pe_down):
                    e.credit(eng)

                def add(b):
                    eo_biased.wait(eng, b)
                    lo_done.wait(eng, b - 1)
                    shutT_done.wait(eng, b - 1)
                    for n in range(NT):
                        m = eng.matmul(bF[n // 2][:, (n % 2) * C:(n % 2 + 1) * C], pick4[:, n * P:(n + 1) * P], eo[:, :],
                                       start=True, stop=True)
                        if n % 2:
                            pe_add.mark(m)
                    ends(pe_add)

                def turn_x(b):
                    xn_done.wait(eng, b)
                    x1_done.wait(eng, b)
                    for k in range(KC):
                        for n in range(NT):
                            m = eng.transpose(bF[k][:, n * P:(n + 1) * P], xn[:, n, k * P:(k + 1) * P], ident[:, :])
                        pe_xT.mark(m)
                    ends(pe_xT)

                def router(b):
                    xT_done.wait(eng, b)
                    logit_done.wait(eng, b - 1)
                    for n in range(NT):
                        for k in range(KC):
                            m = eng.matmul(bR[:, n * NB:(n + 1) * NB], xT[:, k, n * P:(n + 1) * P], rT[:, k, :],
                                           start=(k == 0), stop=(k == KC - 1))
                    pe_r.mark(m)
                    ends(pe_r)

                def turn_shut(b):
                    shut_done.wait(eng, b)
                    for n in range(NT):
                        m = eng.transpose(bF[0][0:NB, n * P:(n + 1) * P], shut[:, n, :], ident[:, :])
                    pe_shut.mark(m)
                    ends(pe_shut)

                def product(b, bank, hi, lo, first, done):
                    start = first
                    for k in range(KC):
                        for w, x in ((lo, xT_hi), (hi, xT_lo), (hi, xT_hi)):
                            m = eng.matmul(bank[:, :], w[:, k, :], x[:, b % 2, k, :], start=start,
                                           stop=(k == KC - 1 and w is hi and x is xT_hi))
                            start = False
                    done.mark(m)

                def memory(b):
                    lo_done.wait(eng, b)
                    shutT_done.wait(eng, b)
                    relu_done.wait(eng, b - 1, HC)
                    product(b, bU[1], readT_hi, readT_lo, True, pe_mem)
                    ends(pe_mem)

                def up(b, hs):
                    for h in hs:
                        if h == 0:
                            relu_done.wait(eng, b - 1, HC - 1, alone=True)
                        elif h == 1:
                            mem_done.wait(eng, b, alone=True)
                        else:
                            relu_done.wait(eng, b, h - 1, alone=True)
                        eng.matmul(bU[h % 2][:, :], spread[:, h, :], shutT[:, b % 2, :], start=True, stop=False)
                        product(b, bU[h % 2], up_hi[:, :, h, :], up_lo[:, :, h, :], False, pe_up)
                    if h == HC - 1:
                        ends(pe_up)

                def down(b, ns):
                    for n in ns:
                        if n == 0:
                            relu_done.wait(eng, b)
                            mem_one.wait(eng, 0)
                            mem_done.wait(eng, b)
                        if n % 2 == 0:
                            out_done.wait(eng, b - 1, n // 2 + 1)
                        o = bD[n // 2][:, (n % 2) * C:(n % 2 + 1) * C]
                        eng.matmul(o, mem[:, n * P:(n + 1) * P], backT[:, :], start=True, stop=False)
                        for h in range(HC):
                            m = eng.matmul(o, hT[:, h, n * P:(n + 1) * P], downT[:, h, :], start=False, stop=(h == HC - 1))
                        if n % 2:
                            pe_down.mark(m)
                    if n == NT - 1:
                        ends(pe_down)

                def first():
                    add(0)
                    turn_x(0)
                    router(0)
                    turn_shut(0)

                def turn(b):
                    add(b + 1)
                    memory(b)
                    up(b, range(0, 3))
                    turn_x(b + 1)
                    up(b, range(3, 6))
                    router(b + 1)
                    up(b, range(6, HC))
                    down(b, (0, 1))
                    turn_shut(b + 1)
                    down(b, (2, 3))

                def last(b):
                    memory(b)
                    up(b, range(HC))
                    down(b, range(NT))
                turns(eng, first, turn, last)

            @block.scalar
            def _(eng):
                for e in (xT_done, mem_done, relu_done):
                    e.credit(eng)

                def copy_x(b):
                    hi_done.wait(eng, b - 1)
                    lo_done.wait(eng, b - 1)
                    pe_r.wait(eng, b - 1)
                    for k in range(KC):
                        pe_xT.wait(eng, b, k + 1)
                        xT_done.mark(eng.activation(xT[:, k, :], bF[k][:, :], ACT.Copy))
                    ends(xT_done)

                def memory(b):
                    pe_mem.wait(eng, b)
                    pe_down.wait(eng, b - 1)
                    mem_done.mark(eng.activation(mem[0:M1, :], bU[1][0:M1, :], ACT.Gelu))
                    ends(mem_done)

                def relu(b, hs):
                    for h in hs:
                        pe_up.wait(eng, b, h + 1)
                        relu_done.mark(eng.activation(hT[:, h, :], bU[h % 2][:, :], ACT.Relu, bias=b1[:, h:h + 1]))
                    if h == HC - 1:
                        ends(relu_done)

                def turn(b):
                    memory(b)
                    relu(b, range(0, 3))
                    copy_x(b + 1)
                    relu(b, range(3, HC))

                def last(b):
                    memory(b)
                    relu(b, range(HC))
                turns(eng, lambda: copy_x(0), turn, last)

            @block.gpsimd
            def _(eng):
                rstd_done.credit(eng)
                mem_one.credit(eng)
                mem_one.mark(eng.memset(mem[M1:M1 + 1, :], 1.0))
                mem_one.wait(eng, 0)
                with eng.Fori(0, B) as b:
                    var_done.wait(eng, b)
                    xn_done.wait(eng, b - 1)
                    rstd_done.mark(eng.tensor_tensor(rstd[:, :], var[:, :], half[:, 0:NT], ALU.pow))
                    rstd_done.turn_ends()

            @block.vector
            def _(eng):
                for e in (eo_biased, x1_done, stat, agg, var_done, xn_done, hi_done, lo_done, logit_done, route,
                          shut_done, shutT_done, out_done):
                    e.credit(eng)

                def norm(b):
                    load.wait(eng, b)
                    eo_biased.mark(eng.tensor_tensor(eo[0:E, :], eo[0:E, :], b2e[:, :], ALU.add))
                    out_done.wait(eng, b - 2)
                    for i in range(2):
                        pe_add.wait(eng, b, i + 1)
                        x1_done.mark(eng.tensor_tensor(
                            x1[:, b % 2, 2 * i:2 * i + 2, :], bF[i][:, :].rearrange("p (n c) -> p n c", n=2),
                            xr[:, 2 * i:2 * i + 2, :], ALU.add))
                    x1_done.wait(eng, b, alone=True)
                    for n in range(NT):
                        stat.mark(eng.bn_stats(stats[:, n, :], x1[:, b % 2, n, :]))
                    stat.wait(eng, b, alone=True)
                    for n in range(NT):
                        agg.mark(eng.bn_aggr(mv[:, n, :], stats[:, n, :]))
                    agg.wait(eng, b)
                    var_done.mark(eng.tensor_scalar(var[:, :], mv[:, :, 1], EPS, None, ALU.add))
                    rstd_done.wait(eng, b)
                    pe_xT.wait(eng, b - 1)
                    for n in range(NT):
                        xn_done.mark(eng.tensor_scalar(xn[:, n, :], x1[:, b % 2, n, :], mv[:, n, 0:1],
                                                       rstd[:, n:n + 1], ALU.subtract, ALU.mult))
                    ends(eo_biased, x1_done, stat, agg, var_done, xn_done)

                def split(b):
                    xT_done.wait(eng, b)
                    pe_up.wait(eng, b - 2)
                    hi_done.mark(eng.tensor_copy(xT_hi[:, b % 2, :, :], xT[:, :, :]))
                    hi_done.wait(eng, b)
                    lo_done.mark(eng.tensor_tensor(xT_lo[:, b % 2, :, :], xT[:, :, :],
                                                   xT_hi[:, b % 2, :, :].bitcast(F32), ALU.subtract))
                    ends(hi_done, lo_done)

                def choose(b):
                    pe_r.wait(eng, b)
                    logit_done.mark(eng.tensor_tensor(
                        logit[:, :, :], bR[:, 0:NT * NB].rearrange("p (n i) -> p n i", n=NT),
                        rb[:, :].unsqueeze(1).to_broadcast([P, NT, NB]), ALU.add))
                    logit_done.wait(eng, b, alone=True)
                    for n in range(NT):
                        route.mark(eng.max(top[:, n, :], logit[:, n, :]))
                    route.wait(eng, b, NT, alone=True)
                    for n in range(NT):
                        route.mark(eng.max_index(idx[:, n, :], top[:, n, :], logit[:, n, :]))
                    route.wait(eng, b, 2 * NT)
                    route.mark(eng.tensor_copy(idxf[:, :, :], idx[:, :, :]))
                    route.wait(eng, b, 2 * NT + 1)
                    full = [P, NT, NB, TOPK]
                    route.mark(eng.tensor_tensor(
                        eq[:, :, :, :], idxf[:, :, 0:TOPK].unsqueeze(2).to_broadcast(full),
                        number[:, :].unsqueeze(1).unsqueeze(3).to_broadcast(full), ALU.is_equal))
                    route.wait(eng, b, 2 * NT + 2)
                    pe_shut.wait(eng, b - 1)
                    route.mark(eng.tensor_reduce(shut[:, :, :], eq[:, :, :, :], AX.X, ALU.add))
                    route.wait(eng, b)
                    shut_done.mark(eng.tensor_scalar(shut[:, :, :], shut[:, :, :], -1.0, -NEG, ALU.add, ALU.mult))
                    ends(logit_done, route, shut_done)

                def copy_shut(b):
                    pe_shut.wait(eng, b)
                    pe_up.wait(eng, b - 2)
                    shutT_done.mark(eng.tensor_copy(shutT[:, b % 2, :], bF[0][0:NB, :]))
                    ends(shutT_done)

                def finish(b):
                    store.wait(eng, b - 1)
                    for i in range(2):
                        pe_down.wait(eng, b, i + 1)
                        out_done.mark(eng.tensor_tensor(
                            xo[:, 2 * i:2 * i + 2, :], bD[i][:, :].rearrange("p (n c) -> p n c", n=2),
                            x1[:, b % 2, 2 * i:2 * i + 2, :], ALU.add))
                    ends(out_done)

                def front(b):
                    norm(b)
                    split(b)
                    choose(b)
                    copy_shut(b)

                def turn(b):
                    norm(b + 1)
                    split(b + 1)
                    choose(b + 1)
                    copy_shut(b + 1)
                    finish(b)
                turns(eng, lambda: front(0), turn, finish)


_INS = ["L0_attn_x", "L0_attn_Wq", "L0_attn_Wk", "L0_attn_Wv", "L0_attn_Wproj", "L0_attn_q_rms_w", "L0_attn_k_rms_w",
        "L0_attn_omega", "L0_attn_u", "L0_ffn_gate_w", "L0_ffn_gate_b", "L0_ffn_w1", "L0_ffn_w2", "L1_attn_W_K",
        "L1_attn_W1", "L1_attn_W2", "L1_ffn_router_w", "L1_ffn_router_b", "L1_ffn_w1", "L1_ffn_b1", "L1_ffn_w2",
        "L1_ffn_b2"]


def kernel(**inputs):
    import numpy as np
    import concourse.bacc as bacc
    from concourse.bass_utils import run_bass_kernel_spmd

    nc = bacc.Bacc("TRN2", target_bir_lowering=False, num_devices=1)
    arrays, t = {}, {}
    for name in _INS:
        arrays["in_" + name] = np.ascontiguousarray(inputs[name])
        t[name] = nc.dram_tensor("in_" + name, arrays["in_" + name].shape, F32, kind="ExternalInput").ap()
    out = nc.dram_tensor("out", arrays["in_L0_attn_x"].shape, F32, kind="ExternalOutput").ap()
    build(nc, t, out)
    return run_bass_kernel_spmd(nc, [arrays], core_ids=[0]).results[0]["out"]
```

```python
from contextlib import ExitStack

import concourse.bass as bass
import concourse.mybir as mybir

F32 = mybir.dt.float32
F32R = mybir.dt.float32r
U32 = mybir.dt.uint32
ALU = mybir.AluOpType
ACT = mybir.ActivationFunctionType
AX = mybir.AxisListType

P = 128
EPS = 1e-5
NEG = -1.0e30
LOWEST = -3.0e38


class Event:

    def __init__(self, ctx, nc, name, per, unit=1, carrier=None):
        self.name, self.per, self.unit, self.n = name, per, unit, 0
        self.carrier = carrier
        self.sem = ctx.enter_context(nc.semaphore(name))

    def credit(self, eng):
        eng.sem_inc(self.sem, self.per * self.unit)

    def mark(self, instruction):
        self.n += 1
        instruction.then_inc(self.sem, self.unit)
        return instruction

    def turn_ends(self):
        assert self.n == self.per, (self.name, self.n, self.per)
        self.n = 0

    def wait(self, eng, turn, n=None, alone=False):
        n = self.per if n is None else n
        value = (turn + 1) * (self.per * self.unit) + n * self.unit
        if isinstance(value, int) and value <= 0:
            return
        eng.wait_ge(self.sem, value)
        if alone:
            eng.sem_inc(self.carrier, 1)


class Chain(Event):

    def settle(self, eng, turn, alone=False):
        self.wait(eng, turn, self.n, alone)


def alibi_slopes(heads):
    start = 2.0 ** (-8.0 / heads)
    return [start * start ** i for i in range(heads)]


def build(nc, t, out):
    x_in = t["L0_attn_x"]
    B, T, C = x_in.shape
    NT = T // P
    KC = C // P
    H, D = t["L0_attn_u"].shape
    HP = H // 2
    E = t["L0_ffn_gate_w"].shape[0]
    F = t["L0_ffn_w1"].shape[2]
    NB = t["L1_ffn_router_w"].shape[0]
    HID = t["L1_ffn_w1"].shape[0]
    HC = HID // P
    M1 = t["L1_attn_W1"].shape[0]
    TOPK = NB // 4
    GRP = P // E
    assert (B, T, C, H, D, E, F) == (8, 512, 256, 16, 64, 32, 1024) and GRP == 4

    scratch = lambda name, shape, dt=F32: nc.dram_tensor(name, shape, dt, kind="Internal").ap()
    xnT_hi_d = scratch("xnT_hi_d", (B, P, KC, T))
    xnT_lo_d = scratch("xnT_lo_d", (B, P, KC, T))
    pick_d = scratch("pick_d", (B, E, T))
    x1_d = scratch("x1_d", (B, T, C))
    eo_d = scratch("eo_d", (GRP, B, E, C))

    with ExitStack() as whole:
        def sb_in(ctx):
            return lambda name, shape, dt=F32: ctx.enter_context(nc.sbuf_tensor(name, shape, dt))

        def banks(ctx, n, name):
            return [ctx.enter_context(nc.psum_tensor(f"{name}{i}", [P, 512], F32)) for i in range(n)]

        sb = sb_in(whole)
        ident = sb("ident", [P, P])
        merged = sb("merged", [P, KC, E, B])
        half = sb("half", [P, 16])
        carrier = whole.enter_context(nc.semaphore("carrier"))

        with ExitStack() as ctx, nc.Block() as block:
            s_zero = ctx.enter_context(nc.semaphore("s_zero"))

            @block.gpsimd
            def _(eng):
                eng.memset(ident[:, :], 0.0).then_inc(s_zero, 1)
                eng.memset(half[:, :], -0.5)
                eng.wait_ge(s_zero, 1)
                eng.affine_select(out=ident[:, :], in_=ident[:, :], compare_op=ALU.not_equal, fill=1.0,
                                  base=0, pattern=[[-1, P]], channel_multiplier=1)

        g = dict(B=B, T=T, C=C, NT=NT, KC=KC, H=H, D=D, HP=HP, E=E, F=F, NB=NB, HC=HC, M1=M1, TOPK=TOPK, GRP=GRP,
                 sb_in=sb_in, banks=banks, ident=ident, merged=merged, half=half, carrier=carrier,
                 xnT_hi_d=xnT_hi_d, xnT_lo_d=xnT_lo_d, pick_d=pick_d, x1_d=x1_d, eo_d=eo_d)
        route_tokens(nc, t, g)
        attend(nc, t, g)
        run_experts(nc, t, g)
        second_layer(nc, t, out, g)


def route_tokens(nc, t, g):
    B, T, C, NT, KC, E = (g[k] for k in ("B", "T", "C", "NT", "KC", "E"))
    ident, merged, half = g["ident"], g["merged"], g["half"]
    xnT_hi_d, xnT_lo_d, pick_d = g["xnT_hi_d"], g["xnT_lo_d"], g["pick_d"]
    with ExitStack() as ctx:
        sb = g["sb_in"](ctx)
        gate_in = sb("gate_in", [E, C])
        gateT = sb("gateT", [P, KC, E])
        gate_b = sb("gate_b", [E, 1])
        x = sb("x", [P, NT, C])
        xn = sb("xn", [P, NT, C])
        stats = sb("stats", [P, NT, 6])
        mv = sb("mv", [P, NT, 2])
        var = sb("var", [P, NT])
        rstd = sb("rstd", [P, NT])
        xT = sb("xT", [P, KC, T])
        xT_hi = sb("xT_hi", [P, KC, T], F32R)
        xT_lo = sb("xT_lo", [P, KC, T], F32R)
        logits = sb("logits", [E, T])
        top8 = sb("top8", [E, 8])
        left = sb("left", [E, T])
        nmax = sb("nmax", [E, 1])
        expd = sb("expd", [E, T])
        den = sb("den", [E, 1])
        rden = sb("rden", [E, 1])
        pick = sb("pick", [E, T])
        pickT = sb("pickT", [P, NT, E])
        bT0, bT1, bL, bG, bP, bM = g["banks"](ctx, 6, "rt")
        bT = [bT0, bT1]

        ev = lambda name, per, unit=1: Event(ctx, nc, name, per, unit, g["carrier"])
        gate_load, gate_t, gate_copied = ev("gate_load", 2, 16), ev("gate_t", 1), ev("gate_copied", 1)
        load, store, store_p = ev("load", 1, 16), ev("store", 2, 16), ev("store_p", 1, 16)
        dve, act, pool = (Chain(ctx, nc, n, k, 1, g["carrier"]) for n, k in (("dve_rt", 21), ("act_rt", 4), ("pool_rt", 1)))
        xn_done, split_done, pick_done = ev("xn_done", 1), ev("split_done", 2), ev("pick_done", 1)
        var_done, merged_done, pickT_done = ev("var_done", 1), ev("merged_done", 1), ev("pickT_done", 1)
        pe_xT, pe_gate, pe_pickT, pe_merged = ev("pe_xT", 2), ev("pe_gate", 1), ev("pe_pickT", 1), ev("pe_merged", 1)
        xT_done, logits_done, exp_done = ev("xT_done", 2), ev("logits_done", 1), ev("exp_done", 1)

        with nc.Block() as block:
            @block.sync
            def _(eng):
                for e in (gate_load, load, store, store_p):
                    e.credit(eng)
                gate_load.mark(eng.dma_start(gate_in[:, :], t["L0_ffn_gate_w"]))
                gate_load.mark(eng.dma_start(gate_b[:, :], t["L0_ffn_gate_b"].unsqueeze(1)))
                load.mark(eng.dma_start(x[:, :, :], t["L0_attn_x"][0].rearrange("(n p) c -> p n c", p=P)))
                load.turn_ends()

                def put(b):
                    split_done.wait(eng, b)
                    store.mark(eng.dma_start(xnT_hi_d[b], xT_hi[:, :, :].bitcast(F32)))
                    store.mark(eng.dma_start(xnT_lo_d[b], xT_lo[:, :, :].bitcast(F32)))
                    pick_done.wait(eng, b)
                    store_p.mark(eng.dma_start(pick_d[b], pick[:, :]))
                    store.turn_ends()
                    store_p.turn_ends()
                with eng.Fori(0, B - 1) as b:
                    xn_done.wait(eng, b)
                    load.mark(eng.dma_start(x[:, :, :],
                                            t["L0_attn_x"][b + 1].rearrange("(n p) c -> p n c", p=P)))
                    load.turn_ends()
                    put(b)
                put(B - 1)
                store.wait(eng, B - 1)
                store_p.wait(eng, B - 1)

            @block.tensor
            def _(eng):
                for e in (gate_t, pe_xT, pe_gate, pe_pickT, pe_merged):
                    e.credit(eng)
                gate_load.wait(eng, 0)
                for k in range(KC):
                    m = eng.transpose(bG[:, k * E:(k + 1) * E], gate_in[:, k * P:(k + 1) * P], ident[0:E, 0:E])
                gate_t.mark(m)
                with eng.Fori(0, B) as b:
                    xn_done.wait(eng, b)
                    for k in range(KC):
                        xT_done.wait(eng, b - 1, k + 1)
                        for n in range(NT):
                            m = eng.transpose(bT[k][:, n * P:(n + 1) * P], xn[:, n, k * P:(k + 1) * P], ident[:, :])
                        pe_xT.mark(m)
                    pe_xT.turn_ends()
                    gate_copied.wait(eng, 0)
                    logits_done.wait(eng, b - 1)
                    for k in range(KC):
                        xT_done.wait(eng, b, k + 1)
                        m = eng.matmul(bL[0:E, :], gateT[:, k, :], xT[:, k, :], start=(k == 0), stop=(k == KC - 1))
                    pe_gate.mark(m)
                    pe_gate.turn_ends()
                    pick_done.wait(eng, b)
                    pickT_done.wait(eng, b - 1, alone=True)
                    for n in range(NT):
                        m = eng.transpose(bP[:, n * E:(n + 1) * E], pick[:, n * P:(n + 1) * P], ident[0:E, 0:E])
                    pe_pickT.mark(m)
                    pe_pickT.turn_ends()
                    pickT_done.wait(eng, b)
                    merged_done.wait(eng, b - 1)
                    for k in range(KC):
                        for n in range(NT):
                            m = eng.matmul(bM[:, k * E:(k + 1) * E], xn[:, n, k * P:(k + 1) * P], pickT[:, n, :],
                                           start=(n == 0), stop=(n == NT - 1))
                    pe_merged.mark(m)
                    pe_merged.turn_ends()

            @block.scalar
            def _(eng):
                for e in (act, xT_done, logits_done, exp_done):
                    e.credit(eng)
                with eng.Fori(0, B) as b:
                    split_done.wait(eng, b - 1)
                    for k in range(KC):
                        pe_xT.wait(eng, b, k + 1)
                        xT_done.mark(eng.activation(xT[:, k, :], bT[k][:, :], ACT.Copy))
                    xT_done.turn_ends()
                    gate_load.wait(eng, 0)
                    pe_gate.wait(eng, b)
                    pick_done.wait(eng, b - 1)
                    logits_done.mark(eng.activation(logits[:, :], bL[0:E, :], ACT.Identity, bias=gate_b[:, 0:1]))
                    logits_done.turn_ends()
                    var_done.wait(eng, b)
                    exp_done.mark(eng.activation(expd[:, :], logits[:, :], ACT.Exp, bias=nmax[:, 0:1],
                                                 accum_out=den[:, 0:1]))
                    exp_done.turn_ends()

            @block.gpsimd
            def _(eng):
                pool.credit(eng)
                with eng.Fori(0, B) as b:
                    dve.wait(eng, b, 9)
                    pool.mark(eng.tensor_tensor(rstd[:, :], var[:, :], half[:, 0:NT], ALU.pow))
                    pool.turn_ends()

            @block.vector
            def _(eng):
                for e in (dve, xn_done, split_done, pick_done, var_done, merged_done, pickT_done, gate_copied):
                    e.credit(eng)
                gate_t.wait(eng, 0)
                gate_copied.mark(eng.tensor_copy(gateT[:, :, :], bG[:, 0:KC * E].rearrange("p (k e) -> p k e", k=KC)))
                with eng.Fori(0, B) as b:
                    load.wait(eng, b)
                    for n in range(NT):
                        dve.mark(eng.bn_stats(stats[:, n, :], x[:, n, :]))
                    dve.settle(eng, b, alone=True)
                    for n in range(NT):
                        dve.mark(eng.bn_aggr(mv[:, n, :], stats[:, n, :]))
                    dve.settle(eng, b)
                    dve.mark(eng.tensor_scalar(var[:, :], mv[:, :, 1], EPS, None, ALU.add))
                    pool.wait(eng, b)
                    pe_merged.wait(eng, b - 1)
                    for n in range(NT):
                        m = eng.tensor_scalar(xn[:, n, :], x[:, n, :], mv[:, n, 0:1], rstd[:, n:n + 1],
                                              ALU.subtract, ALU.mult)
                        if n == NT - 1:
                            xn_done.mark(m)
                        else:
                            dve.mark(m)
                    xn_done.turn_ends()
                    store.wait(eng, b - 1)
                    for k in range(KC):
                        xT_done.wait(eng, b, k + 1)
                        dve.mark(eng.tensor_copy(xT_hi[:, k, :], xT[:, k, :]))
                    dve.settle(eng, b)
                    for k in range(KC):
                        split_done.mark(eng.tensor_tensor(xT_lo[:, k, :], xT[:, k, :], xT_hi[:, k, :].bitcast(F32),
                                                          ALU.subtract))
                    split_done.turn_ends()
                    logits_done.wait(eng, b, alone=True)
                    dve.mark(eng.max(top8[:, :], logits[:, :]))
                    dve.settle(eng, b)
                    var_done.mark(eng.tensor_scalar(nmax[:, :], top8[:, 0:1], -1.0, None, ALU.mult))
                    var_done.turn_ends()
                    dve.mark(eng.match_replace(left[:, :], top8[:, :], logits[:, :], LOWEST))
                    exp_done.wait(eng, b)
                    dve.mark(eng.reciprocal(rden[:, :], den[:, :]))
                    dve.settle(eng, b)
                    dve.mark(eng.scalar_tensor_tensor(left[:, :], left[:, :], LOWEST / 2, expd[:, :],
                                                      ALU.is_le, ALU.mult))
                    dve.settle(eng, b)
                    store_p.wait(eng, b - 1)
                    pick_done.mark(eng.tensor_scalar(pick[:, :], left[:, :], rden[:, 0:1], None, ALU.mult))
                    pick_done.turn_ends()
                    pe_pickT.wait(eng, b)
                    pickT_done.mark(eng.tensor_copy(pickT[:, :, :],
                                                    bP[:, 0:NT * E].rearrange("p (n e) -> p n e", n=NT)))
                    pickT_done.turn_ends()
                    pe_merged.wait(eng, b)
                    merged_done.mark(eng.tensor_copy(merged[:, :, :, b],
                                                     bM[:, 0:KC * E].rearrange("p (k e) -> p k e", k=KC)))
                    merged_done.turn_ends()
                    while dve.n < dve.per:
                        dve.mark(eng.engine_nop())
                    dve.turn_ends()


def attend(nc, t, g):
    B, T, C, NT, KC, H, D, HP = (g[k] for k in ("B", "T", "C", "NT", "KC", "H", "D", "HP"))
    ident, half = g["ident"], g["half"]
    xnT_hi_d, xnT_lo_d, x1_d = g["xnT_hi_d"], g["xnT_lo_d"], g["x1_d"]
    W = 3 * P + 2
    DA = D + 2
    off = [P * c * (c + 1) // 2 for c in range(NT + 1)]
    offT = [0, 512, 896, 1152, 1280]
    slopes = alibi_slopes(H)
    with ExitStack() as ctx:
        sb = g["sb_in"](ctx)
        w_hi = sb("w_hi", [P, KC, HP, W], F32R)
        w_lo = sb("w_lo", [P, KC, HP, W], F32R)
        w_proj = sb("w_proj", [P, HP, C])
        mask = sb("mask", [P, T])
        pos = sb("pos", [P, NT])
        omega = sb("omega", [P, H])
        q_scale = sb("q_scale", [DA, 1])

        with ExitStack() as c2:
            sb2 = g["sb_in"](c2)
            raw_w = sb2("raw_w", [P, KC, 3, H * D])
            u = sb2("u", [P, H, D])
            kw = sb2("kw", [P, D])
            tmp = sb2("tmp", [P, H, D])
            ss = sb2("ss", [P, H])
            slope = sb2("slope", [P, H])
            om = sb2("om", [P, H])
            e0 = sb2("e0", [P, H])
            l0 = sb2("l0", [P, H])
            gk = sb2("gk", [P, KC, H])
            qk_w = sb2("qk_w", [DA, 2])
            s_ld = c2.enter_context(nc.semaphore("s_ld"))
            dv, po, ac = (Chain(c2, nc, n, 0) for n in ("dv_s", "po_s", "ac_s"))
            with nc.Block() as block:
                @block.sync
                def _(eng):
                    for m, w in enumerate(("L0_attn_Wq", "L0_attn_Wk", "L0_attn_Wv")):
                        eng.dma_start(raw_w[:, :, m, :], t[w].rearrange("(k p) n -> p k n", p=P)).then_inc(s_ld, 16)
                    eng.dma_start(w_proj[:, :, :], t["L0_attn_Wproj"].rearrange("(h p) c -> p h c", p=P)).then_inc(s_ld, 16)
                    eng.dma_start(u[:, :, :], t["L0_attn_u"].partition_broadcast(P)).then_inc(s_ld, 16)
                    eng.dma_start(kw[:, :], t["L0_attn_k_rms_w"].partition_broadcast(P)).then_inc(s_ld, 16)
                    eng.dma_start(om[:, :], t["L0_attn_omega"].partition_broadcast(P)).then_inc(s_ld, 16)
                    eng.dma_start(qk_w[0:D, 0:1], t["L0_attn_q_rms_w"].unsqueeze(1)).then_inc(s_ld, 16)
                    eng.dma_start(qk_w[0:D, 1:2], t["L0_attn_k_rms_w"].unsqueeze(1)).then_inc(s_ld, 16)

                @block.gpsimd
                def _(eng):
                    po.mark(eng.memset(mask[:, :], 0.0))
                    po.mark(eng.iota(pos[:, :], pattern=[[P, NT]], base=-(T // 2), channel_multiplier=1,
                                     allow_small_or_imprecise_dtypes=True))
                    po.mark(eng.memset(q_scale[:, :], 1.0))
                    for h in range(H):
                        po.mark(eng.memset(slope[:, h:h + 1], slopes[h]))
                    po.wait(eng, -1, 1)
                    po.mark(eng.affine_select(out=mask[:, T - P:T], in_=mask[:, T - P:T], compare_op=ALU.is_ge,
                                              fill=NEG, base=0, pattern=[[-1, P]], channel_multiplier=1))
                    dv.wait(eng, -1, 4)
                    po.mark(eng.tensor_tensor(ss[:, :], ss[:, :], half[:, 0:H], ALU.pow))

                @block.scalar
                def _(eng):
                    dv.wait(eng, -1, 5)
                    ac.mark(eng.activation(e0[:, :], e0[:, :], ACT.Exp))
                    ac.settle(eng, -1)
                    ac.mark(eng.activation(l0[:, :], e0[:, :], ACT.Ln, bias=1.0))

                @block.vector
                def _(eng):
                    eng.wait_ge(s_ld, 9 * 16)
                    dv.mark(eng.tensor_tensor(tmp[:, :, :], u[:, :, :], u[:, :, :], ALU.mult))
                    dv.settle(eng, -1)
                    dv.mark(eng.tensor_reduce(ss[:, :], tmp[:, :, :], AX.X, ALU.add))
                    dv.mark(eng.tensor_tensor(u[:, :, :], u[:, :, :],
                                              kw[:, :].unsqueeze(1).to_broadcast([P, H, D]), ALU.mult))
                    dv.settle(eng, -1)
                    dv.mark(eng.tensor_scalar(ss[:, :], ss[:, :], 1e-12, None, ALU.max))
                    dv.mark(eng.scalar_tensor_tensor(e0[:, :], om[:, :], -1.0, om[:, :], ALU.mult, ALU.min))
                    ac.wait(eng, -1, 2)
                    dv.mark(eng.scalar_tensor_tensor(om[:, :], om[:, :], 0.0, l0[:, :], ALU.max, ALU.add))
                    po.wait(eng, -1, 3 + H)
                    dv.settle(eng, -1)
                    dv.mark(eng.tensor_tensor(omega[:, :], om[:, :], slope[:, :], ALU.mult))
                    dv.mark(eng.scalar_tensor_tensor(q_scale[0:D, :], qk_w[0:D, 0:1], float(D) ** -0.5, qk_w[0:D, 1:2],
                                                     ALU.mult, ALU.mult))
                    po.wait(eng, -1, 5 + H)
                    dv.mark(eng.tensor_tensor(u[:, :, :], u[:, :, :],
                                              ss[:, :].unsqueeze(2).to_broadcast([P, H, D]), ALU.mult))
                    dv.settle(eng, -1)
                    dv.mark(eng.tensor_scalar(u[:, :, :], u[:, :, :], float(D) ** -0.5, None, ALU.mult))
                    for k in range(KC):
                        dv.settle(eng, -1)
                        dv.mark(eng.tensor_tensor(tmp[:, :, :], raw_w[:, k, 1, :].rearrange("p (h d) -> p h d", h=H),
                                                  u[:, :, :], ALU.mult))
                        dv.settle(eng, -1)
                        dv.mark(eng.tensor_reduce(gk[:, k, :], tmp[:, :, :], AX.X, ALU.add))
                    dv.settle(eng, -1)
                    for k in range(KC):
                        parts = [(m * P, P, raw_w[:, k, m, :]) for m in range(3)] + [(3 * P, 2, gk[:, k, :])]
                        for at, n, src in parts:
                            src = src.rearrange("p (h n) -> p h n", n=n)
                            dv.mark(eng.tensor_copy(w_hi[:, k, :, at:at + n], src))
                            dv.settle(eng, -1)
                            dv.mark(eng.tensor_tensor(w_lo[:, k, :, at:at + n], src,
                                                      w_hi[:, k, :, at:at + n].bitcast(F32), ALU.subtract))

        xT_hi = sb("cT_hi", [P, KC, T], F32R)
        xT_lo = sb("cT_lo", [P, KC, T], F32R)
        raw = sb("raw", [P, 2, NT, W])
        sq = sb("sq", [P, NT, 2 * P])
        ss = sb("ssq", [P, NT * 4])
        rs = sb("rs", [P, NT, 4])
        gl = sb("gl", [P, NT, 2])
        ge = sb("ge", [P, NT, 2])
        gp = sb("gp", [P, NT, 2])
        qk = sb("qk", [P, NT, 4, DA])
        qkT = sb("qkT", [DA, 4, T])
        v = sb("v", [P, NT, P])
        prob = [sb(f"prob{h}", [P, off[NT]]) for h in range(2)]
        probT = [sb(f"probT{h}", [P, off[NT]]) for h in range(2)]
        mx = sb("mx", [P, 2 * NT])
        nm = sb("nm", [P, 2 * NT])
        den = sb("dens", [P, 2 * NT])
        rec = sb("rec", [P, 2 * NT])
        yT = sb("yT", [P, HP, T])
        xr = sb("xr", [P, NT, C])
        v_ring = sb("v_ring", [P, 2, NT, P])
        lnv = sb("lnv", [P, NT * 4])
        r0 = sb("r0", [P, NT * 4])
        nw = sb("nw", [P, NT * 4])
        bank = g["banks"](ctx, 8, "at")
        bQ, bR, bS, bY = bank[0:2], bank[2:5], bank[5:7], bank[7]

        ev = lambda name, per, unit=1: Event(ctx, nc, name, per, unit, g["carrier"])
        xT_load, xr_load, xr_store = ev("xT_load", 2, 16), ev("xr_load", 1, 16), ev("xr_store", 1, 16)
        pe_q, pe_t, pe_s, pe_y = ev("pe_q", 4), ev("pe_t", 4), ev("pe_s", 8), ev("pe_y", 1)
        pe_pt = ev("pe_pt0", 3), ev("pe_pt1", 3)
        pe_o = ev("pe_o", 4)
        raw_A, squared, r0_done, gate_exp, qkT_A = (
            ev("raw_A", NT - 1), ev("squared", 1), ev("r0_done", 2), ev("gate_exp", 2), ev("qkT_A", 2))
        exp_done, pt0_A, pt1_A, y_done = ev("p_exp", 8), ev("pt0_A", 2), ev("pt1_A", 2), ev("y_done", 1)
        raw_D, ssd, newton, norm_done, gate_in, gate_g, qkT_D = (
            ev("raw_D", 1), ev("ssd", 2), ev("newton", 3), ev("norm_done", 1), ev("gate_in", 2), ev("gate_g", 1),
            ev("qkT_D", 2))
        maxed, negated, rec_done, p_done, pt0_D, pt1_D = (
            ev("maxed", 8), ev("negated", 4), ev("rec_done", 2), ev("p_done", 2), ev("pt0_D", 1), ev("pt1_D", 1))
        o_done = ev("o_done", 4)
        aug_done, v_taken, v_done, consts = ev("aug_done", 2), ev("v_taken", 1), ev("v_done", 1), ev("consts", 3)

        def ends(*events):
            for e in events:
                e.turn_ends()

        def copied(u, s):
            return ((pt0_A, s, 1), (pt0_A, s, 2), (pt0_D, s, 1),
                    (qkT_D, s + 1, 1), (qkT_A, s + 1, 1), (qkT_D, s + 1, 2), (qkT_A, s + 1, 2),
                    (pt1_A, s, 1), (pt1_A, s, 2), (pt1_D, s, 1))[u]

        def free_R(eng, u, s):
            event, turn, n = copied((9, 7, 8)[u], s - 1) if u < 3 else copied(u - 3, s)
            event.wait(eng, turn, n)

        def copy_P(eng, copy, u, s):
            h, i = (0, u) if u < 3 else (1, u - 7)
            (x, y), (event, _, _) = segT[i], copied(u, s)
            pe_pt[h].wait(eng, s, i + 1)
            event.mark(copy(probT[h][:, x:y], bR[u % 3][:, 0:y - x]))
        qk_of_unit = (0, 2, 1, 3)
        segT = ((0, 512), (512, 896), (896, 1280))

        def at_start(s):
            return isinstance(s, int) and s == 0

        with nc.Block() as block:
            def turns(eng, first, turn, finish):
                first()
                turn(0, 0, None)
                with eng.Fori(0, B - 1) as b:
                    with eng.Fori(1, HP) as hp:
                        turn(b * HP + hp, hp, None)
                    turn(b * HP + HP, 0, b)
                with eng.Fori(1, HP) as hp:
                    turn((B - 1) * HP + hp, hp, None)
                finish(B * HP, B - 1)

            @block.sync
            def _(eng):
                for e in (xT_load, xr_load, xr_store):
                    e.credit(eng)

                def load_xT(b):
                    xT_load.mark(eng.dma_start(xT_hi[:, :, :].bitcast(F32), xnT_hi_d[b]))
                    xT_load.mark(eng.dma_start(xT_lo[:, :, :].bitcast(F32), xnT_lo_d[b]))
                    ends(xT_load)
                load_xT(0)

                def batch(b, nxt):
                    xr_store.wait(eng, b - 1)
                    xr_load.mark(eng.dma_start(xr[:, :, :], t["L0_attn_x"][b].rearrange("(n p) c -> p n c", p=P)))
                    pe_q.wait(eng, b * HP + (HP - 1))
                    load_xT(nxt)
                    o_done.wait(eng, b)
                    xr_store.mark(eng.dma_start(x1_d[b].rearrange("(n p) c -> p n c", p=P), xr[:, :, :]))
                    ends(xr_load, xr_store)
                with eng.Fori(0, B - 1) as b:
                    batch(b, b + 1)
                batch(B - 1, B - 1)
                xr_store.wait(eng, B - 1)
                xT_load.wait(eng, B)

            @block.tensor
            def _(eng):
                for e in (pe_q, pe_t, pe_s, *pe_pt, pe_y, pe_o):
                    e.credit(eng)

                def project(j, hp):
                    for n in range(NT):
                        if n < 2:
                            raw_A.wait(eng, j - 1, n + 2)
                        elif n == 2:
                            raw_D.wait(eng, j)
                        else:
                            raw_A.wait(eng, j, 1)
                        first = True
                        for k in range(KC):
                            for a, w in ((xT_lo, w_hi), (xT_hi, w_lo), (xT_hi, w_hi)):
                                m = eng.matmul(bQ[n % 2][:, 0:W], a[:, k, n * P:(n + 1) * P], w[:, k, hp, :],
                                               start=first, stop=(k == KC - 1 and a is xT_hi and w is w_hi))
                                first = False
                        pe_q.mark(m)
                    ends(pe_q)

                def turn_qk(j, fresh=False):
                    norm_done.wait(eng, j)
                    aug_done.wait(eng, j)
                    for u, i in enumerate(qk_of_unit, 3):
                        if u == 6 or not fresh:
                            free_R(eng, u, j - 1)
                        for n in range(NT):
                            m = eng.transpose(bR[u % 3][0:DA, n * P:(n + 1) * P], qk[:, n, i, :], ident[:, :])
                        pe_t.mark(m)
                    ends(pe_t)

                def scores(s, h):
                    for c in range(NT):
                        i = NT * h + c
                        if i < 2:
                            maxed.wait(eng, s - 1, i + 7)
                        else:
                            maxed.wait(eng, s, i - 1)
                        m = eng.matmul(bS[i % 2][:, 0:(c + 1) * P], qkT[:, h, c * P:(c + 1) * P],
                                       qkT[:, 2 + h, 0:(c + 1) * P], start=True, stop=True)
                        pe_s.mark(m)

                def turn_p(s, h):
                    p_done.wait(eng, s, h + 1)
                    for i, chunks in enumerate(((0,), (1,), (2, 3))):
                        u = 7 * h + i
                        free_R(eng, u, s)
                        at = 0
                        for kc in chunks:
                            for c in range(kc, NT):
                                m = eng.transpose(bR[u % 3][:, at:at + P],
                                                  prob[h][:, off[c] + kc * P:off[c] + (kc + 1) * P], ident[:, :])
                                at += P
                        pe_pt[h].mark(m)
                    ends(pe_pt[h])

                def values(s):
                    for e in (pt0_A, pt0_D, pt1_A, pt1_D):
                        e.wait(eng, s)
                    v_done.wait(eng, s)
                    y_done.wait(eng, s - 1)
                    for kc in range(NT):
                        for h in range(2):
                            m = eng.matmul(bY[h * D:(h + 1) * D, kc * P:T], v[:, kc, h * D:(h + 1) * D],
                                           probT[h][:, offT[kc]:offT[kc + 1]], start=(kc == 0), stop=(kc == NT - 1))
                    pe_y.mark(m)
                    ends(pe_y)

                def output(s, b, projected):
                    raw_A.wait(eng, projected)
                    raw_D.wait(eng, projected)
                    y_done.wait(eng, s)
                    for n in range(NT):
                        if n >= 2:
                            o_done.wait(eng, b, n - 1)
                        for h in range(HP):
                            m = eng.matmul(bQ[n % 2][:, 0:C], yT[:, h, n * P:(n + 1) * P], w_proj[:, h, :],
                                           start=(h == 0), stop=(h == HP - 1))
                        pe_o.mark(m)
                    ends(pe_o)

                def first():
                    consts.wait(eng, 0)
                    xT_load.wait(eng, 0)
                    project(0, 0)
                    project(1, 1)
                    turn_qk(0, fresh=True)

                def turn(s, hp, ended):
                    qkT_A.wait(eng, s)
                    qkT_D.wait(eng, s)
                    scores(s, 0)
                    xT_load.wait(eng, (s + 2) // HP)
                    if not at_start(s):
                        o_done.wait(eng, (s - 1) // HP - 1)
                    project(s + 2, (hp + 2) % HP)
                    scores(s, 1)
                    ends(pe_s)
                    if not at_start(s):
                        values(s - 1)
                    turn_p(s, 0)
                    turn_qk(s + 1)
                    turn_p(s, 1)
                    if ended is not None:
                        output(s - 1, ended, s + 2)

                def finish(s, b):
                    values(s - 1)
                    output(s - 1, b, s + 1)
                turns(eng, first, turn, finish)

            @block.scalar
            def _(eng):
                for e in (raw_A, squared, r0_done, gate_exp, qkT_A, exp_done, pt0_A, pt1_A, y_done):
                    e.credit(eng)
                eng.preload_act_table_set("natural_log_exp_and_others")

                def project(j):
                    for n in range(1, NT):
                        pe_q.wait(eng, j, n + 1)
                        if n == 1:
                            v_taken.wait(eng, j - 2)
                            norm_done.wait(eng, j - 2)
                            gate_in.wait(eng, j - 2)
                        raw_A.mark(eng.activation(raw[:, j % 2, n, :], bQ[n % 2][:, 0:W], ACT.Copy))
                    ends(raw_A)

                def square(j):
                    raw_A.wait(eng, j)
                    raw_D.wait(eng, j)
                    ssd.wait(eng, j - 1, 1)
                    squared.mark(eng.activation(sq[:, :, :], raw[:, j % 2, :, 0:2 * P], ACT.Square))
                    ends(squared)

                def rsqrt(j):
                    ssd.wait(eng, j)
                    r0_done.mark(eng.activation(lnv[:, :], ss[:, :], ACT.Ln))
                    newton.wait(eng, j - 1)
                    r0_done.wait(eng, j, 1)
                    r0_done.mark(eng.activation(r0[:, :], lnv[:, :], ACT.Exp, scale=-0.5))
                    ends(r0_done)

                def gate(j):
                    gate_in.wait(eng, j)
                    gate_g.wait(eng, j - 1)
                    gate_exp.mark(eng.activation(ge[:, :, :], ge[:, :, :], ACT.Exp))
                    gate_exp.wait(eng, j, 1)
                    gate_exp.mark(eng.activation(gp[:, :, :], ge[:, :, :], ACT.Ln, bias=1.0))
                    ends(gate_exp)

                def copy_qk(j):
                    pe_s.wait(eng, j - 1)
                    pe_t.wait(eng, j, 2)
                    qkT_A.mark(eng.activation(qkT[:, 2, :], bR[1][0:DA, :], ACT.Copy))
                    pe_t.wait(eng, j, 4)
                    qkT_A.mark(eng.activation(qkT[:, 3, :], bR[0][0:DA, :], ACT.Copy))
                    ends(qkT_A)

                def exps(s, h):
                    if h == 0:
                        rec_done.wait(eng, s - 1)
                    for c in range(NT):
                        i = NT * h + c
                        if c in (0, NT - 1):
                            negated.wait(eng, s, 2 * h + 1 + (c > 0))
                        sl = prob[h][:, off[c]:off[c + 1]]
                        exp_done.mark(eng.activation(sl, sl, ACT.Exp, bias=nm[:, i:i + 1], accum_out=den[:, i:i + 1]))

                def copy_p0(s):
                    pe_y.wait(eng, s - 1)
                    copy_P(eng, copy, 0, s)
                    copy_P(eng, copy, 1, s)
                    ends(pt0_A)

                def copy_p1(s):
                    copy_P(eng, copy, 7, s)
                    copy_P(eng, copy, 8, s)
                    ends(pt1_A)

                def copy(dst, src):
                    return eng.activation(dst, src, ACT.Copy)

                def copy_y(s, hp):
                    pe_o.wait(eng, s // HP - 1)
                    pe_y.wait(eng, s)
                    y_done.mark(copy(yT[:, hp, :], bY[:, :]))
                    ends(y_done)

                def first():
                    project(0)
                    square(0)
                    rsqrt(0)
                    gate(0)
                    project(1)
                    square(1)
                    copy_qk(0)
                    rsqrt(1)
                    gate(1)

                def turn(s, hp, ended):
                    exps(s, 0)
                    project(s + 2)
                    square(s + 2)
                    exps(s, 1)
                    ends(exp_done)
                    rsqrt(s + 2)
                    copy_p0(s)
                    if not at_start(s):
                        copy_y(s - 1, (hp + HP - 1) % HP)
                    copy_qk(s + 1)
                    copy_p1(s)
                    gate(s + 2)
                turns(eng, first, turn, lambda s, b: copy_y(s - 1, HP - 1))

            @block.vector
            def _(eng):
                for e in (raw_D, ssd, newton, norm_done, gate_in, gate_g, qkT_D, maxed, negated, rec_done, p_done,
                          pt0_D, pt1_D, o_done):
                    e.credit(eng)

                def project(j):
                    pe_q.wait(eng, j, 1)
                    v_taken.wait(eng, j - 2)
                    squared.wait(eng, j - 2)
                    raw_D.mark(eng.tensor_copy(raw[:, j % 2, 0, :], bQ[0][:, 0:W]))
                    ends(raw_D)

                def mean_square(j):
                    squared.wait(eng, j)
                    ssd.mark(eng.tensor_reduce(ss[:, :], sq[:, :, :].rearrange("p n (i d) -> p (n i) d", d=D), AX.X, ALU.add))
                    ssd.wait(eng, j, 1)
                    ssd.mark(eng.tensor_scalar(ss[:, :], ss[:, :], 1.0 / D, EPS, ALU.mult, ALU.add))
                    ends(ssd)

                def newton_step(j):
                    r0_done.wait(eng, j)
                    newton.mark(eng.scalar_tensor_tensor(nw[:, :], r0[:, :], -0.5, r0[:, :], ALU.mult, ALU.mult))
                    newton.wait(eng, j, 1)
                    newton.mark(eng.tensor_tensor(nw[:, :], nw[:, :], ss[:, :], ALU.mult))
                    newton.wait(eng, j, 2)
                    newton.mark(eng.scalar_tensor_tensor(rs[:, :, :].rearrange("p n i -> p (n i)"), nw[:, :], 1.5,
                                                         r0[:, :], ALU.add, ALU.mult))
                    ends(newton)

                def gate_input(j):
                    newton.wait(eng, j)
                    raw_A.wait(eng, j)
                    gate_exp.wait(eng, j - 1)
                    aug_done.wait(eng, j - 1)
                    gate_in.mark(eng.tensor_tensor(gl[:, :, :], raw[:, j % 2, :, 3 * P:W], rs[:, :, 2:4], ALU.mult))
                    gate_in.wait(eng, j, 1)
                    gate_in.mark(eng.scalar_tensor_tensor(ge[:, :, :], gl[:, :, :], -1.0, gl[:, :, :], ALU.mult, ALU.min))
                    ends(gate_in)

                def gate(j):
                    gate_exp.wait(eng, j)
                    gate_g.mark(eng.scalar_tensor_tensor(gl[:, :, :], gl[:, :, :], 0.0, gp[:, :, :], ALU.max, ALU.add))
                    ends(gate_g)

                def norm(j):
                    pe_t.wait(eng, j - 1)
                    norm_done.mark(eng.tensor_tensor(
                        qk[:, :, :, 0:D], raw[:, j % 2, :, 0:2 * P].rearrange("p n (i d) -> p n i d", d=D),
                        rs[:, :, :].unsqueeze(3).to_broadcast([P, NT, 4, D]), ALU.mult))
                    ends(norm_done)

                def copy_q(j, h):
                    pe_s.wait(eng, j - 1)
                    pe_t.wait(eng, j, 2 * h + 1)
                    qkT_D.mark(eng.tensor_scalar(qkT[:, h, :], bR[2 * h][0:DA, :], q_scale[:, 0:1], None, ALU.mult))

                def maxes(s, h):
                    for c in range(NT):
                        i = NT * h + c
                        if c == 0:
                            pe_pt[h].wait(eng, s - 1)
                            exp_done.wait(eng, s - 1)
                        pe_s.wait(eng, s, i + 1, alone=True)
                        maxed.mark(eng.tensor_tensor_reduce(
                            out=prob[h][:, off[c]:off[c + 1]], in0=bS[i % 2][:, 0:(c + 1) * P],
                            in1=mask[:, (NT - 1 - c) * P:T], scale=1.0, scalar=LOWEST, op0=ALU.add, op1=ALU.max,
                            accum_out=mx[:, i:i + 1]))
                        if c >= NT - 2:
                            maxed.wait(eng, s, i + 1)
                            at = NT * h if c == NT - 2 else i
                            negated.mark(eng.tensor_scalar(nm[:, at:i + 1], mx[:, at:i + 1], -1.0, None, ALU.mult))

                def reciprocals(s, h):
                    exp_done.wait(eng, s, 4 * h + 4)
                    rec_done.mark(eng.reciprocal(rec[:, 4 * h:4 * h + 4], den[:, 4 * h:4 * h + 4]))

                def divide(s, h):
                    rec_done.wait(eng, s, h + 1)
                    for c in range(NT):
                        i = NT * h + c
                        sl = prob[h][:, off[c]:off[c + 1]]
                        m = eng.tensor_scalar(sl, sl, rec[:, i:i + 1], None, ALU.mult)
                    p_done.mark(m)

                def copy_p(s, u):
                    pe_y.wait(eng, s - 1)
                    copy_P(eng, eng.tensor_copy, u, s)

                def output(b):
                    xr_load.wait(eng, b)
                    for n in range(NT):
                        pe_o.wait(eng, b, n + 1)
                        o_done.mark(eng.tensor_tensor(xr[:, n, :], bQ[n % 2][:, 0:C], xr[:, n, :], ALU.add))
                    ends(o_done)

                def prepare(j):
                    mean_square(j)
                    newton_step(j)
                    gate_input(j)

                def first():
                    for j in range(2):
                        project(j)
                        if j == 0:
                            prepare(0)
                            gate(0)
                            norm(0)
                    copy_q(0, 0)
                    copy_q(0, 1)
                    ends(qkT_D)
                    prepare(1)

                def turn(s, hp, ended):
                    maxes(s, 0)
                    project(s + 2)
                    gate(s + 1)
                    norm(s + 1)
                    reciprocals(s, 0)
                    divide(s, 0)
                    maxes(s, 1)
                    mean_square(s + 2)
                    reciprocals(s, 1)
                    divide(s, 1)
                    copy_p(s, 2)
                    copy_q(s + 1, 0)
                    newton_step(s + 2)
                    copy_q(s + 1, 1)
                    gate_input(s + 2)
                    copy_p(s, 9)
                    ends(maxed, negated, rec_done, p_done, pt0_D, pt1_D, qkT_D)
                    if ended is not None:
                        output(ended)

                def finish(s, b):
                    output(b)
                turns(eng, first, turn, finish)

            @block.gpsimd
            def _(eng):
                for e in (aug_done, v_taken, v_done, consts):
                    e.credit(eng)
                for h in range(2):
                    consts.mark(eng.tensor_scalar(qk[:, :, h, D], pos[:, :], -1.0, None, ALU.mult))
                consts.mark(eng.memset(qk[:, :, 0:2, D + 1], 1.0))

                def augment(j, hp):
                    gate_g.wait(eng, j)
                    pe_t.wait(eng, j - 1)
                    aug_done.mark(eng.tensor_tensor(
                        qk[:, :, 2:4, D], gl[:, :, :],
                        omega[:, bass.ds(hp * 2, 2)].unsqueeze(1).to_broadcast([P, NT, 2]), ALU.mult))
                    aug_done.wait(eng, j, 1)
                    aug_done.mark(eng.tensor_tensor(
                        qk[:, :, 2:4, D + 1], qk[:, :, 2:4, D],
                        pos[:, :].unsqueeze(2).to_broadcast([P, NT, 2]), ALU.mult))
                    ends(aug_done)

                def take_v(j):
                    raw_A.wait(eng, j)
                    raw_D.wait(eng, j)
                    v_done.wait(eng, j - 2, alone=True)
                    v_taken.mark(eng.tensor_copy(v_ring[:, j % 2, :, :], raw[:, j % 2, :, 2 * P:3 * P]))
                    ends(v_taken)

                def first():
                    augment(0, 0)
                    for j in range(2):
                        take_v(j)

                def turn(s, hp, ended):
                    augment(s + 1, (hp + 1) % HP)
                    v_taken.wait(eng, s)
                    pe_y.wait(eng, s - 1, alone=True)
                    v_done.mark(eng.tensor_copy(v[:, :, :], v_ring[:, s % 2, :, :]))
                    ends(v_done)
                    take_v(s + 2)
                turns(eng, first, turn, lambda s, b: None)


def run_experts(nc, t, g):
    B, C, KC, E, F, GRP = (g[k] for k in ("B", "C", "KC", "E", "F", "GRP"))
    ident, merged, eo_d = g["ident"], g["merged"], g["eo_d"]
    FW = F // GRP
    NF = FW // P
    U = 4
    with ExitStack() as ctx:
        sb = g["sb_in"](ctx)
        w1 = [sb(f"w1_{u}", [P, KC, F]) for u in range(U)]
        w1b = [sb(f"w1b_{u}", [1, F]) for u in range(U)]
        w2 = [sb(f"w2_{u}", [P, GRP * NF, C]) for u in range(U)]
        tok = sb("tok", [P, U, KC, E])
        one = sb("one", [1, E])
        hid = [sb(f"hid{u}", [P, FW]) for u in range(2)]
        hidT = [sb(f"hidT{u}", [P, NF, P]) for u in range(2)]
        eo = sb("eo", [P, E, C])
        bH, bT, bO = (g["banks"](ctx, 2, n) for n in ("xh", "xt", "xo"))
        ev = lambda name, per, unit=1: Event(ctx, nc, name, per, unit, g["carrier"])
        wl = [ev(f"wl{u}", 3, 16) for u in range(U)]
        st = ev("eo_store", GRP, 16)
        tok0, tok_done = ev("tok0", 2), ev("tok_done", 1)
        pe_h, pe_t, pe_o = ev("xpe_h", U), ev("xpe_t", U), ev("xpe_o", U)
        hid_done, hidT_done, eo_done = ev("hid_done", U), ev("hidT_done", U), ev("eo_done", U)
        NTURN = E // U
        with nc.Block() as block:
            @block.sync
            def _(eng):
                for e in (*wl, st):
                    e.credit(eng)
                with eng.Fori(0, NTURN) as i:
                    for u in range(U):
                        e = i * U + u
                        pe_o.wait(eng, i - 1, u + 1)
                        wl[u].mark(eng.dma_start(w1[u][:, :, :], t["L0_ffn_w1"][e, 0:C, :].rearrange("(k p) f -> p k f", p=P)))
                        wl[u].mark(eng.dma_start(w1b[u][:, :], t["L0_ffn_w1"][e, C:C + 1, :]))
                        wl[u].mark(eng.dma_start(w2[u][:, :, :], t["L0_ffn_w2"][e, 0:F, :].rearrange("(j p) c -> p j c", p=P)))
                        wl[u].turn_ends()
                eo_done.wait(eng, NTURN - 1)
                for j in range(GRP):
                    st.mark(eng.dma_start(eo_d[j], eo[j * E:j * E + B, :, :]))
                st.wait(eng, 0)

            @block.gpsimd
            def _(eng):
                for e in (tok0, tok_done):
                    e.credit(eng)
                tok0.mark(eng.memset(tok[:, :, :, :], 0.0))
                tok0.mark(eng.memset(one[:, :], 1.0))
                tok0.wait(eng, 0)
                with eng.Fori(0, NTURN) as i:
                    pe_h.wait(eng, i - 1)
                    tok_done.mark(eng.tensor_copy(
                        tok[:, :, :, 0:B], merged[:, :, bass.ds(i * U, U), :].rearrange("p k u b -> p u k b")))
                    tok_done.turn_ends()

            @block.tensor
            def _(eng):
                for e in (pe_h, pe_t, pe_o):
                    e.credit(eng)
                tok0.wait(eng, 0)
                with eng.Fori(0, NTURN) as i:
                    tok_done.wait(eng, i)
                    for u in range(U):
                        wl[u].wait(eng, i)
                        if u < 2:
                            hid_done.wait(eng, i - 1, u + 3)
                        else:
                            hid_done.wait(eng, i, u - 1)
                        for k in range(KC + 1):
                            for j in range(GRP):
                                o = bH[u % 2][j * E:(j + 1) * E, 0:FW]
                                if k < KC:
                                    m = eng.matmul(o, tok[:, u, k, :], w1[u][:, k, j * FW:(j + 1) * FW],
                                                   start=(k == 0), stop=False)
                                else:
                                    m = eng.matmul(o, one[:, :], w1b[u][:, j * FW:(j + 1) * FW], start=False, stop=True,
                                                   tile_position=(0, j * E))
                        pe_h.mark(m)
                        hid_done.wait(eng, i, u + 1)
                        for f in range(NF):
                            m = eng.transpose(bT[u % 2][:, f * P:(f + 1) * P], hid[u % 2][:, f * P:(f + 1) * P], ident[:, :])
                        pe_t.mark(m)
                        hidT_done.wait(eng, i, u + 1)
                        if u < 2:
                            eo_done.wait(eng, i - 1, u + 3)
                        else:
                            eo_done.wait(eng, i, u - 1)
                        for f in range(NF):
                            for j in range(GRP):
                                m = eng.matmul(bO[u % 2][j * E:(j + 1) * E, 0:C], hidT[u % 2][:, f, j * E:(j + 1) * E],
                                               w2[u][:, j * NF + f, :], start=(f == 0), stop=(f == NF - 1))
                        pe_o.mark(m)
                    for e in (pe_h, pe_t, pe_o):
                        e.turn_ends()

            @block.scalar
            def _(eng):
                hid_done.credit(eng)
                with eng.Fori(0, NTURN) as i:
                    for u in range(U):
                        pe_h.wait(eng, i, u + 1)
                        if u < 2:
                            pe_t.wait(eng, i - 1, u + 3)
                        else:
                            pe_t.wait(eng, i, u - 1)
                        hid_done.mark(eng.activation(hid[u % 2][:, :], bH[u % 2][:, 0:FW], ACT.Gelu))
                    hid_done.turn_ends()

            @block.vector
            def _(eng):
                for e in (hidT_done, eo_done):
                    e.credit(eng)
                with eng.Fori(0, NTURN) as i:
                    for u in range(U):
                        pe_t.wait(eng, i, u + 1)
                        hidT_done.mark(eng.tensor_copy(hidT[u % 2][:, :, :],
                                                       bT[u % 2][:, 0:FW].rearrange("p (f q) -> p f q", f=NF)))
                        pe_o.wait(eng, i, u + 1)
                        eo_done.mark(eng.tensor_copy(eo[:, i * U + u, :], bO[u % 2][:, 0:C]))
                    hidT_done.turn_ends()
                    eo_done.turn_ends()


def second_layer(nc, t, out, g):
    B, T, C, NT, KC, E, NB, HC, M1, TOPK, GRP, F = (g[k] for k in (
        "B", "T", "C", "NT", "KC", "E", "NB", "HC", "M1", "TOPK", "GRP", "F"))
    ident, half, pick_d, x1_d, eo_d = g["ident"], g["half"], g["pick_d"], g["x1_d"], g["eo_d"]
    with ExitStack() as ctx:
        sb = g["sb_in"](ctx)
        b2e = sb("b2e", [E, C])
        rT = sb("rT", [P, KC, NB])
        rb = sb("rb", [P, NB])
        b1 = sb("b1", [P, HC])
        up_hi = sb("up_hi", [P, KC, HC, P], F32R)
        up_lo = sb("up_lo", [P, KC, HC, P], F32R)
        downT = sb("downT", [P, HC, C])
        readT_hi = sb("readT_hi", [P, KC, P], F32R)
        readT_lo = sb("readT_lo", [P, KC, P], F32R)
        backT = sb("backT", [M1 + 1, C])
        spread = sb("spread", [NB, HC, P], F32R)
        number = sb("number", [P, NB])

        with ExitStack() as c2:
            sb2 = g["sb_in"](c2)
            w1n = sb2("w1n", [P, HC, C])
            w2n = sb2("w2n", [P, KC, HC * P])
            wk = sb2("wk", [P, KC, C])
            m1n = sb2("m1n", [M1, C])
            m1T = sb2("m1T", [P, KC, M1])
            m2n = sb2("m2n", [P, KC, M1])
            rn = sb2("rn", [NB, C])
            sp = sb2("sp", [NB, HC, P])
            sld = c2.enter_context(nc.semaphore("sld"))
            pe, dv, hi, po = (Chain(c2, nc, n, 0) for n in ("pe_s3", "dv_s3", "hi_s3", "po_s3"))
            bk = g["banks"](c2, 2, "s3")
            jobs = []
            for h in range(HC):
                for k in range(KC):
                    jobs.append(("up", (k, h), w1n[:, h, k * P:(k + 1) * P], P, P))
            for h in range(HC):
                for k in range(KC):
                    jobs.append(("down", (k, h), w2n[:, k, h * P:(h + 1) * P], P, P))
            for k in range(KC):
                jobs.append(("m1", k, m1n[:, k * P:(k + 1) * P], M1, P))
                jobs.append(("m2", k, m2n[:, k, :], P, M1))
                jobs.append(("r", k, rn[:, k * P:(k + 1) * P], NB, P))
            for k in range(KC):
                jobs.append(("read", k, None, 0, 0))
            with nc.Block() as block:
                @block.sync
                def _(eng):
                    for dst, src in (
                        (w1n[:, :, :], t["L1_ffn_w1"].rearrange("(h p) c -> p h c", p=P)),
                        (w2n[:, :, :], t["L1_ffn_w2"].rearrange("(k p) f -> p k f", p=P)),
                        (wk[:, :, :], t["L1_attn_W_K"].rearrange("(k p) c -> p k c", p=P)),
                        (m1n[:, :], t["L1_attn_W1"]),
                        (m2n[:, :, :], t["L1_attn_W2"].rearrange("(k p) m -> p k m", p=P)),
                        (rn[:, :], t["L1_ffn_router_w"]),
                        (rb[:, :], t["L1_ffn_router_b"].partition_broadcast(P)),
                        (b2e[:, :], t["L0_ffn_w2"][:, F, :]),
                        (backT[M1:M1 + 1, :], t["L1_ffn_b2"].unsqueeze(0)),
                    ):
                        eng.dma_start(dst, src).then_inc(sld, 16)
                    with nc.allow_non_contiguous_dma(reason="1024 biases, once"):
                        eng.dma_start(b1[:, :], t["L1_ffn_b1"].rearrange("(h p) -> p h", p=P)).then_inc(sld, 16)
                    eng.wait_ge(sld, 160)

                @block.gpsimd
                def _(eng):
                    po.mark(eng.iota(number[:, :], pattern=[[1, NB]], base=0, channel_multiplier=0,
                                     allow_small_or_imprecise_dtypes=True))
                    po.mark(eng.memset(sp[:, :, :], 1.0))
                    po.settle(eng, -1)
                    w = HC * P // NB
                    po.mark(eng.affine_select(out=sp[:, :, :], in_=sp[:, :, :], compare_op=ALU.is_ge, fill=0.0, base=0,
                                              pattern=[[P, HC], [1, P]], channel_multiplier=-w))
                    po.settle(eng, -1)
                    po.mark(eng.affine_select(out=sp[:, :, :], in_=sp[:, :, :], compare_op=ALU.is_ge, fill=0.0,
                                              base=w - 1, pattern=[[-P, HC], [-1, P]], channel_multiplier=w))

                @block.tensor
                def _(eng):
                    eng.wait_ge(sld, 160)
                    for n, (what, _, src, rows, cols) in enumerate(jobs):
                        if n >= 2:
                            dv.wait(eng, -1, n - 1)
                        if what == "read":
                            k = jobs[n][1]
                            dv.wait(eng, -1, len(jobs) - KC)
                            for kk in range(KC):
                                m = eng.matmul(bk[n % 2][:, 0:M1], wk[:, kk, k * P:(k + 1) * P], m1T[:, kk, :],
                                               start=(kk == 0), stop=(kk == KC - 1))
                        else:
                            m = eng.transpose(bk[n % 2][0:cols, 0:rows], src, ident[0:rows, 0:rows])
                        pe.mark(m)

                @block.vector
                def _(eng):
                    for n, (what, at, _, rows, cols) in enumerate(jobs):
                        pe.wait(eng, -1, n + 1)
                        b = bk[n % 2]
                        if what == "up":
                            k, h = at
                            hi.mark(eng.tensor_copy(up_hi[:, k, h, :], b[:, 0:P]))
                            hi.settle(eng, -1)
                            m = eng.tensor_tensor(up_lo[:, k, h, :], b[:, 0:P], up_hi[:, k, h, :].bitcast(F32), ALU.subtract)
                        elif what == "down":
                            k, h = at
                            m = eng.tensor_copy(downT[:, h, k * P:(k + 1) * P], b[:, 0:P])
                        elif what == "m1":
                            m = eng.tensor_copy(m1T[:, at, :], b[:, 0:M1])
                        elif what == "m2":
                            m = eng.tensor_copy(backT[0:M1, at * P:(at + 1) * P], b[0:M1, 0:P])
                        elif what == "r":
                            m = eng.tensor_copy(rT[:, at, :], b[:, 0:NB])
                        else:
                            hi.mark(eng.tensor_copy(readT_hi[:, at, 0:M1], b[:, 0:M1]))
                            hi.settle(eng, -1)
                            m = eng.tensor_tensor(readT_lo[:, at, 0:M1], b[:, 0:M1],
                                                  readT_hi[:, at, 0:M1].bitcast(F32), ALU.subtract)
                        dv.mark(m)
                    for part in (readT_hi, readT_lo):
                        eng.tensor_scalar(part[:, :, M1:P], up_lo[:, :, 0, M1:P].bitcast(F32), 0.0, None, ALU.mult)
                    po.wait(eng, -1, 4)
                    eng.tensor_copy(spread[:, :, :], sp[:, :, :])

        xr = sb("xr3", [P, NT, C])
        x1 = sb("x1", [P, 2, NT, C])
        xT_hi = sb("xT3_hi", [P, 2, KC, T], F32R)
        xT_lo = sb("xT3_lo", [P, 2, KC, T], F32R)
        shutT = sb("shutT", [NB, 2, T], F32R)
        pick4 = sb("pick4", [P, T])
        eo = sb("eo3", [P, C])
        stats = sb("stats3", [P, NT, 6])
        mv = sb("mv3", [P, NT, 2])
        var = sb("var3", [P, NT])
        rstd = sb("rstd3", [P, NT])
        xn = sb("xn3", [P, NT, C])
        xT = sb("xT3", [P, KC, T])
        logit = sb("logit3", [P, NT, NB])
        top = sb("top3", [P, NT, 8])
        idx = sb("idx3", [P, NT, 8], U32)
        idxf = sb("idxf3", [P, NT, 8])
        eq = sb("eq3", [P, NT, NB, TOPK])
        shut = sb("shut3", [P, NT, NB])
        mem = sb("mem3", [M1 + 1, T])
        hT = sb("hT3", [P, HC, T])
        xo = sb("xo3", [P, NT, C])
        b8 = g["banks"](ctx, 7, "l1")
        bF, bR, bU, bD = b8[0:2], b8[2], b8[3:5], b8[5:7]

        ev = lambda name, per, unit=1: Event(ctx, nc, name, per, unit, g["carrier"])
        load, store = ev("load3", 2 * GRP + 1, 16), ev("store3", 1, 16)
        pe_add, pe_xT, pe_r, pe_shut = ev("pe_add", 2), ev("pe_xT3", 2), ev("pe_r", 1), ev("pe_shut", 1)
        pe_mem, pe_up, pe_down = ev("pe_mem", 1), ev("pe_up", HC), ev("pe_down", 2)
        xT_done, mem_done, relu_done = ev("xT_done3", 2), ev("mem_done", 1), ev("relu_done", HC)
        eo_biased, x1_done, stat, agg, var_done = ev("eo_biased", 1), ev("x1_done", 2), ev("stat", NT), ev("agg", NT), ev("var_done3", 1)
        xn_done, hi_done, lo_done = ev("xn_done3", NT), ev("hi_done", 1), ev("lo_done", 1)
        logit_done, route, shut_done, shutT_done, out_done = (
            ev("logit_done", 1), ev("route", 2 * NT + 3), ev("shut_done", 1), ev("shutT_done", 1), ev("out_done", 2))
        rstd_done, mem_one = ev("rstd_done", 1), ev("mem_one", 1)

        def ends(*events):
            for e in events:
                e.turn_ends()

        with nc.Block() as block:
            @block.sync
            def _(eng):
                for e in (load, store):
                    e.credit(eng)

                def get(b):
                    load.mark(eng.dma_start(xr[:, :, :], x1_d[b].rearrange("(n p) c -> p n c", p=P)))
                    for j in range(GRP):
                        load.mark(eng.dma_start(pick4[j * E:(j + 1) * E, :], pick_d[b]))
                        load.mark(eng.dma_start(eo[j * E:(j + 1) * E, :], eo_d[j, b]))
                    ends(load)

                def put(b):
                    out_done.wait(eng, b)
                    store.mark(eng.dma_start(out[b].rearrange("(n p) c -> p n c", p=P), xo[:, :, :]))
                    ends(store)

                def free(b):
                    pe_add.wait(eng, b)
                    x1_done.wait(eng, b)
                get(0)
                free(0)
                get(1)
                with eng.Fori(0, B - 2) as b:
                    free(b + 1)
                    get(b + 2)
                    put(b)
                put(B - 2)
                put(B - 1)
                store.wait(eng, B - 1)

            def turns(eng, front_of_first, turn, last):
                front_of_first()
                with eng.Fori(0, B - 1) as b:
                    turn(b)
                last(B - 1)

            @block.tensor
            def _(eng):
                for e in (pe_add, pe_xT, pe_r, pe_shut, pe_mem, pe_up, pe_down):
                    e.credit(eng)

                def add(b):
                    eo_biased.wait(eng, b)
                    lo_done.wait(eng, b - 1)
                    shutT_done.wait(eng, b - 1)
                    for n in range(NT):
                        m = eng.matmul(bF[n // 2][:, (n % 2) * C:(n % 2 + 1) * C], pick4[:, n * P:(n + 1) * P], eo[:, :],
                                       start=True, stop=True)
                        if n % 2:
                            pe_add.mark(m)
                    ends(pe_add)

                def turn_x(b):
                    xn_done.wait(eng, b)
                    x1_done.wait(eng, b)
                    for k in range(KC):
                        for n in range(NT):
                            m = eng.transpose(bF[k][:, n * P:(n + 1) * P], xn[:, n, k * P:(k + 1) * P], ident[:, :])
                        pe_xT.mark(m)
                    ends(pe_xT)

                def router(b):
                    xT_done.wait(eng, b)
                    logit_done.wait(eng, b - 1)
                    for n in range(NT):
                        for k in range(KC):
                            m = eng.matmul(bR[:, n * NB:(n + 1) * NB], xT[:, k, n * P:(n + 1) * P], rT[:, k, :],
                                           start=(k == 0), stop=(k == KC - 1))
                    pe_r.mark(m)
                    ends(pe_r)

                def turn_shut(b):
                    shut_done.wait(eng, b)
                    for n in range(NT):
                        m = eng.transpose(bF[0][0:NB, n * P:(n + 1) * P], shut[:, n, :], ident[:, :])
                    pe_shut.mark(m)
                    ends(pe_shut)

                def product(b, bank, hi, lo, first, done):
                    start = first
                    for k in range(KC):
                        for w, x in ((lo, xT_hi), (hi, xT_lo), (hi, xT_hi)):
                            m = eng.matmul(bank[:, :], w[:, k, :], x[:, b % 2, k, :], start=start,
                                           stop=(k == KC - 1 and w is hi and x is xT_hi))
                            start = False
                    done.mark(m)

                def memory(b):
                    lo_done.wait(eng, b)
                    shutT_done.wait(eng, b)
                    relu_done.wait(eng, b - 1, HC)
                    product(b, bU[1], readT_hi, readT_lo, True, pe_mem)
                    ends(pe_mem)

                def up(b, hs):
                    for h in hs:
                        if h == 0:
                            relu_done.wait(eng, b - 1, HC - 1, alone=True)
                        elif h == 1:
                            mem_done.wait(eng, b, alone=True)
                        else:
                            relu_done.wait(eng, b, h - 1, alone=True)
                        eng.matmul(bU[h % 2][:, :], spread[:, h, :], shutT[:, b % 2, :], start=True, stop=False)
                        product(b, bU[h % 2], up_hi[:, :, h, :], up_lo[:, :, h, :], False, pe_up)
                    if h == HC - 1:
                        ends(pe_up)

                def down(b, ns):
                    for n in ns:
                        if n == 0:
                            relu_done.wait(eng, b)
                            mem_one.wait(eng, 0)
                            mem_done.wait(eng, b)
                        if n % 2 == 0:
                            out_done.wait(eng, b - 1, n // 2 + 1)
                        o = bD[n // 2][:, (n % 2) * C:(n % 2 + 1) * C]
                        eng.matmul(o, mem[:, n * P:(n + 1) * P], backT[:, :], start=True, stop=False)
                        for h in range(HC):
                            m = eng.matmul(o, hT[:, h, n * P:(n + 1) * P], downT[:, h, :], start=False, stop=(h == HC - 1))
                        if n % 2:
                            pe_down.mark(m)
                    if n == NT - 1:
                        ends(pe_down)

                def first():
                    add(0)
                    turn_x(0)
                    router(0)
                    turn_shut(0)

                def turn(b):
                    add(b + 1)
                    memory(b)
                    up(b, range(0, 3))
                    turn_x(b + 1)
                    up(b, range(3, 6))
                    router(b + 1)
                    up(b, range(6, HC))
                    down(b, (0, 1))
                    turn_shut(b + 1)
                    down(b, (2, 3))

                def last(b):
                    memory(b)
                    up(b, range(HC))
                    down(b, range(NT))
                turns(eng, first, turn, last)

            @block.scalar
            def _(eng):
                for e in (xT_done, mem_done, relu_done):
                    e.credit(eng)

                def copy_x(b):
                    hi_done.wait(eng, b - 1)
                    lo_done.wait(eng, b - 1)
                    pe_r.wait(eng, b - 1)
                    for k in range(KC):
                        pe_xT.wait(eng, b, k + 1)
                        xT_done.mark(eng.activation(xT[:, k, :], bF[k][:, :], ACT.Copy))
                    ends(xT_done)

                def memory(b):
                    pe_mem.wait(eng, b)
                    pe_down.wait(eng, b - 1)
                    mem_done.mark(eng.activation(mem[0:M1, :], bU[1][0:M1, :], ACT.Gelu))
                    ends(mem_done)

                def relu(b, hs):
                    for h in hs:
                        pe_up.wait(eng, b, h + 1)
                        relu_done.mark(eng.activation(hT[:, h, :], bU[h % 2][:, :], ACT.Relu, bias=b1[:, h:h + 1]))
                    if h == HC - 1:
                        ends(relu_done)

                def turn(b):
                    memory(b)
                    relu(b, range(0, 3))
                    copy_x(b + 1)
                    relu(b, range(3, HC))

                def last(b):
                    memory(b)
                    relu(b, range(HC))
                turns(eng, lambda: copy_x(0), turn, last)

            @block.gpsimd
            def _(eng):
                rstd_done.credit(eng)
                mem_one.credit(eng)
                mem_one.mark(eng.memset(mem[M1:M1 + 1, :], 1.0))
                mem_one.wait(eng, 0)
                with eng.Fori(0, B) as b:
                    var_done.wait(eng, b)
                    xn_done.wait(eng, b - 1)
                    rstd_done.mark(eng.tensor_tensor(rstd[:, :], var[:, :], half[:, 0:NT], ALU.pow))
                    rstd_done.turn_ends()

            @block.vector
            def _(eng):
                for e in (eo_biased, x1_done, stat, agg, var_done, xn_done, hi_done, lo_done, logit_done, route,
                          shut_done, shutT_done, out_done):
                    e.credit(eng)

                def norm(b):
                    load.wait(eng, b)
                    eo_biased.mark(eng.tensor_tensor(eo[0:E, :], eo[0:E, :], b2e[:, :], ALU.add))
                    out_done.wait(eng, b - 2)
                    for i in range(2):
                        pe_add.wait(eng, b, i + 1)
                        x1_done.mark(eng.tensor_tensor(
                            x1[:, b % 2, 2 * i:2 * i + 2, :], bF[i][:, :].rearrange("p (n c) -> p n c", n=2),
                            xr[:, 2 * i:2 * i + 2, :], ALU.add))
                    x1_done.wait(eng, b, alone=True)
                    for n in range(NT):
                        stat.mark(eng.bn_stats(stats[:, n, :], x1[:, b % 2, n, :]))
                    stat.wait(eng, b, alone=True)
                    for n in range(NT):
                        agg.mark(eng.bn_aggr(mv[:, n, :], stats[:, n, :]))
                    agg.wait(eng, b)
                    var_done.mark(eng.tensor_scalar(var[:, :], mv[:, :, 1], EPS, None, ALU.add))
                    rstd_done.wait(eng, b)
                    pe_xT.wait(eng, b - 1)
                    for n in range(NT):
                        xn_done.mark(eng.tensor_scalar(xn[:, n, :], x1[:, b % 2, n, :], mv[:, n, 0:1],
                                                       rstd[:, n:n + 1], ALU.subtract, ALU.mult))
                    ends(eo_biased, x1_done, stat, agg, var_done, xn_done)

                def split(b):
                    xT_done.wait(eng, b)
                    pe_up.wait(eng, b - 2)
                    hi_done.mark(eng.tensor_copy(xT_hi[:, b % 2, :, :], xT[:, :, :]))
                    hi_done.wait(eng, b)
                    lo_done.mark(eng.tensor_tensor(xT_lo[:, b % 2, :, :], xT[:, :, :],
                                                   xT_hi[:, b % 2, :, :].bitcast(F32), ALU.subtract))
                    ends(hi_done, lo_done)

                def choose(b):
                    pe_r.wait(eng, b)
                    logit_done.mark(eng.tensor_tensor(
                        logit[:, :, :], bR[:, 0:NT * NB].rearrange("p (n i) -> p n i", n=NT),
                        rb[:, :].unsqueeze(1).to_broadcast([P, NT, NB]), ALU.add))
                    logit_done.wait(eng, b, alone=True)
                    for n in range(NT):
                        route.mark(eng.max(top[:, n, :], logit[:, n, :]))
                    route.wait(eng, b, NT, alone=True)
                    for n in range(NT):
                        route.mark(eng.max_index(idx[:, n, :], top[:, n, :], logit[:, n, :]))
                    route.wait(eng, b, 2 * NT)
                    route.mark(eng.tensor_copy(idxf[:, :, :], idx[:, :, :]))
                    route.wait(eng, b, 2 * NT + 1)
                    full = [P, NT, NB, TOPK]
                    route.mark(eng.tensor_tensor(
                        eq[:, :, :, :], idxf[:, :, 0:TOPK].unsqueeze(2).to_broadcast(full),
                        number[:, :].unsqueeze(1).unsqueeze(3).to_broadcast(full), ALU.is_equal))
                    route.wait(eng, b, 2 * NT + 2)
                    pe_shut.wait(eng, b - 1)
                    route.mark(eng.tensor_reduce(shut[:, :, :], eq[:, :, :, :], AX.X, ALU.add))
                    route.wait(eng, b)
                    shut_done.mark(eng.tensor_scalar(shut[:, :, :], shut[:, :, :], -1.0, -NEG, ALU.add, ALU.mult))
                    ends(logit_done, route, shut_done)

                def copy_shut(b):
                    pe_shut.wait(eng, b)
                    pe_up.wait(eng, b - 2)
                    shutT_done.mark(eng.tensor_copy(shutT[:, b % 2, :], bF[0][0:NB, :]))
                    ends(shutT_done)

                def finish(b):
                    store.wait(eng, b - 1)
                    for i in range(2):
                        pe_down.wait(eng, b, i + 1)
                        out_done.mark(eng.tensor_tensor(
                            xo[:, 2 * i:2 * i + 2, :], bD[i][:, :].rearrange("p (n c) -> p n c", n=2),
                            x1[:, b % 2, 2 * i:2 * i + 2, :], ALU.add))
                    ends(out_done)

                def front(b):
                    norm(b)
                    split(b)
                    choose(b)
                    copy_shut(b)

                def turn(b):
                    norm(b + 1)
                    split(b + 1)
                    choose(b + 1)
                    copy_shut(b + 1)
                    finish(b)
                turns(eng, lambda: front(0), turn, finish)


_INS = ["L0_attn_x", "L0_attn_Wq", "L0_attn_Wk", "L0_attn_Wv", "L0_attn_Wproj", "L0_attn_q_rms_w", "L0_attn_k_rms_w",
        "L0_attn_omega", "L0_attn_u", "L0_ffn_gate_w", "L0_ffn_gate_b", "L0_ffn_w1", "L0_ffn_w2", "L1_attn_W_K",
        "L1_attn_W1", "L1_attn_W2", "L1_ffn_router_w", "L1_ffn_router_b", "L1_ffn_w1", "L1_ffn_b1", "L1_ffn_w2",
        "L1_ffn_b2"]


def kernel(**inputs):
    import numpy as np
    import concourse.bacc as bacc
    from concourse.bass_utils import run_bass_kernel_spmd

    nc = bacc.Bacc("TRN2", target_bir_lowering=False, num_devices=1)
    arrays, t = {}, {}
    for name in _INS:
        arrays["in_" + name] = np.ascontiguousarray(inputs[name])
        t[name] = nc.dram_tensor("in_" + name, arrays["in_" + name].shape, F32, kind="ExternalInput").ap()
    out = nc.dram_tensor("out", arrays["in_L0_attn_x"].shape, F32, kind="ExternalOutput").ap()
    build(nc, t, out)
    return run_bass_kernel_spmd(nc, [arrays], core_ids=[0]).results[0]["out"]
```

```python
from contextlib import ExitStack

import concourse.bass as bass
import concourse.mybir as mybir

F32 = mybir.dt.float32
F32R = mybir.dt.float32r
U32 = mybir.dt.uint32
ALU = mybir.AluOpType
ACT = mybir.ActivationFunctionType
AX = mybir.AxisListType

P = 128
EPS = 1e-5
NEG = -1.0e30
LOWEST = -3.0e38


class Event:

    def __init__(self, ctx, nc, name, per, unit=1, carrier=None):
        self.name, self.per, self.unit, self.n = name, per, unit, 0
        self.carrier = carrier
        self.sem = ctx.enter_context(nc.semaphore(name))

    def credit(self, eng):
        eng.sem_inc(self.sem, self.per * self.unit)

    def mark(self, instruction):
        self.n += 1
        instruction.then_inc(self.sem, self.unit)
        return instruction

    def turn_ends(self):
        assert self.n == self.per, (self.name, self.n, self.per)
        self.n = 0

    def wait(self, eng, turn, n=None, alone=False):
        n = self.per if n is None else n
        value = (turn + 1) * (self.per * self.unit) + n * self.unit
        if isinstance(value, int) and value <= 0:
            return
        eng.wait_ge(self.sem, value)
        if alone:
            eng.sem_inc(self.carrier, 1)


class Chain(Event):

    def settle(self, eng, turn, alone=False):
        self.wait(eng, turn, self.n, alone)


def alibi_slopes(heads):
    start = 2.0 ** (-8.0 / heads)
    return [start * start ** i for i in range(heads)]


def build(nc, t, out):
    x_in = t["L0_attn_x"]
    B, T, C = x_in.shape
    NT = T // P
    KC = C // P
    H, D = t["L0_attn_u"].shape
    HP = H // 2
    E = t["L0_ffn_gate_w"].shape[0]
    F = t["L0_ffn_w1"].shape[2]
    NB = t["L1_ffn_router_w"].shape[0]
    HID = t["L1_ffn_w1"].shape[0]
    HC = HID // P
    M1 = t["L1_attn_W1"].shape[0]
    TOPK = NB // 4
    GRP = P // E
    assert (B, T, C, H, D, E, F) == (8, 512, 256, 16, 64, 32, 1024) and GRP == 4

    scratch = lambda name, shape, dt=F32: nc.dram_tensor(name, shape, dt, kind="Internal").ap()
    xnT_hi_d = scratch("xnT_hi_d", (B, P, KC, T))
    xnT_lo_d = scratch("xnT_lo_d", (B, P, KC, T))
    pick_d = scratch("pick_d", (B, E, T))
    x1_d = scratch("x1_d", (B, T, C))
    eo_d = scratch("eo_d", (E, P, C))

    with ExitStack() as whole:
        def sb_in(ctx):
            return lambda name, shape, dt=F32: ctx.enter_context(nc.sbuf_tensor(name, shape, dt))

        def banks(ctx, n, name):
            return [ctx.enter_context(nc.psum_tensor(f"{name}{i}", [P, 512], F32)) for i in range(n)]

        sb = sb_in(whole)
        ident = sb("ident", [P, P])
        merged = sb("merged", [P, KC, E, B])
        half = sb("half", [P, 16])
        carrier = whole.enter_context(nc.semaphore("carrier"))

        with ExitStack() as ctx, nc.Block() as block:
            s_zero = ctx.enter_context(nc.semaphore("s_zero"))

            @block.gpsimd
            def _(eng):
                eng.memset(ident[:, :], 0.0).then_inc(s_zero, 1)
                eng.memset(half[:, :], -0.5)
                eng.wait_ge(s_zero, 1)
                eng.affine_select(out=ident[:, :], in_=ident[:, :], compare_op=ALU.not_equal, fill=1.0,
                                  base=0, pattern=[[-1, P]], channel_multiplier=1)

        g = dict(B=B, T=T, C=C, NT=NT, KC=KC, H=H, D=D, HP=HP, E=E, F=F, NB=NB, HC=HC, M1=M1, TOPK=TOPK, GRP=GRP,
                 sb_in=sb_in, banks=banks, ident=ident, merged=merged, half=half, carrier=carrier,
                 xnT_hi_d=xnT_hi_d, xnT_lo_d=xnT_lo_d, pick_d=pick_d, x1_d=x1_d, eo_d=eo_d)
        g.update(second_layer_inputs(nc, g, whole))
        with ExitStack() as ctx:
            with_attention = {**g, **attention_constants(g, ctx)}
            route_tokens(nc, t, with_attention)
            attend(nc, t, with_attention)
        second_layer(nc, t, out, g)


def attention_constants(g, ctx):
    KC, HP, NT, T, C, H, D = (g[k] for k in ("KC", "HP", "NT", "T", "C", "H", "D"))
    sb = g["sb_in"](ctx)
    W = 3 * P + 2
    return dict(
        W=W, DA=D + 2,
        w_hi=sb("w_hi", [P, KC, HP, W], F32R),
        w_lo=sb("w_lo", [P, KC, HP, W], F32R),
        w_proj=sb("w_proj", [P, HP, C]),
        mask=sb("mask", [P, T]),
        pos=sb("pos", [P, NT]),
        omega=sb("omega", [P, H]),
        q_scale=sb("q_scale", [D + 2, 1]))


def second_layer_inputs(nc, g, ctx):
    KC, C, HC, M1, NB = (g[k] for k in ("KC", "C", "HC", "M1", "NB"))
    sb = g["sb_in"](ctx)
    return dict(
        w1n=sb("w1n", [P, HC, C]),
        w2n=sb("w2n", [P, KC, HC * P]),
        wk=sb("wk", [P, KC, C]),
        m1n=sb("m1n", [M1, C]),
        m2n=sb("m2n", [P, KC, M1]),
        rn=sb("rn", [NB, C]),
        rb=sb("rb", [P, NB]),
        backT=sb("backT", [M1 + 1, C]),
        b1=sb("b1", [P, HC]),
        l1_load=ctx.enter_context(nc.semaphore("l1_load")))


def route_tokens(nc, t, g):
    B, T, C, NT, KC, E, H, D = (g[k] for k in ("B", "T", "C", "NT", "KC", "E", "H", "D"))
    ident, merged, half = g["ident"], g["merged"], g["half"]
    xnT_hi_d, xnT_lo_d, pick_d = g["xnT_hi_d"], g["xnT_lo_d"], g["pick_d"]
    w_hi, w_lo, w_proj, mask, pos, omega, q_scale, DA = (g[k] for k in (
        "w_hi", "w_lo", "w_proj", "mask", "pos", "omega", "q_scale", "DA"))
    slopes = alibi_slopes(H)
    with ExitStack() as ctx:
        sb = g["sb_in"](ctx)
        gate_in = sb("gate_in", [E, C])
        gateT = sb("gateT", [P, KC, E])
        gate_b = sb("gate_b", [E, 1])
        x = [sb(f"x_in{u}", [P, NT, C]) for u in range(2)]
        xn = [sb(f"xn_{u}", [P, NT, C]) for u in range(2)]
        stats = sb("stats", [P, NT, 6])
        mv = sb("mv", [P, NT, 2])
        var = sb("var", [P, NT])
        rstd = sb("rstd", [P, NT])
        xT = sb("xT", [P, KC, T])
        xT_hi = sb("xT_hi", [P, KC, T], F32R)
        xT_lo = sb("xT_lo", [P, KC, T], F32R)
        logits = sb("logits", [E, T])
        top8 = sb("top8", [E, 8])
        left = sb("left", [E, T])
        nmax = sb("nmax", [E, 1])
        expd = sb("expd", [E, T])
        den = sb("den", [E, 1])
        rden = sb("rden", [E, 1])
        pick = sb("pick", [E, T])
        pickT = sb("pickT", [P, NT, E])
        raw_w = sb("raw_w", [P, KC, 3, H * D])
        u_in = sb("u_in", [P, H, D])
        kw = sb("kw", [P, D])
        tmp = sb("tmp", [P, H, D])
        ss = sb("ss", [P, H])
        slope = sb("slope", [P, H])
        om = sb("om", [P, H])
        e0 = sb("e0", [P, H])
        l0 = sb("l0", [P, H])
        gk = sb("gk", [P, KC, H])
        qk_w = sb("qk_w", [DA, 2])
        bT0, bT1, bL, bG, bP, bM = g["banks"](ctx, 6, "rt")
        bT = [bT0, bT1]

        ev = lambda name, per, unit=1: Event(ctx, nc, name, per, unit, g["carrier"])
        gate_load, gate_t, gate_copied = ev("gate_load", 2, 16), ev("gate_t", 1), ev("gate_copied", 1)
        load = [ev(f"load{u}", 1, 16) for u in range(2)]
        store, store_p = ev("store", 2, 16), ev("store_p", 1, 16)
        stat, agg, var_done, rstd_done = ev("stat", NT), ev("agg", NT), ev("var_done", 1), ev("rstd_done", 1)
        xn_done, hi_done, split_done = ev("xn_done", NT), ev("hi_done", 1), ev("split_done", 1)
        topped, nmax_done, left_done, rden_done = ev("topped", 1), ev("nmax_done", 1), ev("left_done", 1), ev("rden_done", 1)
        kept_done, pick_done, merged_done, pickT_done = (
            ev("kept_done", 1), ev("pick_done", 1), ev("merged_done", 1), ev("pickT_done", 1))
        pe_xT, pe_gate, pe_pickT, pe_merged = ev("pe_xT", 2), ev("pe_gate", 1), ev("pe_pickT", 1), ev("pe_merged", 1)
        xT_done, logits_done, exp_done = ev("xT_done", 2), ev("logits_done", 1), ev("exp_done", 1)
        w_hi_done = ev("w_hi_done", 1)
        w_load = ctx.enter_context(nc.semaphore("w_load"))
        dv, po, ac = (Chain(ctx, nc, n, 0) for n in ("dv_s", "po_s", "ac_s"))

        def ends(*events):
            for e in events:
                e.turn_ends()

        def steps(eng, begin, step, last):
            begin(0, 0, 0)
            with eng.Fori(0, B // 2 - 1) as i:
                step(2 * i, i, 0)
                step(2 * i + 1, i, 1)
            step(B - 2, B // 2 - 1, 0)
            last(B - 1, B // 2 - 1, 1)

        def following(b, i, u):
            return b + 1, i + u, 1 - u

        with nc.Block() as block:
            @block.sync
            def _(eng):
                for e in (gate_load, *load, store, store_p):
                    e.credit(eng)

                def get(b, u):
                    load[u].mark(eng.dma_start(x[u][:, :, :], t["L0_attn_x"][b].rearrange("(n p) c -> p n c", p=P)))
                    ends(load[u])
                get(0, 0)
                gate_load.mark(eng.dma_start(gate_in[:, :], t["L0_ffn_gate_w"]))
                gate_load.mark(eng.dma_start(gate_b[:, :], t["L0_ffn_gate_b"].unsqueeze(1)))
                get(1, 1)
                for dst, src in (
                    (u_in[:, :, :], t["L0_attn_u"].partition_broadcast(P)),
                    (kw[:, :], t["L0_attn_k_rms_w"].partition_broadcast(P)),
                    (om[:, :], t["L0_attn_omega"].partition_broadcast(P)),
                    (qk_w[0:D, 0:1], t["L0_attn_q_rms_w"].unsqueeze(1)),
                    (qk_w[0:D, 1:2], t["L0_attn_k_rms_w"].unsqueeze(1)),
                    (raw_w[:, :, 0, :], t["L0_attn_Wq"].rearrange("(k p) n -> p k n", p=P)),
                    (raw_w[:, :, 1, :], t["L0_attn_Wk"].rearrange("(k p) n -> p k n", p=P)),
                    (raw_w[:, :, 2, :], t["L0_attn_Wv"].rearrange("(k p) n -> p k n", p=P)),
                    (w_proj[:, :, :], t["L0_attn_Wproj"].rearrange("(h p) c -> p h c", p=P)),
                ):
                    eng.dma_start(dst, src).then_inc(w_load, 16)

                def put(b):
                    split_done.wait(eng, b)
                    store.mark(eng.dma_start(xnT_hi_d[b], xT_hi[:, :, :].bitcast(F32)))
                    store.mark(eng.dma_start(xnT_lo_d[b], xT_lo[:, :, :].bitcast(F32)))
                    pick_done.wait(eng, b)
                    store_p.mark(eng.dma_start(pick_d[b], pick[:, :]))
                    ends(store, store_p)

                def step(b, u):
                    xn_done.wait(eng, b)
                    get(b + 2, u)
                    put(b)
                with eng.Fori(0, B // 2 - 1) as i:
                    step(2 * i, 0)
                    step(2 * i + 1, 1)
                put(B - 2)
                put(B - 1)
                store.wait(eng, B - 1)
                store_p.wait(eng, B - 1)

            @block.tensor
            def _(eng):
                for e in (gate_t, pe_xT, pe_gate, pe_pickT, pe_merged):
                    e.credit(eng)
                gate_load.wait(eng, 0)
                for k in range(KC):
                    m = eng.transpose(bG[:, k * E:(k + 1) * E], gate_in[:, k * P:(k + 1) * P], ident[0:E, 0:E])
                gate_t.mark(m)

                def turn_x(b, i, u):
                    xn_done.wait(eng, b)
                    for k in range(KC):
                        xT_done.wait(eng, b - 1, k + 1)
                        for n in range(NT):
                            m = eng.transpose(bT[k][:, n * P:(n + 1) * P], xn[u][:, n, k * P:(k + 1) * P], ident[:, :])
                        pe_xT.mark(m)
                    ends(pe_xT)

                def gate(b):
                    logits_done.wait(eng, b - 1)
                    for k in range(KC):
                        xT_done.wait(eng, b, k + 1)
                        m = eng.matmul(bL[0:E, :], gateT[:, k, :], xT[:, k, :], start=(k == 0), stop=(k == KC - 1))
                    pe_gate.mark(m)
                    ends(pe_gate)

                def turn_pick(b):
                    pick_done.wait(eng, b)
                    pickT_done.wait(eng, b - 1, alone=True)
                    for n in range(NT):
                        m = eng.transpose(bP[:, n * E:(n + 1) * E], pick[:, n * P:(n + 1) * P], ident[0:E, 0:E])
                    pe_pickT.mark(m)
                    ends(pe_pickT)

                def merge(b, u):
                    pickT_done.wait(eng, b)
                    merged_done.wait(eng, b - 1)
                    for k in range(KC):
                        for n in range(NT):
                            m = eng.matmul(bM[:, k * E:(k + 1) * E], xn[u][:, n, k * P:(k + 1) * P], pickT[:, n, :],
                                           start=(n == 0), stop=(n == NT - 1))
                    pe_merged.mark(m)
                    ends(pe_merged)

                def begin(b, i, u):
                    turn_x(b, i, u)
                    gate_copied.wait(eng, 0)
                    gate(b)

                def step(b, i, u):
                    turn_x(*following(b, i, u))
                    turn_pick(b)
                    gate(b + 1)
                    merge(b, u)

                def last(b, i, u):
                    turn_pick(b)
                    merge(b, u)
                steps(eng, begin, step, last)

            @block.scalar
            def _(eng):
                for e in (xT_done, logits_done, exp_done, w_hi_done, merged_done):
                    e.credit(eng)
                eng.preload_act_table_set("natural_log_exp_and_others")

                def copy_x(b):
                    split_done.wait(eng, b - 1)
                    pe_gate.wait(eng, b - 1)
                    for k in range(KC):
                        pe_xT.wait(eng, b, k + 1)
                        xT_done.mark(eng.activation(xT[:, k, :], bT[k][:, :], ACT.Copy))
                    ends(xT_done)

                def copy_logits(b):
                    pe_gate.wait(eng, b)
                    left_done.wait(eng, b - 1)
                    exp_done.wait(eng, b - 1)
                    logits_done.mark(eng.activation(logits[:, :], bL[0:E, :], ACT.Identity, bias=gate_b[:, 0:1]))
                    ends(logits_done)

                def exp(b):
                    nmax_done.wait(eng, b)
                    pick_done.wait(eng, b - 1)
                    exp_done.mark(eng.activation(expd[:, :], logits[:, :], ACT.Exp, bias=nmax[:, 0:1],
                                                 accum_out=den[:, 0:1]))
                    ends(exp_done)

                def begin(b, i, u):
                    copy_x(b)
                    gate_load.wait(eng, 0)
                    copy_logits(b)

                def copy_merged(b):
                    pe_merged.wait(eng, b)
                    merged_done.mark(eng.activation(merged[:, :, :, b],
                                                    bM[:, 0:KC * E].rearrange("p (k e) -> p k e", k=KC), ACT.Copy))
                    ends(merged_done)

                def split_weights(b, i, k):
                    eng.wait_ge(w_load, 9 * 16)
                    w_hi_done.mark(eng.activation(w_hi[:, k, :, bass.ds(i * P, P)],
                                                  raw_w[:, k, i, :].rearrange("p (h n) -> p h n", n=P), ACT.Copy))
                    ends(w_hi_done)

                def step(b, i, u):
                    exp(b)
                    if not isinstance(b, int):
                        split_weights(b, i, u)
                    copy_x(b + 1)
                    copy_logits(b + 1)
                    copy_merged(b)

                def last(b, i, u):
                    dv.wait(eng, -1, 5)
                    ac.mark(eng.activation(e0[:, :], e0[:, :], ACT.Exp))
                    ac.settle(eng, -1)
                    ac.mark(eng.activation(l0[:, :], e0[:, :], ACT.Ln, bias=1.0))
                    exp(b)
                    copy_merged(b)
                steps(eng, begin, step, last)

            @block.gpsimd
            def _(eng):
                rstd_done.credit(eng)
                po.mark(eng.memset(mask[:, :], 0.0))
                po.mark(eng.iota(pos[:, :], pattern=[[P, NT]], base=-(T // 2), channel_multiplier=1,
                                 allow_small_or_imprecise_dtypes=True))
                po.mark(eng.memset(q_scale[:, :], 1.0))
                for h in range(H):
                    po.mark(eng.memset(slope[:, h:h + 1], slopes[h]))
                po.wait(eng, -1, 1)
                po.mark(eng.affine_select(out=mask[:, T - P:T], in_=mask[:, T - P:T], compare_op=ALU.is_ge,
                                          fill=NEG, base=0, pattern=[[-1, P]], channel_multiplier=1))

                def power(b):
                    var_done.wait(eng, b)
                    xn_done.wait(eng, b - 1)
                    rstd_done.mark(eng.tensor_tensor(rstd[:, :], var[:, :], half[:, 0:NT], ALU.pow))
                    ends(rstd_done)

                def split_weights(b, i, k):
                    w_hi_done.wait(eng, b)
                    eng.tensor_tensor(w_lo[:, k, :, bass.ds(i * P, P)],
                                      raw_w[:, k, i, :].rearrange("p (h n) -> p h n", n=P),
                                      w_hi[:, k, :, bass.ds(i * P, P)].bitcast(F32), ALU.subtract)

                def step(b, i, u):
                    power(b + 1)
                    if not isinstance(b, int):
                        split_weights(b, i, u)
                assert (B // 2 - 1) * 2 == 3 * KC
                steps(eng, lambda b, i, u: power(b), step, lambda b, i, u: None)
                dv.wait(eng, -1, 4)
                po.mark(eng.tensor_tensor(ss[:, :], ss[:, :], half[:, 0:H], ALU.pow))

            @block.vector
            def _(eng):
                for e in (stat, agg, var_done, xn_done, hi_done, split_done, topped, nmax_done, left_done, rden_done,
                          kept_done, pick_done, pickT_done, gate_copied):
                    e.credit(eng)

                def moments(b, i, u):
                    load[u].wait(eng, i)
                    for n in range(NT):
                        stat.mark(eng.bn_stats(stats[:, n, :], x[u][:, n, :]))
                    stat.wait(eng, b, alone=True)
                    for n in range(NT):
                        agg.mark(eng.bn_aggr(mv[:, n, :], stats[:, n, :]))
                    agg.wait(eng, b)
                    var_done.mark(eng.tensor_scalar(var[:, :], mv[:, :, 1], EPS, None, ALU.add))
                    ends(stat, agg, var_done)

                def norm(b, i, u):
                    rstd_done.wait(eng, b)
                    pe_merged.wait(eng, b - 2)
                    for n in range(NT):
                        xn_done.mark(eng.tensor_scalar(xn[u][:, n, :], x[u][:, n, :], mv[:, n, 0:1], rstd[:, n:n + 1],
                                                       ALU.subtract, ALU.mult))
                    ends(xn_done)

                def split(b):
                    store.wait(eng, b - 1)
                    xT_done.wait(eng, b)
                    hi_done.mark(eng.tensor_copy(xT_hi[:, :, :], xT[:, :, :]))
                    hi_done.wait(eng, b)
                    split_done.mark(eng.tensor_tensor(xT_lo[:, :, :], xT[:, :, :], xT_hi[:, :, :].bitcast(F32),
                                                      ALU.subtract))
                    ends(hi_done, split_done)

                def choose(b):
                    logits_done.wait(eng, b, alone=True)
                    topped.mark(eng.max(top8[:, :], logits[:, :]))
                    topped.wait(eng, b)
                    nmax_done.mark(eng.tensor_scalar(nmax[:, :], top8[:, 0:1], -1.0, None, ALU.mult))
                    left_done.mark(eng.match_replace(left[:, :], top8[:, :], logits[:, :], LOWEST))
                    ends(topped, nmax_done, left_done)

                def weigh(b):
                    exp_done.wait(eng, b)
                    rden_done.mark(eng.reciprocal(rden[:, :], den[:, :]))
                    left_done.wait(eng, b)
                    kept_done.mark(eng.scalar_tensor_tensor(left[:, :], left[:, :], LOWEST / 2, expd[:, :],
                                                            ALU.is_le, ALU.mult))
                    rden_done.wait(eng, b)
                    kept_done.wait(eng, b)
                    store_p.wait(eng, b - 1)
                    pick_done.mark(eng.tensor_scalar(pick[:, :], left[:, :], rden[:, 0:1], None, ALU.mult))
                    ends(rden_done, kept_done, pick_done)

                def copy_pick(b):
                    pe_merged.wait(eng, b - 1)
                    pe_pickT.wait(eng, b)
                    pickT_done.mark(eng.tensor_copy(pickT[:, :, :],
                                                    bP[:, 0:NT * E].rearrange("p (n e) -> p n e", n=NT)))
                    ends(pickT_done)

                def prepare_u():
                    eng.wait_ge(w_load, 9 * 16)
                    dv.mark(eng.tensor_tensor(tmp[:, :, :], u_in[:, :, :], u_in[:, :, :], ALU.mult))
                    dv.settle(eng, -1)
                    dv.mark(eng.tensor_reduce(ss[:, :], tmp[:, :, :], AX.X, ALU.add))
                    dv.mark(eng.tensor_tensor(u_in[:, :, :], u_in[:, :, :],
                                              kw[:, :].unsqueeze(1).to_broadcast([P, H, D]), ALU.mult))
                    dv.settle(eng, -1)
                    dv.mark(eng.tensor_scalar(ss[:, :], ss[:, :], 1e-12, None, ALU.max))
                    dv.mark(eng.scalar_tensor_tensor(e0[:, :], om[:, :], -1.0, om[:, :], ALU.mult, ALU.min))

                def begin(b, i, u):
                    moments(b, i, u)
                    norm(b, i, u)
                    gate_t.wait(eng, 0)
                    gate_copied.mark(eng.tensor_copy(gateT[:, :, :], bG[:, 0:KC * E].rearrange("p (k e) -> p k e", k=KC)))
                    split(b)

                def step(b, i, u):
                    moments(*following(b, i, u))
                    choose(b)
                    norm(*following(b, i, u))
                    weigh(b)
                    copy_pick(b)
                    split(b + 1)

                def last(b, i, u):
                    prepare_u()
                    choose(b)
                    weigh(b)
                    copy_pick(b)
                steps(eng, begin, step, last)

                ac.wait(eng, -1, 2)
                dv.mark(eng.scalar_tensor_tensor(om[:, :], om[:, :], 0.0, l0[:, :], ALU.max, ALU.add))
                po.wait(eng, -1, 3 + H)
                dv.settle(eng, -1)
                dv.mark(eng.tensor_tensor(omega[:, :], om[:, :], slope[:, :], ALU.mult))
                dv.mark(eng.scalar_tensor_tensor(q_scale[0:D, :], qk_w[0:D, 0:1], float(D) ** -0.5, qk_w[0:D, 1:2],
                                                 ALU.mult, ALU.mult))
                po.wait(eng, -1, 5 + H)
                dv.mark(eng.tensor_scalar(ss[:, :], ss[:, :], float(D) ** -0.5, None, ALU.mult))
                dv.settle(eng, -1)
                dv.mark(eng.tensor_tensor(u_in[:, :, :], u_in[:, :, :],
                                          ss[:, :].unsqueeze(2).to_broadcast([P, H, D]), ALU.mult))
                for k in range(KC):
                    dv.settle(eng, -1)
                    dv.mark(eng.tensor_tensor(tmp[:, :, :], raw_w[:, k, 1, :].rearrange("p (h d) -> p h d", h=H),
                                              u_in[:, :, :], ALU.mult))
                    dv.settle(eng, -1)
                    dv.mark(eng.tensor_reduce(gk[:, k, :], tmp[:, :, :], AX.X, ALU.add))
                for k in range(KC):
                    src = gk[:, k, :].rearrange("p (h n) -> p h n", n=2)
                    dv.settle(eng, -1)
                    dv.mark(eng.tensor_copy(w_hi[:, k, :, 3 * P:], src))
                    dv.settle(eng, -1)
                    dv.mark(eng.tensor_tensor(w_lo[:, k, :, 3 * P:], src, w_hi[:, k, :, 3 * P:].bitcast(F32),
                                              ALU.subtract))


def attend(nc, t, g):
    B, T, C, NT, KC, H, D, HP, E, F, GRP = (g[k] for k in (
        "B", "T", "C", "NT", "KC", "H", "D", "HP", "E", "F", "GRP"))
    merged, eo_d = g["merged"], g["eo_d"]
    FW = F // GRP
    NF = FW // P
    assert E * 2 == B * HP
    ident, half = g["ident"], g["half"]
    xnT_hi_d, xnT_lo_d, x1_d = g["xnT_hi_d"], g["xnT_lo_d"], g["x1_d"]
    w_hi, w_lo, w_proj, mask, pos, omega, q_scale, W, DA = (g[k] for k in (
        "w_hi", "w_lo", "w_proj", "mask", "pos", "omega", "q_scale", "W", "DA"))
    off = [P * c * (c + 1) // 2 for c in range(NT + 1)]
    offT = [0, 512, 896, 1152, 1280]
    with ExitStack() as ctx:
        sb = g["sb_in"](ctx)
        xT_hi = sb("cT_hi", [P, KC, T], F32R)
        xT_lo = sb("cT_lo", [P, KC, T], F32R)
        raw = sb("raw", [P, 2, NT, W])
        sq = sb("sq", [P, NT, 2 * P])
        ss = sb("ssq", [P, NT * 4])
        rs = sb("rs", [P, NT, 4])
        gl = sb("gl", [P, NT, 2])
        ge = sb("ge", [P, NT, 2])
        gp = sb("gp", [P, NT, 2])
        qk = sb("qk", [P, NT, 4, DA])
        qkT = sb("qkT", [DA, 4, T])
        v = sb("v", [P, NT, P])
        prob = [sb(f"prob{h}", [P, off[NT]]) for h in range(2)]
        probT = [sb(f"probT{h}", [P, off[NT]]) for h in range(2)]
        mx = sb("mx", [P, 2 * NT])
        nm = sb("nm", [P, 2 * NT])
        den = sb("dens", [P, 2 * NT])
        rec = sb("rec", [P, 2 * NT])
        yT = sb("yT", [P, HP, T])
        xr = sb("xr", [P, NT, C])
        v_ring = sb("v_ring", [P, 2, NT, P])
        lnv = sb("lnv", [P, NT * 4])
        r0 = sb("r0", [P, NT * 4])
        nw = sb("nw", [P, NT * 4])
        w1 = sb("w1", [P, KC, F])
        w1b = sb("w1b", [1, F])
        w2 = sb("w2", [P, GRP * NF, C])
        w2b = sb("w2b", [1, C])
        tok = sb("tok", [P, KC, E])
        one = sb("one", [1, E])
        hid = sb("hid", [P, FW])
        hidT = sb("hidT", [P, NF, P])
        eo = sb("eo", [P, C])
        bank = g["banks"](ctx, 8, "at")
        bQ, bR, bS, bY = bank[0:2], bank[2:5], bank[5:7], bank[7]

        ev = lambda name, per, unit=1: Event(ctx, nc, name, per, unit, g["carrier"])
        xT_load, xr_load, xr_store = ev("xT_load", 2, 16), ev("xr_load", 1, 16), ev("xr_store", 1, 16)
        pe_q, pe_t, pe_s, pe_y = ev("pe_q", 4), ev("pe_t", 4), ev("pe_s", 8), ev("pe_y", 1)
        pe_pt = ev("pe_pt0", 3), ev("pe_pt1", 3)
        pe_o = ev("pe_o", 4)
        raw_A, squared, r0_done, gate_exp, qkT_A = (
            ev("raw_A", NT - 1), ev("squared", 1), ev("r0_done", 2), ev("gate_exp", 2), ev("qkT_A", 2))
        exp_done, pt0_A, pt1_A, y_done = ev("p_exp", 8), ev("pt0_A", 2), ev("pt1_A", 2), ev("y_done", 1)
        raw_D, ssd, newton, norm_done, gate_in, gate_g, qkT_D = (
            ev("raw_D", 1), ev("ssd", 2), ev("newton", 3), ev("norm_done", 1), ev("gate_in", 2), ev("gate_g", 1),
            ev("qkT_D", 2))
        maxed, negated, rec_done, p_done, pt0_D, pt1_D = (
            ev("maxed", 8), ev("negated", 4), ev("rec_done", 2), ev("p_done", 2), ev("pt0_D", 1), ev("pt1_D", 1))
        o_done = ev("o_done", 4)
        aug_done, v_taken, v_done, consts = ev("aug_done", 2), ev("v_taken", 1), ev("v_done", 1), ev("consts", 5)

        w1_load, w2_load, eo_store = ev("w1_load", 2, 16), ev("w2_load", 2, 16), ev("eo_store", 1, 16)
        tok_done, pe_h, pe_hT, pe_eo = ev("tok_done", 1), ev("pe_h", 1), ev("pe_hT", 1), ev("pe_eo", 1)
        hid_done, hidT_done, eo_done = ev("hid_done", 1), ev("hidT_done", 1), ev("eo_done", 1)

        def ends(*events):
            for e in events:
                e.turn_ends()

        def copied(u, s):
            return ((pt0_A, s, 1), (pt0_A, s, 2), (pt0_D, s, 1),
                    (qkT_D, s + 1, 1), (qkT_A, s + 1, 1), (qkT_D, s + 1, 2), (qkT_A, s + 1, 2),
                    (pt1_A, s, 1), (pt1_A, s, 2), (pt1_D, s, 1))[u]

        def free_R(eng, u, s):
            event, turn, n = copied((9, 7, 8)[u], s - 1) if u < 3 else copied(u - 3, s)
            event.wait(eng, turn, n)

        def copy_P(eng, copy, u, s):
            h, i = (0, u) if u < 3 else (1, u - 7)
            (x, y), (event, _, _) = segT[i], copied(u, s)
            pe_pt[h].wait(eng, s, i + 1)
            event.mark(copy(probT[h][:, x:y], bR[u % 3][:, 0:y - x]))
        qk_of_unit = (0, 2, 1, 3)
        segT = ((0, 512), (512, 896), (896, 1280))

        def at_start(s):
            return isinstance(s, int) and s == 0

        with nc.Block() as block:
            def turns(eng, first, turn, finish):
                first()
                turn(0, 0, None, False, None)

                def six(b):
                    with eng.Fori(0, HP // 2 - 1) as i:
                        turn(b * HP + 1 + 2 * i, 1 + 2 * i, b * (HP // 2) + i, True, None)
                        turn(b * HP + 2 + 2 * i, 2 + 2 * i, b * (HP // 2) + i, False, None)
                with eng.Fori(0, B - 1) as b:
                    six(b)
                    turn(b * HP + HP - 1, HP - 1, b * (HP // 2) + HP // 2 - 1, True, None)
                    turn(b * HP + HP, 0, b * (HP // 2) + HP // 2 - 1, False, b)
                six(B - 1)
                turn(B * HP - 1, HP - 1, E - 1, True, None)
                finish(B * HP, B - 1, E - 1)

            @block.sync
            def _(eng):
                for e in (xT_load, xr_load, xr_store, w1_load, w2_load, eo_store):
                    e.credit(eng)

                def load_xT(b):
                    xT_load.mark(eng.dma_start(xT_hi[:, :, :].bitcast(F32), xnT_hi_d[b]))
                    xT_load.mark(eng.dma_start(xT_lo[:, :, :].bitcast(F32), xnT_lo_d[b]))
                    ends(xT_load)

                def load_w1(m):
                    pe_h.wait(eng, m - 1)
                    w1_load.mark(eng.dma_start(w1[:, :, :], t["L0_ffn_w1"][m, 0:C, :].rearrange("(k p) f -> p k f", p=P)))
                    w1_load.mark(eng.dma_start(w1b[:, :], t["L0_ffn_w1"][m, C:C + 1, :]))
                    ends(w1_load)

                def load_w2(m):
                    pe_eo.wait(eng, m - 1)
                    w2_load.mark(eng.dma_start(w2[:, :, :], t["L0_ffn_w2"][m, 0:F, :].rearrange("(j p) c -> p j c", p=P)))
                    w2_load.mark(eng.dma_start(w2b[:, :], t["L0_ffn_w2"][m, F:F + 1, :]))
                    ends(w2_load)

                def store_eo(m):
                    eo_done.wait(eng, m)
                    eo_store.mark(eng.dma_start(eo_d[m], eo[:, :]))
                    ends(eo_store)
                load_xT(0)
                load_w1(0)
                for name, src in (
                    ("w1n", t["L1_ffn_w1"].rearrange("(h p) c -> p h c", p=P)),
                    ("w2n", t["L1_ffn_w2"].rearrange("(k p) f -> p k f", p=P)),
                    ("wk", t["L1_attn_W_K"].rearrange("(k p) c -> p k c", p=P)),
                    ("m1n", t["L1_attn_W1"]),
                    ("m2n", t["L1_attn_W2"].rearrange("(k p) m -> p k m", p=P)),
                    ("rn", t["L1_ffn_router_w"]),
                    ("rb", t["L1_ffn_router_b"].partition_broadcast(P)),
                ):
                    eng.dma_start(g[name][:], src).then_inc(g["l1_load"], 16)
                eng.dma_start(g["backT"][g["M1"]:g["M1"] + 1, :], t["L1_ffn_b2"].unsqueeze(0)).then_inc(g["l1_load"], 16)
                with nc.allow_non_contiguous_dma(reason="1024 biases, once"):
                    eng.dma_start(g["b1"][:, :], t["L1_ffn_b1"].rearrange("(h p) -> p h", p=P)).then_inc(g["l1_load"], 16)

                def batch(b, nxt):
                    xr_store.wait(eng, b - 1)
                    xr_load.mark(eng.dma_start(xr[:, :, :], t["L0_attn_x"][b].rearrange("(n p) c -> p n c", p=P)))
                    with eng.Fori(0, HP // 2 - 2) as i:
                        m = b * (HP // 2) + i
                        load_w2(m)
                        load_w1(m + 1)
                        store_eo(m)
                    m = b * (HP // 2) + HP // 2 - 2
                    load_w2(m)
                    pe_q.wait(eng, b * HP + (HP - 1))
                    load_xT(nxt)
                    load_w1(m + 1)
                    store_eo(m)
                    load_w2(m + 1)
                    if not isinstance(b, int):
                        load_w1(m + 2)
                    store_eo(m + 1)
                    o_done.wait(eng, b)
                    xr_store.mark(eng.dma_start(x1_d[b].rearrange("(n p) c -> p n c", p=P), xr[:, :, :]))
                    ends(xr_load, xr_store)
                with eng.Fori(0, B - 1) as b:
                    batch(b, b + 1)
                batch(B - 1, B - 1)
                xr_store.wait(eng, B - 1)
                eo_store.wait(eng, E - 1)
                xT_load.wait(eng, B)
                eng.wait_ge(g["l1_load"], 9 * 16)

            @block.tensor
            def _(eng):
                for e in (pe_q, pe_t, pe_s, *pe_pt, pe_y, pe_o, pe_h, pe_hT, pe_eo):
                    e.credit(eng)

                def project(j, hp):
                    for n in range(NT):
                        if n < 2:
                            raw_A.wait(eng, j - 1, n + 2)
                        elif n == 2:
                            raw_D.wait(eng, j)
                        else:
                            raw_A.wait(eng, j, 1)
                        first = True
                        for k in range(KC):
                            for a, w in ((xT_lo, w_hi), (xT_hi, w_lo), (xT_hi, w_hi)):
                                m = eng.matmul(bQ[n % 2][:, 0:W], a[:, k, n * P:(n + 1) * P], w[:, k, hp, :],
                                               start=first, stop=(k == KC - 1 and a is xT_hi and w is w_hi))
                                first = False
                        pe_q.mark(m)
                    ends(pe_q)

                def turn_qk(j, fresh=False):
                    norm_done.wait(eng, j)
                    aug_done.wait(eng, j)
                    for u, i in enumerate(qk_of_unit, 3):
                        if u == 6 or not fresh:
                            free_R(eng, u, j - 1)
                        for n in range(NT):
                            m = eng.transpose(bR[u % 3][0:DA, n * P:(n + 1) * P], qk[:, n, i, :], ident[:, :])
                        pe_t.mark(m)
                    ends(pe_t)

                def scores(s, h):
                    for c in range(NT):
                        i = NT * h + c
                        if i < 2:
                            maxed.wait(eng, s - 1, i + 7)
                        else:
                            maxed.wait(eng, s, i - 1)
                        m = eng.matmul(bS[i % 2][:, 0:(c + 1) * P], qkT[:, h, c * P:(c + 1) * P],
                                       qkT[:, 2 + h, 0:(c + 1) * P], start=True, stop=True)
                        pe_s.mark(m)

                def turn_p(s, h):
                    p_done.wait(eng, s, h + 1)
                    for i, chunks in enumerate(((0,), (1,), (2, 3))):
                        u = 7 * h + i
                        free_R(eng, u, s)
                        at = 0
                        for kc in chunks:
                            for c in range(kc, NT):
                                m = eng.transpose(bR[u % 3][:, at:at + P],
                                                  prob[h][:, off[c] + kc * P:off[c] + (kc + 1) * P], ident[:, :])
                                at += P
                        pe_pt[h].mark(m)
                    ends(pe_pt[h])

                def values(s):
                    for e in (pt0_A, pt0_D, pt1_A, pt1_D):
                        e.wait(eng, s)
                    v_done.wait(eng, s)
                    y_done.wait(eng, s - 1)
                    for kc in range(NT):
                        for h in range(2):
                            m = eng.matmul(bY[h * D:(h + 1) * D, kc * P:T], v[:, kc, h * D:(h + 1) * D],
                                           probT[h][:, offT[kc]:offT[kc + 1]], start=(kc == 0), stop=(kc == NT - 1))
                    pe_y.mark(m)
                    ends(pe_y)

                def hidden(m, s):
                    raw_A.wait(eng, s + 2, 2)
                    tok_done.wait(eng, m)
                    w1_load.wait(eng, m)
                    for k in range(KC + 1):
                        for j in range(GRP):
                            o = bQ[0][j * E:(j + 1) * E, 0:FW]
                            if k < KC:
                                p = eng.matmul(o, tok[:, k, :], w1[:, k, j * FW:(j + 1) * FW], start=(k == 0), stop=False)
                            else:
                                p = eng.matmul(o, one[:, :], w1b[:, j * FW:(j + 1) * FW], start=False, stop=True,
                                               tile_position=(0, j * E))
                    pe_h.mark(p)
                    ends(pe_h)

                def turn_hidden(m, projected):
                    raw_A.wait(eng, projected, 3)
                    hid_done.wait(eng, m)
                    for f in range(NF):
                        p = eng.transpose(bQ[1][:, f * P:(f + 1) * P], hid[:, f * P:(f + 1) * P], ident[:, :])
                    pe_hT.mark(p)
                    ends(pe_hT)

                def expert_output(m):
                    hidT_done.wait(eng, m)
                    w2_load.wait(eng, m)
                    for f in range(NF):
                        for j in range(GRP):
                            p = eng.matmul(bQ[0][j * E:(j + 1) * E, 0:C], hidT[:, f, j * E:(j + 1) * E],
                                           w2[:, j * NF + f, :], start=(f == 0), stop=(f == NF - 1 and j > 0))
                    p = eng.matmul(bQ[0][0:E, 0:C], one[:, :], w2b[:, :], start=False, stop=True, tile_position=(0, 0))
                    pe_eo.mark(p)
                    ends(pe_eo)

                def output(s, b, projected, m):
                    raw_A.wait(eng, projected)
                    eo_done.wait(eng, m)
                    y_done.wait(eng, s)
                    for n in range(NT):
                        if n >= 2:
                            o_done.wait(eng, b, n - 1)
                        for h in range(HP):
                            m = eng.matmul(bQ[n % 2][:, 0:C], yT[:, h, n * P:(n + 1) * P], w_proj[:, h, :],
                                           start=(h == 0), stop=(h == HP - 1))
                        pe_o.mark(m)
                    ends(pe_o)

                def first():
                    consts.wait(eng, 0)
                    xT_load.wait(eng, 0)
                    project(0, 0)
                    project(1, 1)
                    turn_qk(0, fresh=True)

                def turn(s, hp, m, first, ended):
                    qkT_A.wait(eng, s)
                    qkT_D.wait(eng, s)
                    scores(s, 0)
                    xT_load.wait(eng, (s + 2) // HP)
                    if not at_start(s):
                        o_done.wait(eng, (s - 1) // HP - 1)
                        if first:
                            eo_done.wait(eng, m - 1)
                        else:
                            hid_done.wait(eng, m)
                    project(s + 2, (hp + 2) % HP)
                    scores(s, 1)
                    ends(pe_s)
                    if not at_start(s):
                        values(s - 1)
                        if first:
                            hidden(m, s)
                        else:
                            turn_hidden(m, s + 2)
                    turn_p(s, 0)
                    turn_qk(s + 1)
                    if not first and not at_start(s):
                        expert_output(m)
                    turn_p(s, 1)
                    if ended is not None:
                        output(s - 1, ended, s + 2, m)

                def finish(s, b, m):
                    values(s - 1)
                    turn_hidden(m, s + 1)
                    expert_output(m)
                    output(s - 1, b, s + 1, m)
                turns(eng, first, turn, finish)

            @block.scalar
            def _(eng):
                for e in (raw_A, squared, r0_done, gate_exp, qkT_A, exp_done, pt0_A, pt1_A, y_done, hid_done):
                    e.credit(eng)
                eng.preload_act_table_set("natural_log_exp_and_others")

                def project(j):
                    for n in range(1, NT):
                        pe_q.wait(eng, j, n + 1)
                        if n == 1:
                            v_taken.wait(eng, j - 2)
                            norm_done.wait(eng, j - 2)
                            gate_in.wait(eng, j - 2)
                        raw_A.mark(eng.activation(raw[:, j % 2, n, :], bQ[n % 2][:, 0:W], ACT.Copy))
                    ends(raw_A)

                def square(j):
                    raw_A.wait(eng, j)
                    raw_D.wait(eng, j)
                    ssd.wait(eng, j - 1, 1)
                    squared.mark(eng.activation(sq[:, :, :], raw[:, j % 2, :, 0:2 * P], ACT.Square))
                    ends(squared)

                def rsqrt(j):
                    ssd.wait(eng, j)
                    r0_done.mark(eng.activation(lnv[:, :], ss[:, :], ACT.Ln))
                    newton.wait(eng, j - 1)
                    r0_done.wait(eng, j, 1)
                    r0_done.mark(eng.activation(r0[:, :], lnv[:, :], ACT.Exp, scale=-0.5))
                    ends(r0_done)

                def gate(j):
                    gate_in.wait(eng, j)
                    gate_g.wait(eng, j - 1)
                    gate_exp.mark(eng.activation(ge[:, :, :], ge[:, :, :], ACT.Exp))
                    gate_exp.wait(eng, j, 1)
                    gate_exp.mark(eng.activation(gp[:, :, :], ge[:, :, :], ACT.Ln, bias=1.0))
                    ends(gate_exp)

                def copy_qk(j):
                    pe_s.wait(eng, j - 1)
                    pe_t.wait(eng, j, 2)
                    qkT_A.mark(eng.activation(qkT[:, 2, :], bR[1][0:DA, :], ACT.Copy))
                    pe_t.wait(eng, j, 4)
                    qkT_A.mark(eng.activation(qkT[:, 3, :], bR[0][0:DA, :], ACT.Copy))
                    ends(qkT_A)

                def exps(s, h):
                    if h == 0:
                        rec_done.wait(eng, s - 1)
                    for c in range(NT):
                        i = NT * h + c
                        if c in (0, NT - 1):
                            negated.wait(eng, s, 2 * h + 1 + (c > 0))
                        sl = prob[h][:, off[c]:off[c + 1]]
                        exp_done.mark(eng.activation(sl, sl, ACT.Exp, bias=nm[:, i:i + 1], accum_out=den[:, i:i + 1]))

                def copy_p0(s):
                    pe_y.wait(eng, s - 1)
                    copy_P(eng, copy, 0, s)
                    copy_P(eng, copy, 1, s)
                    ends(pt0_A)

                def copy_p1(s):
                    copy_P(eng, copy, 7, s)
                    copy_P(eng, copy, 8, s)
                    ends(pt1_A)

                def copy(dst, src):
                    return eng.activation(dst, src, ACT.Copy)

                def copy_y(s, hp):
                    pe_o.wait(eng, s // HP - 1)
                    pe_y.wait(eng, s)
                    y_done.mark(copy(yT[:, hp, :], bY[:, :]))
                    ends(y_done)

                def first():
                    project(0)
                    square(0)
                    rsqrt(0)
                    gate(0)
                    project(1)
                    square(1)
                    copy_qk(0)
                    rsqrt(1)
                    gate(1)

                def gelu(m):
                    pe_h.wait(eng, m)
                    pe_hT.wait(eng, m - 1)
                    hid_done.mark(eng.activation(hid[:, :], bQ[0][:, 0:FW], ACT.Gelu))
                    ends(hid_done)
                    eng.preload_act_table_set("natural_log_exp_and_others")

                def turn(s, hp, m, first, ended):
                    exps(s, 0)
                    project(s + 2)
                    square(s + 2)
                    exps(s, 1)
                    ends(exp_done)
                    rsqrt(s + 2)
                    copy_p0(s)
                    if not at_start(s):
                        copy_y(s - 1, (hp + HP - 1) % HP)
                    copy_qk(s + 1)
                    copy_p1(s)
                    gate(s + 2)
                    if first:
                        gelu(m)
                turns(eng, first, turn, lambda s, b, m: copy_y(s - 1, HP - 1))

            @block.vector
            def _(eng):
                for e in (raw_D, ssd, newton, norm_done, gate_in, gate_g, qkT_D, maxed, negated, rec_done, p_done,
                          pt0_D, pt1_D, o_done, hidT_done, eo_done):
                    e.credit(eng)

                def project(j):
                    pe_q.wait(eng, j, 1)
                    v_taken.wait(eng, j - 2)
                    squared.wait(eng, j - 2)
                    raw_D.mark(eng.tensor_copy(raw[:, j % 2, 0, :], bQ[0][:, 0:W]))
                    ends(raw_D)

                def mean_square(j):
                    squared.wait(eng, j)
                    ssd.mark(eng.tensor_reduce(ss[:, :], sq[:, :, :].rearrange("p n (i d) -> p (n i) d", d=D), AX.X, ALU.add))
                    ssd.wait(eng, j, 1)
                    ssd.mark(eng.tensor_scalar(ss[:, :], ss[:, :], 1.0 / D, EPS, ALU.mult, ALU.add))
                    ends(ssd)

                def newton_step(j):
                    r0_done.wait(eng, j)
                    newton.mark(eng.scalar_tensor_tensor(nw[:, :], r0[:, :], -0.5, r0[:, :], ALU.mult, ALU.mult))
                    newton.wait(eng, j, 1)
                    newton.mark(eng.tensor_tensor(nw[:, :], nw[:, :], ss[:, :], ALU.mult))
                    newton.wait(eng, j, 2)
                    newton.mark(eng.scalar_tensor_tensor(rs[:, :, :].rearrange("p n i -> p (n i)"), nw[:, :], 1.5,
                                                         r0[:, :], ALU.add, ALU.mult))
                    ends(newton)

                def gate_input(j):
                    newton.wait(eng, j)
                    raw_A.wait(eng, j)
                    gate_exp.wait(eng, j - 1)
                    aug_done.wait(eng, j - 1)
                    gate_in.mark(eng.tensor_tensor(gl[:, :, :], raw[:, j % 2, :, 3 * P:W], rs[:, :, 2:4], ALU.mult))
                    gate_in.wait(eng, j, 1)
                    gate_in.mark(eng.scalar_tensor_tensor(ge[:, :, :], gl[:, :, :], -1.0, gl[:, :, :], ALU.mult, ALU.min))
                    ends(gate_in)

                def gate(j):
                    gate_exp.wait(eng, j)
                    gate_g.mark(eng.scalar_tensor_tensor(gl[:, :, :], gl[:, :, :], 0.0, gp[:, :, :], ALU.max, ALU.add))
                    ends(gate_g)

                def norm(j):
                    pe_t.wait(eng, j - 1)
                    norm_done.mark(eng.tensor_tensor(
                        qk[:, :, :, 0:D], raw[:, j % 2, :, 0:2 * P].rearrange("p n (i d) -> p n i d", d=D),
                        rs[:, :, :].unsqueeze(3).to_broadcast([P, NT, 4, D]), ALU.mult))
                    ends(norm_done)

                def copy_q(j, h):
                    pe_s.wait(eng, j - 1)
                    pe_t.wait(eng, j, 2 * h + 1)
                    qkT_D.mark(eng.tensor_scalar(qkT[:, h, :], bR[2 * h][0:DA, :], q_scale[:, 0:1], None, ALU.mult))

                def maxes(s, h):
                    for c in range(NT):
                        i = NT * h + c
                        if c == 0:
                            pe_pt[h].wait(eng, s - 1)
                            exp_done.wait(eng, s - 1)
                        pe_s.wait(eng, s, i + 1, alone=True)
                        maxed.mark(eng.tensor_tensor_reduce(
                            out=prob[h][:, off[c]:off[c + 1]], in0=bS[i % 2][:, 0:(c + 1) * P],
                            in1=mask[:, (NT - 1 - c) * P:T], scale=1.0, scalar=LOWEST, op0=ALU.add, op1=ALU.max,
                            accum_out=mx[:, i:i + 1]))
                        if c >= NT - 2:
                            maxed.wait(eng, s, i + 1)
                            at = NT * h if c == NT - 2 else i
                            negated.mark(eng.tensor_scalar(nm[:, at:i + 1], mx[:, at:i + 1], -1.0, None, ALU.mult))

                def reciprocals(s, h):
                    exp_done.wait(eng, s, 4 * h + 4)
                    rec_done.mark(eng.reciprocal(rec[:, 4 * h:4 * h + 4], den[:, 4 * h:4 * h + 4]))

                def divide(s, h):
                    rec_done.wait(eng, s, h + 1)
                    for c in range(NT):
                        i = NT * h + c
                        sl = prob[h][:, off[c]:off[c + 1]]
                        m = eng.tensor_scalar(sl, sl, rec[:, i:i + 1], None, ALU.mult)
                    p_done.mark(m)

                def copy_p(s, u):
                    pe_y.wait(eng, s - 1)
                    copy_P(eng, eng.tensor_copy, u, s)

                def output(b):
                    xr_load.wait(eng, b)
                    for n in range(NT):
                        pe_o.wait(eng, b, n + 1)
                        o_done.mark(eng.tensor_tensor(xr[:, n, :], bQ[n % 2][:, 0:C], xr[:, n, :], ALU.add))
                    ends(o_done)

                def prepare(j):
                    mean_square(j)
                    newton_step(j)
                    gate_input(j)

                def first():
                    for j in range(2):
                        project(j)
                        if j == 0:
                            prepare(0)
                            gate(0)
                            norm(0)
                    copy_q(0, 0)
                    copy_q(0, 1)
                    ends(qkT_D)
                    prepare(1)

                def copy_hidden(m):
                    pe_hT.wait(eng, m)
                    pe_eo.wait(eng, m - 1)
                    hidT_done.mark(eng.tensor_copy(hidT[:, :, :], bQ[1][:, 0:FW].rearrange("p (f q) -> p f q", f=NF)))
                    ends(hidT_done)

                def copy_expert_output(m):
                    pe_eo.wait(eng, m)
                    eo_store.wait(eng, m - 1)
                    eo_done.mark(eng.tensor_copy(eo[:, :], bQ[0][:, 0:C]))
                    ends(eo_done)

                def turn(s, hp, m, first, ended):
                    maxes(s, 0)
                    project(s + 2)
                    gate(s + 1)
                    norm(s + 1)
                    reciprocals(s, 0)
                    divide(s, 0)
                    maxes(s, 1)
                    mean_square(s + 2)
                    reciprocals(s, 1)
                    divide(s, 1)
                    if not first and not at_start(s):
                        copy_hidden(m)
                    copy_p(s, 2)
                    copy_q(s + 1, 0)
                    newton_step(s + 2)
                    copy_q(s + 1, 1)
                    gate_input(s + 2)
                    if not first and not at_start(s):
                        copy_expert_output(m)
                    copy_p(s, 9)
                    ends(maxed, negated, rec_done, p_done, pt0_D, pt1_D, qkT_D)
                    if ended is not None:
                        output(ended)

                def finish(s, b, m):
                    copy_hidden(m)
                    copy_expert_output(m)
                    output(b)
                turns(eng, first, turn, finish)

            @block.gpsimd
            def _(eng):
                for e in (aug_done, v_taken, v_done, consts, tok_done):
                    e.credit(eng)
                consts.mark(eng.memset(tok[:, :, :], 0.0))
                consts.mark(eng.memset(one[:, :], 1.0))
                for h in range(2):
                    consts.mark(eng.tensor_scalar(qk[:, :, h, D], pos[:, :], -1.0, None, ALU.mult))
                consts.mark(eng.memset(qk[:, :, 0:2, D + 1], 1.0))

                def augment(j, hp):
                    gate_g.wait(eng, j)
                    pe_t.wait(eng, j - 1)
                    aug_done.mark(eng.tensor_tensor(
                        qk[:, :, 2:4, D], gl[:, :, :],
                        omega[:, bass.ds(hp * 2, 2)].unsqueeze(1).to_broadcast([P, NT, 2]), ALU.mult))
                    aug_done.wait(eng, j, 1)
                    aug_done.mark(eng.tensor_tensor(
                        qk[:, :, 2:4, D + 1], qk[:, :, 2:4, D],
                        pos[:, :].unsqueeze(2).to_broadcast([P, NT, 2]), ALU.mult))
                    ends(aug_done)

                def take_v(j):
                    raw_A.wait(eng, j)
                    raw_D.wait(eng, j)
                    v_done.wait(eng, j - 2, alone=True)
                    v_taken.mark(eng.tensor_copy(v_ring[:, j % 2, :, :], raw[:, j % 2, :, 2 * P:3 * P]))
                    ends(v_taken)

                def first():
                    consts.wait(eng, 0)
                    augment(0, 0)
                    for j in range(2):
                        take_v(j)

                def take_tokens(m):
                    pe_h.wait(eng, m - 1, alone=True)
                    tok_done.mark(eng.tensor_copy(tok[:, :, 0:B], merged[:, :, m, :]))
                    ends(tok_done)

                def turn(s, hp, m, first, ended):
                    if first:
                        take_tokens(m)
                    augment(s + 1, (hp + 1) % HP)
                    v_taken.wait(eng, s)
                    pe_y.wait(eng, s - 1, alone=True)
                    v_done.mark(eng.tensor_copy(v[:, :, :], v_ring[:, s % 2, :, :]))
                    ends(v_done)
                    take_v(s + 2)
                turns(eng, first, turn, lambda s, b, m: None)


def second_layer(nc, t, out, g):
    B, T, C, NT, KC, E, NB, HC, M1, TOPK, GRP, F = (g[k] for k in (
        "B", "T", "C", "NT", "KC", "E", "NB", "HC", "M1", "TOPK", "GRP", "F"))
    ident, half, pick_d, x1_d, eo_d = g["ident"], g["half"], g["pick_d"], g["x1_d"], g["eo_d"]
    w1n, w2n, wk, m1n, m2n, rn, rb, backT, b1 = (g[k] for k in (
        "w1n", "w2n", "wk", "m1n", "m2n", "rn", "rb", "backT", "b1"))
    with ExitStack() as ctx:
        sb = g["sb_in"](ctx)
        rT = sb("rT", [P, KC, NB])
        up_hi = sb("up_hi", [P, KC, HC, P], F32R)
        up_lo = sb("up_lo", [P, KC, HC, P], F32R)
        downT_hi = sb("downT_hi", [P, HC, C], F32R)
        downT_lo = sb("downT_lo", [P, HC, C], F32R)
        readT_hi = sb("readT_hi", [P, KC, P], F32R)
        readT_lo = sb("readT_lo", [P, KC, P], F32R)
        spread = sb("spread", [NB, HC, P], F32R)
        number = sb("number", [P, NB])

        with ExitStack() as c2:
            sb2 = g["sb_in"](c2)
            m1T = sb2("m1T", [P, KC, M1])
            sp = sb2("sp", [NB, HC, P])
            pe, dv, hi, po = (Chain(c2, nc, n, 0) for n in ("pe_s3", "dv_s3", "hi_s3", "po_s3"))
            bk = g["banks"](c2, 4, "s3")
            jobs = [((m1T[:, :, :],), M1, [m1n[:, k * P:(k + 1) * P] for k in range(KC)]),
                    ((rT[:, :, :],), NB, [rn[:, k * P:(k + 1) * P] for k in range(KC)]),
                    ((backT[0:M1, :],), P, [m2n[:, k, :] for k in range(KC)])]
            for k in range(KC):
                for h in range(0, HC, 4):
                    jobs.append(((up_hi[:, k, h:h + 4, :], up_lo[:, k, h:h + 4, :]), P,
                                 [w1n[:, h + i, k * P:(k + 1) * P] for i in range(4)]))
            for h in range(0, HC, 2):
                jobs.append(((downT_hi[:, h:h + 2, :], downT_lo[:, h:h + 2, :]), P,
                             [w2n[:, k, (h + i) * P:(h + i + 1) * P] for i in range(2) for k in range(KC)]))
            jobs.append(((readT_hi[:, :, 0:M1], readT_lo[:, :, 0:M1]), M1, None))

            def filled(n):
                dst, width, srcs = jobs[n]
                rows, cols = dst[0].shape[0], width * len(srcs or (0,) * KC)
                view = bk[n % 4][0:rows, 0:cols]
                return view.rearrange("p (a b) -> p a b", b=dst[0].shape[2]) if len(dst[0].shape) == 3 else view
            halves = [n for n in range(len(jobs)) if len(jobs[n][0]) == 2]
            with nc.Block() as block:
                @block.gpsimd
                def _(eng):
                    po.mark(eng.iota(number[:, :], pattern=[[1, NB]], base=0, channel_multiplier=0,
                                     allow_small_or_imprecise_dtypes=True))
                    po.mark(eng.memset(sp[:, :, :], 1.0))
                    po.settle(eng, -1)
                    w = HC * P // NB
                    po.mark(eng.affine_select(out=sp[:, :, :], in_=sp[:, :, :], compare_op=ALU.is_ge, fill=0.0, base=0,
                                              pattern=[[P, HC], [1, P]], channel_multiplier=-w))
                    po.settle(eng, -1)
                    po.mark(eng.affine_select(out=sp[:, :, :], in_=sp[:, :, :], compare_op=ALU.is_ge, fill=0.0,
                                              base=w - 1, pattern=[[-P, HC], [-1, P]], channel_multiplier=w))

                @block.tensor
                def _(eng):
                    for n, (dst, width, srcs) in enumerate(jobs):
                        if n >= 4:
                            dv.wait(eng, -1, n - 3)
                        if srcs is None:
                            dv.wait(eng, -1, 1)
                            for k in range(KC):
                                for kk in range(KC):
                                    m = eng.matmul(bk[n % 4][:, k * M1:(k + 1) * M1], wk[:, kk, k * P:(k + 1) * P],
                                                   m1T[:, kk, :], start=(kk == 0), stop=(kk == KC - 1))
                        else:
                            for i, src in enumerate(srcs):
                                rows, cols = src.shape
                                m = eng.transpose(bk[n % 4][0:cols, i * width:(i + 1) * width], src, ident[0:rows, 0:rows])
                        pe.mark(m)

                @block.scalar
                def _(eng):
                    for n in halves:
                        pe.wait(eng, -1, n + 1)
                        hi.mark(eng.activation(jobs[n][0][0], filled(n), ACT.Copy))

                @block.vector
                def _(eng):
                    for n, (dst, _, _) in enumerate(jobs):
                        pe.wait(eng, -1, n + 1)
                        if len(dst) == 1:
                            dv.mark(eng.tensor_copy(dst[0], filled(n)))
                        else:
                            hi.wait(eng, -1, halves.index(n) + 1)
                            dv.mark(eng.tensor_tensor(dst[1], filled(n), dst[0].bitcast(F32), ALU.subtract))
                    dv.settle(eng, -1)
                    for part in (readT_hi, readT_lo):
                        eng.tensor_scalar(part[:, :, M1:P], up_lo[:, :, 0, M1:P].bitcast(F32), 0.0, None, ALU.mult)
                    po.wait(eng, -1, 4)
                    eng.tensor_copy(spread[:, :, :], sp[:, :, :])

        xr = sb("xr3", [P, NT, C])
        x1 = sb("x1", [P, 2, NT, C])
        xT_hi = sb("xT3_hi", [P, 2, KC, T], F32R)
        xT_lo = sb("xT3_lo", [P, 2, KC, T], F32R)
        shutT = sb("shutT", [NB, 2, T], F32R)
        pick4 = sb("pick4", [P, T])
        eo = sb("eo3", [P, C])
        stats = sb("stats3", [P, NT, 6])
        mv = sb("mv3", [P, NT, 2])
        var = sb("var3", [P, NT])
        rstd = sb("rstd3", [P, NT])
        xn = sb("xn3", [P, NT, C])
        xT = sb("xT3", [P, KC, T])
        logit = sb("logit3", [P, NT, NB])
        top = sb("top3", [P, NT, 8])
        idx = sb("idx3", [P, NT, 8], U32)
        idxf = sb("idxf3", [P, NT, 8])
        eq = sb("eq3", [P, NT, NB, TOPK])
        shut = sb("shut3", [P, NT, NB])
        mem = sb("mem3", [M1 + 1, T])
        hT = sb("hT3", [P, HC, T])
        hT_hi = sb("hT3_hi", [P, HC, T], F32R)
        hT_lo = sb("hT3_lo", [P, HC, T], F32R)
        xo = sb("xo3", [P, NT, C])
        b8 = g["banks"](ctx, 8, "l1")
        bF, bR, bU, bD, bMem = b8[0:2], b8[2], b8[3:5], b8[5:7], b8[7]

        ev = lambda name, per, unit=1: Event(ctx, nc, name, per, unit, g["carrier"])
        load, store = ev("load3", 2 * GRP + 1, 16), ev("store3", 1, 16)
        pe_add, pe_xT, pe_r, pe_shut = ev("pe_add", 2), ev("pe_xT3", 2), ev("pe_r", 1), ev("pe_shut", 1)
        pe_mem, pe_up, pe_down = ev("pe_mem", 1), ev("pe_up", HC), ev("pe_down", 2)
        xT_done, mem_done, relu_done = ev("xT_done3", 2), ev("mem_done", 1), ev("relu_done", HC)
        relu32_done, relu_lo_done = ev("relu32_done", HC), ev("relu_lo_done", HC)
        x1_done, stat, agg, var_done = ev("x1_done", 2), ev("stat", NT), ev("agg", NT), ev("var_done3", 1)
        xn_done, hi_done, lo_done = ev("xn_done3", NT), ev("hi_done", 1), ev("lo_done", 1)
        logit_done, route, shut_done, shutT_done, out_done = (
            ev("logit_done", 1), ev("route", 2 * NT + 3), ev("shut_done", 1), ev("shutT_done", 1), ev("out_done", 2))
        rstd_done, mem_one = ev("rstd_done", 1), ev("mem_one", 1)

        def ends(*events):
            for e in events:
                e.turn_ends()

        with nc.Block() as block:
            @block.sync
            def _(eng):
                for e in (load, store):
                    e.credit(eng)

                def get(b):
                    load.mark(eng.dma_start(xr[:, :, :], x1_d[b].rearrange("(n p) c -> p n c", p=P)))
                    for j in range(GRP):
                        load.mark(eng.dma_start(pick4[j * E:(j + 1) * E, :], pick_d[b]))
                        load.mark(eng.dma_start(eo[j * E:(j + 1) * E, :], eo_d[:, j * E + b, :]))
                    ends(load)

                def put(b):
                    out_done.wait(eng, b)
                    store.mark(eng.dma_start(out[b].rearrange("(n p) c -> p n c", p=P), xo[:, :, :]))
                    ends(store)

                def free(b):
                    pe_add.wait(eng, b)
                    x1_done.wait(eng, b)
                get(0)
                free(0)
                get(1)
                with eng.Fori(0, B - 2) as b:
                    free(b + 1)
                    get(b + 2)
                    put(b)
                put(B - 2)
                put(B - 1)
                store.wait(eng, B - 1)

            def turns(eng, front_of_first, turn, last):
                front_of_first()
                with eng.Fori(0, B - 1) as b:
                    turn(b)
                last(B - 1)

            @block.tensor
            def _(eng):
                for e in (pe_add, pe_xT, pe_r, pe_shut, pe_mem, pe_up, pe_down):
                    e.credit(eng)

                def add(b):
                    load.wait(eng, b)
                    lo_done.wait(eng, b - 1)
                    shutT_done.wait(eng, b - 1)
                    for n in range(NT):
                        m = eng.matmul(bF[n // 2][:, (n % 2) * C:(n % 2 + 1) * C], pick4[:, n * P:(n + 1) * P], eo[:, :],
                                       start=True, stop=True)
                        if n % 2:
                            pe_add.mark(m)
                    ends(pe_add)

                def turn_x(b):
                    xn_done.wait(eng, b)
                    x1_done.wait(eng, b)
                    for k in range(KC):
                        for n in range(NT):
                            m = eng.transpose(bF[k][:, n * P:(n + 1) * P], xn[:, n, k * P:(k + 1) * P], ident[:, :])
                        pe_xT.mark(m)
                    ends(pe_xT)

                def router(b):
                    xT_done.wait(eng, b)
                    logit_done.wait(eng, b - 1)
                    for n in range(NT):
                        for k in range(KC):
                            m = eng.matmul(bR[:, n * NB:(n + 1) * NB], xT[:, k, n * P:(n + 1) * P], rT[:, k, :],
                                           start=(k == 0), stop=(k == KC - 1))
                    pe_r.mark(m)
                    ends(pe_r)

                def turn_shut(b):
                    shut_done.wait(eng, b)
                    for n in range(NT):
                        m = eng.transpose(bF[0][0:NB, n * P:(n + 1) * P], shut[:, n, :], ident[:, :])
                    pe_shut.mark(m)
                    ends(pe_shut)

                def product(b, bank, hi, lo, first, done):
                    start = first
                    for k in range(KC):
                        for w, x in ((lo, xT_hi), (hi, xT_lo), (hi, xT_hi)):
                            m = eng.matmul(bank[:, :], w[:, k, :], x[:, b % 2, k, :], start=start,
                                           stop=(k == KC - 1 and w is hi and x is xT_hi))
                            start = False
                    done.mark(m)

                def memory(b):
                    lo_done.wait(eng, b)
                    shutT_done.wait(eng, b)
                    mem_done.wait(eng, b - 1)
                    product(b, bMem, readT_hi, readT_lo, True, pe_mem)
                    ends(pe_mem)

                def up(b, hs):
                    for h in hs:
                        if h == 0:
                            relu_done.wait(eng, b - 1, HC - 1, alone=True)
                        elif h == 1:
                            relu_done.wait(eng, b - 1, HC, alone=True)
                        else:
                            relu_done.wait(eng, b, h - 1, alone=True)
                        eng.matmul(bU[h % 2][:, :], spread[:, h, :], shutT[:, b % 2, :], start=True, stop=False)
                        product(b, bU[h % 2], up_hi[:, :, h, :], up_lo[:, :, h, :], False, pe_up)
                    if h == HC - 1:
                        ends(pe_up)

                def down(b, ns):
                    for n in ns:
                        if n == 0:
                            mem_one.wait(eng, 0)
                            mem_done.wait(eng, b)
                        if n % 2 == 0:
                            out_done.wait(eng, b - 1, n // 2 + 1)
                        o = bD[n // 2][:, (n % 2) * C:(n % 2 + 1) * C]
                        eng.matmul(o, mem[:, n * P:(n + 1) * P], backT[:, :], start=True, stop=False)
                        for h in range(HC):
                            if n == 0:
                                relu_done.wait(eng, b, h + 1)
                                relu_lo_done.wait(eng, b, h + 1)
                            for part, w in ((hT_lo, downT_hi), (hT_hi, downT_lo), (hT_hi, downT_hi)):
                                m = eng.matmul(o, part[:, h, n * P:(n + 1) * P], w[:, h, :], start=False,
                                               stop=(h == HC - 1 and part is hT_hi and w is downT_hi))
                        if n % 2:
                            pe_down.mark(m)
                    if n == NT - 1:
                        ends(pe_down)

                def first():
                    add(0)
                    turn_x(0)
                    router(0)
                    turn_shut(0)

                def turn(b):
                    add(b + 1)
                    memory(b)
                    up(b, range(0, 3))
                    turn_x(b + 1)
                    up(b, range(3, 6))
                    router(b + 1)
                    up(b, range(6, HC))
                    down(b, (0, 1))
                    turn_shut(b + 1)
                    down(b, (2, 3))

                def last(b):
                    memory(b)
                    up(b, range(HC))
                    down(b, range(NT))
                turns(eng, first, turn, last)

            @block.scalar
            def _(eng):
                for e in (xT_done, mem_done, relu_done, relu32_done):
                    e.credit(eng)

                def copy_x(b):
                    hi_done.wait(eng, b - 1)
                    lo_done.wait(eng, b - 1)
                    pe_r.wait(eng, b - 1)
                    for k in range(KC):
                        pe_xT.wait(eng, b, k + 1)
                        xT_done.mark(eng.activation(xT[:, k, :], bF[k][:, :], ACT.Copy))
                    ends(xT_done)

                def memory(b):
                    pe_mem.wait(eng, b)
                    pe_down.wait(eng, b - 1)
                    mem_done.mark(eng.activation(mem[0:M1, :], bMem[0:M1, :], ACT.Gelu))
                    ends(mem_done)

                def relu(b, hs):
                    for h in hs:
                        pe_up.wait(eng, b, h + 1)
                        relu_lo_done.wait(eng, b - 1, h + 1)
                        relu32_done.mark(eng.activation(hT[:, h, :], bU[h % 2][:, :], ACT.Relu, bias=b1[:, h:h + 1]))
                        relu_done.mark(eng.activation(hT_hi[:, h, :], bU[h % 2][:, :], ACT.Relu, bias=b1[:, h:h + 1]))
                    if h == HC - 1:
                        ends(relu_done, relu32_done)

                def turn(b):
                    memory(b)
                    relu(b, range(0, 3))
                    copy_x(b + 1)
                    relu(b, range(3, HC))

                def last(b):
                    memory(b)
                    relu(b, range(HC))
                turns(eng, lambda: copy_x(0), turn, last)

            @block.gpsimd
            def _(eng):
                rstd_done.credit(eng)
                mem_one.credit(eng)
                mem_one.mark(eng.memset(mem[M1:M1 + 1, :], 1.0))
                mem_one.wait(eng, 0)
                with eng.Fori(0, B) as b:
                    var_done.wait(eng, b)
                    xn_done.wait(eng, b - 1)
                    rstd_done.mark(eng.tensor_tensor(rstd[:, :], var[:, :], half[:, 0:NT], ALU.pow))
                    rstd_done.turn_ends()

            @block.vector
            def _(eng):
                for e in (relu_lo_done, x1_done, stat, agg, var_done, xn_done, hi_done, lo_done, logit_done, route,
                          shut_done, shutT_done, out_done):
                    e.credit(eng)

                def norm(b):
                    load.wait(eng, b)
                    out_done.wait(eng, b - 2)
                    for i in range(2):
                        pe_add.wait(eng, b, i + 1)
                        x1_done.mark(eng.tensor_tensor(
                            x1[:, b % 2, 2 * i:2 * i + 2, :], bF[i][:, :].rearrange("p (n c) -> p n c", n=2),
                            xr[:, 2 * i:2 * i + 2, :], ALU.add))
                    x1_done.wait(eng, b, alone=True)
                    for n in range(NT):
                        stat.mark(eng.bn_stats(stats[:, n, :], x1[:, b % 2, n, :]))
                    stat.wait(eng, b, alone=True)
                    for n in range(NT):
                        agg.mark(eng.bn_aggr(mv[:, n, :], stats[:, n, :]))
                    agg.wait(eng, b)
                    var_done.mark(eng.tensor_scalar(var[:, :], mv[:, :, 1], EPS, None, ALU.add))
                    rstd_done.wait(eng, b)
                    pe_xT.wait(eng, b - 1)
                    for n in range(NT):
                        xn_done.mark(eng.tensor_scalar(xn[:, n, :], x1[:, b % 2, n, :], mv[:, n, 0:1],
                                                       rstd[:, n:n + 1], ALU.subtract, ALU.mult))
                    ends(x1_done, stat, agg, var_done, xn_done)

                def split(b):
                    xT_done.wait(eng, b)
                    pe_up.wait(eng, b - 2)
                    hi_done.mark(eng.tensor_copy(xT_hi[:, b % 2, :, :], xT[:, :, :]))
                    hi_done.wait(eng, b)
                    lo_done.mark(eng.tensor_tensor(xT_lo[:, b % 2, :, :], xT[:, :, :],
                                                   xT_hi[:, b % 2, :, :].bitcast(F32), ALU.subtract))
                    ends(hi_done, lo_done)

                def choose(b):
                    pe_r.wait(eng, b)
                    logit_done.mark(eng.tensor_tensor(
                        logit[:, :, :], bR[:, 0:NT * NB].rearrange("p (n i) -> p n i", n=NT),
                        rb[:, :].unsqueeze(1).to_broadcast([P, NT, NB]), ALU.add))
                    logit_done.wait(eng, b, alone=True)
                    for n in range(NT):
                        route.mark(eng.max(top[:, n, :], logit[:, n, :]))
                    route.wait(eng, b, NT, alone=True)
                    for n in range(NT):
                        route.mark(eng.max_index(idx[:, n, :], top[:, n, :], logit[:, n, :]))
                    route.wait(eng, b, 2 * NT)
                    route.mark(eng.tensor_copy(idxf[:, :, :], idx[:, :, :]))
                    route.wait(eng, b, 2 * NT + 1)
                    full = [P, NT, NB, TOPK]
                    route.mark(eng.tensor_tensor(
                        eq[:, :, :, :], idxf[:, :, 0:TOPK].unsqueeze(2).to_broadcast(full),
                        number[:, :].unsqueeze(1).unsqueeze(3).to_broadcast(full), ALU.is_equal))
                    route.wait(eng, b, 2 * NT + 2)
                    pe_shut.wait(eng, b - 1)
                    route.mark(eng.tensor_reduce(shut[:, :, :], eq[:, :, :, :], AX.X, ALU.add))
                    route.wait(eng, b)
                    shut_done.mark(eng.tensor_scalar(shut[:, :, :], shut[:, :, :], -1.0, -NEG, ALU.add, ALU.mult))
                    ends(logit_done, route, shut_done)

                def copy_shut(b):
                    pe_shut.wait(eng, b)
                    pe_up.wait(eng, b - 2)
                    shutT_done.mark(eng.tensor_copy(shutT[:, b % 2, :], bF[0][0:NB, :]))
                    ends(shutT_done)

                def relu_low(b, hs):
                    for h in hs:
                        if h == 0:
                            pe_down.wait(eng, b - 1)
                        relu32_done.wait(eng, b, h + 1)
                        relu_done.wait(eng, b, h + 1)
                        relu_lo_done.mark(eng.tensor_tensor(hT_lo[:, h, :], hT[:, h, :], hT_hi[:, h, :].bitcast(F32),
                                                            ALU.subtract))
                    if h == HC - 1:
                        ends(relu_lo_done)

                def finish(b):
                    store.wait(eng, b - 1)
                    for i in range(2):
                        pe_down.wait(eng, b, i + 1)
                        out_done.mark(eng.tensor_tensor(
                            xo[:, 2 * i:2 * i + 2, :], bD[i][:, :].rearrange("p (n c) -> p n c", n=2),
                            x1[:, b % 2, 2 * i:2 * i + 2, :], ALU.add))
                    ends(out_done)

                def front(b):
                    norm(b)
                    split(b)
                    choose(b)
                    copy_shut(b)

                def turn(b):
                    norm(b + 1)
                    relu_low(b, range(0, 3))
                    split(b + 1)
                    relu_low(b, range(3, 6))
                    choose(b + 1)
                    relu_low(b, range(6, HC))
                    copy_shut(b + 1)
                    finish(b)

                def last(b):
                    relu_low(b, range(HC))
                    finish(b)
                turns(eng, lambda: front(0), turn, last)


_INS = ["L0_attn_x", "L0_attn_Wq", "L0_attn_Wk", "L0_attn_Wv", "L0_attn_Wproj", "L0_attn_q_rms_w", "L0_attn_k_rms_w",
        "L0_attn_omega", "L0_attn_u", "L0_ffn_gate_w", "L0_ffn_gate_b", "L0_ffn_w1", "L0_ffn_w2", "L1_attn_W_K",
        "L1_attn_W1", "L1_attn_W2", "L1_ffn_router_w", "L1_ffn_router_b", "L1_ffn_w1", "L1_ffn_b1", "L1_ffn_w2",
        "L1_ffn_b2"]


def kernel(**inputs):
    import numpy as np
    import concourse.bacc as bacc
    from concourse.bass_utils import run_bass_kernel_spmd

    nc = bacc.Bacc("TRN2", target_bir_lowering=False, num_devices=1)
    arrays, t = {}, {}
    for name in _INS:
        arrays["in_" + name] = np.ascontiguousarray(inputs[name])
        t[name] = nc.dram_tensor("in_" + name, arrays["in_" + name].shape, F32, kind="ExternalInput").ap()
    out = nc.dram_tensor("out", arrays["in_L0_attn_x"].shape, F32, kind="ExternalOutput").ap()
    build(nc, t, out)
    return run_bass_kernel_spmd(nc, [arrays], core_ids=[0]).results[0]["out"]
```
